# Optimizing a Trainium2 kernel written in Bass

```python
import numpy as np
import jax
import jax.numpy as jnp

def _softmax(x, axis=-1):
    return jax.nn.softmax(x, axis=axis)

def _gelu(x):
    return jax.nn.gelu(x, approximate=True)

def _silu(x):
    return jax.nn.silu(x)

def _sigmoid(x):
    return jax.nn.sigmoid(x)

def _layernorm(x, axis=-1, eps=1e-05):
    m = jnp.mean(x, axis=axis, keepdims=True)
    v = jnp.var(x, axis=axis, keepdims=True)
    return (x - m) / jnp.sqrt(v + eps)

def _scatter_add(tgt, idx, src, axis=0):
    return tgt.at[idx].add(src)

def _segment_sum(src, seg, n):
    return jax.ops.segment_sum(src, seg, n)
kernel_name = 'mk_audio_tower_d2_tok_audfeat256_r4_a113b7'

def setup_inputs(seed: int=0):
    np.random.seed(seed)
    _w = jnp.asarray

    def _rec_inputs():
        import jax
        import jax.numpy as jnp
        _rk = jax.random.key(seed)
        x = 7.22013e-05 + 1.00017 * jax.random.normal(jax.random.fold_in(_rk, 1), (32, 256, 64), jnp.float32)
        return x
    x = _rec_inputs()

    def _L0_tok_setup():
        import jax, jax.numpy as jnp
        import numpy as np
        WIN = 9
        key = jax.random.key(seed)
        ks = jax.random.split(key, 4)
        N, L, C, U = (8, 1024, 64, 64)
        x = jax.random.normal(ks[0], (N, L, C), dtype=jnp.float32)
        W_qry = jax.random.normal(ks[1], (C, U), dtype=jnp.float32) * 0.05
        W_key = jax.random.normal(ks[2], (C, U), dtype=jnp.float32) * 0.05
        v = jax.random.normal(ks[3], (U,), dtype=jnp.float32) * 0.05
        b = jnp.zeros((U,), dtype=jnp.float32)
        return {'x': x, 'W_qry': W_qry, 'W_key': W_key, 'v': v, 'b': b}
    _L0_tok_all = _L0_tok_setup()
    _L0_tok_in = {k: v for k, v in _L0_tok_all.items() if k in ('W_qry', 'W_key', 'v', 'b')}
    del _L0_tok_all

    def _L0_attn_setup():
        import jax, jax.numpy as jnp
        import numpy as np
        B, L, D, K, KU, KY = (4, 512, 64, 24, 3, 2)

        def _hankel_eigh(l, k):
            i = np.arange(1, l + 1, dtype=np.float64)
            s = i[:, None] + i[None, :]
            Z = 2.0 / (s ** 3 - s)
            vals, vecs = np.linalg.eigh(Z)
            return (jnp.asarray(vals[-k:], jnp.float32), jnp.asarray(vecs[:, -k:], jnp.float32))

        def _stu_forward(inputs, m_u, m_phi, m_y, eig_vals, eig_vecs):
            b, l, d = inputs.shape
            k = eig_vals.shape[0]
            n = 2 * l
            V = jnp.fft.rfft(eig_vecs, n=n, axis=0)
            U = jnp.fft.rfft(inputs, n=n, axis=1)
            conv = jnp.fft.irfft(V[None, :, :, None] * U[:, :, None, :], n=n, axis=1)[:, :l]
            x_tilde = conv * (eig_vals ** 0.25)[None, None, :, None]
            delta_phi = x_tilde.reshape(b, l, k * d) @ m_phi
            ar = jnp.zeros_like(delta_phi)
            for i in range(m_u.shape[-1]):
                c = jnp.einsum('oi,bli->blo', m_u[:, :, i], inputs)
                ar = ar + jnp.pad(c, ((0, 0), (i, 0), (0, 0)))[:, :l]
            deltas = delta_phi + ar
            ky = m_y.shape[1]

            def step(carry, delta_t):
                out = jnp.einsum('okd,bkd->bo', m_y, carry) + delta_t
                carry = jnp.concatenate([out[:, None, :], carry[:, :-1, :]], axis=1)
                return (carry, out)
            _, ys = jax.lax.scan(step, jnp.zeros((b, ky, d), deltas.dtype), jnp.swapaxes(deltas, 0, 1))
            return jnp.swapaxes(ys, 0, 1)
        key = jax.random.key(seed)
        k1, k2, k3, k4 = jax.random.split(key, 4)
        eig_vals, eig_vecs = _hankel_eigh(L, K)
        return {'inputs': jax.random.normal(k1, (B, L, D), jnp.float32), 'm_u': jax.random.normal(k2, (D, D, KU), jnp.float32) / jnp.sqrt(jnp.float32(D)), 'm_phi': jax.random.normal(k3, (D * K, D), jnp.float32) / jnp.sqrt(jnp.float32(D * K)), 'm_y': jax.random.normal(k4, (D, KY, D), jnp.float32) * (0.5 / jnp.sqrt(jnp.float32(KY * D))), 'eig_vals': eig_vals, 'eig_vecs': eig_vecs}
    _L0_attn_all = _L0_attn_setup()
    _L0_attn_in = {k: v for k, v in _L0_attn_all.items() if k in ('m_u', 'm_phi', 'm_y', 'eig_vals', 'eig_vecs')}
    del _L0_attn_all

    def _L0_ffn_setup():
        import math
        import jax, jax.numpy as jnp
        import numpy as np
        CAPACITY_FACTOR = 1.25
        TOP_K = 2
        LN_EPS = 1e-05

        def _layer_norm(x, gamma, beta):
            mu = jnp.mean(x, axis=-1, keepdims=True)
            var = jnp.var(x, axis=-1, keepdims=True)
            return (x - mu) * jax.lax.rsqrt(var + LN_EPS) * gamma + beta
        key = jax.random.key(seed)
        ks = jax.random.split(key, 4)
        B, S, D, F, E = (8, 1024, 64, 128, 8)
        x = jax.random.normal(ks[0], (B, S, D), dtype=jnp.float32)
        Wr = jax.random.normal(ks[1], (D, E), dtype=jnp.float32) / np.sqrt(D)
        br = jnp.zeros((E,), jnp.float32)
        W1 = jax.random.normal(ks[2], (E, D, F), dtype=jnp.float32) / np.sqrt(D)
        b1 = jnp.zeros((E, F), jnp.float32)
        W2 = jax.random.normal(ks[3], (E, F, D), dtype=jnp.float32) / np.sqrt(F)
        b2 = jnp.zeros((E, D), jnp.float32)
        gamma = jnp.ones((D,), jnp.float32)
        beta = jnp.zeros((D,), jnp.float32)
        return {'x': x, 'Wr': Wr, 'br': br, 'W1': W1, 'b1': b1, 'W2': W2, 'b2': b2, 'gamma': gamma, 'beta': beta}
    _L0_ffn_all = _L0_ffn_setup()
    _L0_ffn_in = {k: v for k, v in _L0_ffn_all.items() if k in ('Wr', 'br', 'W1', 'b1', 'W2', 'b2', 'gamma', 'beta')}
    del _L0_ffn_all

    def _L1_attn_setup():
        import jax, jax.numpy as jnp
        import numpy as np
        D_MODEL = 64
        N_BRANCH = 4
        PH = 16
        KMAX = 15
        REL_HID = 64
        B, T = (2, 512)
        REL_IN = KMAX + 2
        SCALE_ACT = float(np.pi / np.sqrt(3.0))

        def _rope_tables(t_len, dim):
            inv = 1.0 / 10000.0 ** (np.arange(0, dim, 2, dtype=np.float32) / dim)
            f = np.outer(np.arange(t_len, dtype=np.float32), inv)
            return (jnp.asarray(np.cos(f)), jnp.asarray(np.sin(f)))

        def _rope(x, cos, sin):
            x1 = x[..., 0::2]
            x2 = x[..., 1::2]
            y1 = x1 * cos - x2 * sin
            y2 = x1 * sin + x2 * cos
            return jnp.stack((y1, y2), axis=-1).reshape(x.shape)

        def _l2n(v):
            n = jnp.linalg.norm(v, axis=-1, keepdims=True)
            return v / jnp.maximum(n, 1e-12)

        def _mlp(x, W1, b1, W2, b2):
            h = x @ W1 + b1
            h = h * jax.nn.sigmoid(SCALE_ACT * h)
            return h @ W2 + b2

        def _grid_sample_border(pal, g):
            D, H, W = pal.shape
            gx = jnp.clip((g[..., 0] + 1.0) * 0.5 * (W - 1), 0.0, W - 1.0)
            gy = jnp.clip((g[..., 1] + 1.0) * 0.5 * (H - 1), 0.0, H - 1.0)
            x0 = jnp.floor(gx)
            y0 = jnp.floor(gy)
            wx = gx - x0
            wy = gy - y0
            x0i = x0.astype(jnp.int32)
            y0i = y0.astype(jnp.int32)
            x1i = jnp.minimum(x0i + 1, W - 1)
            y1i = jnp.minimum(y0i + 1, H - 1)
            v00 = pal[:, y0i, x0i]
            v01 = pal[:, y0i, x1i]
            v10 = pal[:, y1i, x0i]
            v11 = pal[:, y1i, x1i]
            out = v00 * (1 - wx) * (1 - wy) + v01 * wx * (1 - wy) + v10 * (1 - wx) * wy + v11 * wx * wy
            return jnp.moveaxis(out, 0, -1)
        key = jax.random.key(seed)
        ks = jax.random.split(key, 12)
        D, BR, H = (D_MODEL, N_BRANCH, REL_HID)
        s = D ** (-0.5)
        return {'x': jax.random.normal(ks[0], (B, T, D), jnp.float32), 'Wi': jax.random.normal(ks[1], (D, BR * D), jnp.float32) * s, 'Wp': jax.random.normal(ks[2], (D, D), jnp.float32) * s, 'W1': jax.random.normal(ks[3], (REL_IN, H), jnp.float32) * REL_IN ** (-0.5), 'b1': jnp.zeros((H,), jnp.float32), 'W2': jax.random.normal(ks[4], (H, H), jnp.float32) * H ** (-0.5), 'b2': jnp.zeros((H,), jnp.float32), 'Wc': jax.random.normal(ks[5], (H, 2), jnp.float32) * H ** (-0.5), 'bc': jnp.zeros((2,), jnp.float32), 'Wm': jax.random.normal(ks[6], (H, 1), jnp.float32) * H ** (-0.5), 'bm': jnp.zeros((1,), jnp.float32), 'palette': jax.random.normal(ks[7], (D, PH, PH), jnp.float32) * s, 'Wo': jax.random.normal(ks[8], (BR, D, D), jnp.float32) * s}
    _L1_attn_all = _L1_attn_setup()
    _L1_attn_in = {k: v for k, v in _L1_attn_all.items() if k in ('Wi', 'Wp', 'W1', 'b1', 'W2', 'b2', 'Wc', 'bc', 'Wm', 'bm', 'palette', 'Wo')}
    del _L1_attn_all

    def _L1_ffn_setup():
        import jax, jax.numpy as jnp
        import numpy as np
        B, S, H, NH, NE = (4, 256, 64, 4, 4)
        D = H // NH
        EPS = 1e-08

        def layernorm(x, g, b):
            m = jnp.mean(x, axis=-1, keepdims=True)
            v = jnp.mean((x - m) ** 2, axis=-1, keepdims=True)
            return (x - m) / jnp.sqrt(v + EPS) * g + b
        key = jax.random.key(seed)
        ks = jax.random.split(key, 18)
        sc = 0.05
        return {'x': jax.random.normal(ks[0], (B, S, H), jnp.float32), 'hl_w': jax.random.normal(ks[1], (NH, D, H), jnp.float32) * sc, 'hl_b': jax.random.normal(ks[2], (NH, D), jnp.float32) * sc, 'wq': jax.random.normal(ks[3], (NH, NE, D, D), jnp.float32) * sc, 'wk': jax.random.normal(ks[4], (NH, D, D), jnp.float32) * sc, 'wv': jax.random.normal(ks[5], (NH, D, D), jnp.float32) * sc, 'gate_w': jax.random.normal(ks[6], (NH, NE, NE * D), jnp.float32) * sc, 'gate_b': jax.random.normal(ks[7], (NH, NE), jnp.float32) * sc, 'ln_g': jnp.ones((D,), jnp.float32), 'ln_b': jnp.zeros((D,), jnp.float32), 'fc1_w': jax.random.normal(ks[8], (D, D), jnp.float32) * sc, 'fc1_b': jax.random.normal(ks[9], (D,), jnp.float32) * sc, 'fc2_w': jax.random.normal(ks[10], (D, D), jnp.float32) * sc, 'fc2_b': jax.random.normal(ks[11], (D,), jnp.float32) * sc, 'fnorm_g': jnp.ones((D,), jnp.float32), 'fnorm_b': jnp.zeros((D,), jnp.float32), 'fgate_w': jax.random.normal(ks[12], (NH, H), jnp.float32) * sc}
    _L1_ffn_all = _L1_ffn_setup()
    _L1_ffn_in = {k: v for k, v in _L1_ffn_all.items() if k in ('hl_w', 'hl_b', 'wq', 'wk', 'wv', 'gate_w', 'gate_b', 'ln_g', 'ln_b', 'fc1_w', 'fc1_b', 'fc2_w', 'fc2_b', 'fnorm_g', 'fnorm_b', 'fgate_w')}
    del _L1_ffn_all
    return {'x': x, 'L0_tok_W_qry': _L0_tok_in['W_qry'], 'L0_tok_W_key': _L0_tok_in['W_key'], 'L0_tok_v': _L0_tok_in['v'], 'L0_tok_b': _L0_tok_in['b'], 'L0_attn_m_u': _L0_attn_in['m_u'], 'L0_attn_m_phi': _L0_attn_in['m_phi'], 'L0_attn_m_y': _L0_attn_in['m_y'], 'L0_attn_eig_vals': _L0_attn_in['eig_vals'], 'L0_attn_eig_vecs': _L0_attn_in['eig_vecs'], 'L0_ffn_Wr': _L0_ffn_in['Wr'], 'L0_ffn_br': _L0_ffn_in['br'], 'L0_ffn_W1': _L0_ffn_in['W1'], 'L0_ffn_b1': _L0_ffn_in['b1'], 'L0_ffn_W2': _L0_ffn_in['W2'], 'L0_ffn_b2': _L0_ffn_in['b2'], 'L0_ffn_gamma': _L0_ffn_in['gamma'], 'L0_ffn_beta': _L0_ffn_in['beta'], 'L1_attn_Wi': _L1_attn_in['Wi'], 'L1_attn_Wp': _L1_attn_in['Wp'], 'L1_attn_W1': _L1_attn_in['W1'], 'L1_attn_b1': _L1_attn_in['b1'], 'L1_attn_W2': _L1_attn_in['W2'], 'L1_attn_b2': _L1_attn_in['b2'], 'L1_attn_Wc': _L1_attn_in['Wc'], 'L1_attn_bc': _L1_attn_in['bc'], 'L1_attn_Wm': _L1_attn_in['Wm'], 'L1_attn_bm': _L1_attn_in['bm'], 'L1_attn_palette': _L1_attn_in['palette'], 'L1_attn_Wo': _L1_attn_in['Wo'], 'L1_ffn_hl_w': _L1_ffn_in['hl_w'], 'L1_ffn_hl_b': _L1_ffn_in['hl_b'], 'L1_ffn_wq': _L1_ffn_in['wq'], 'L1_ffn_wk': _L1_ffn_in['wk'], 'L1_ffn_wv': _L1_ffn_in['wv'], 'L1_ffn_gate_w': _L1_ffn_in['gate_w'], 'L1_ffn_gate_b': _L1_ffn_in['gate_b'], 'L1_ffn_ln_g': _L1_ffn_in['ln_g'], 'L1_ffn_ln_b': _L1_ffn_in['ln_b'], 'L1_ffn_fc1_w': _L1_ffn_in['fc1_w'], 'L1_ffn_fc1_b': _L1_ffn_in['fc1_b'], 'L1_ffn_fc2_w': _L1_ffn_in['fc2_w'], 'L1_ffn_fc2_b': _L1_ffn_in['fc2_b'], 'L1_ffn_fnorm_g': _L1_ffn_in['fnorm_g'], 'L1_ffn_fnorm_b': _L1_ffn_in['fnorm_b'], 'L1_ffn_fgate_w': _L1_ffn_in['fgate_w']}

def reference(x, L0_tok_W_qry, L0_tok_W_key, L0_tok_v, L0_tok_b, L0_attn_m_u, L0_attn_m_phi, L0_attn_m_y, L0_attn_eig_vals, L0_attn_eig_vecs, L0_ffn_Wr, L0_ffn_br, L0_ffn_W1, L0_ffn_b1, L0_ffn_W2, L0_ffn_b2, L0_ffn_gamma, L0_ffn_beta, L1_attn_Wi, L1_attn_Wp, L1_attn_W1, L1_attn_b1, L1_attn_W2, L1_attn_b2, L1_attn_Wc, L1_attn_bc, L1_attn_Wm, L1_attn_bm, L1_attn_palette, L1_attn_Wo, L1_ffn_hl_w, L1_ffn_hl_b, L1_ffn_wq, L1_ffn_wk, L1_ffn_wv, L1_ffn_gate_w, L1_ffn_gate_b, L1_ffn_ln_g, L1_ffn_ln_b, L1_ffn_fc1_w, L1_ffn_fc1_b, L1_ffn_fc2_w, L1_ffn_fc2_b, L1_ffn_fnorm_g, L1_ffn_fnorm_b, L1_ffn_fgate_w):
    import jax
    import jax.numpy as jnp

    def _L0_tok_ref(x, W_qry, W_key, v, b):
        import jax, jax.numpy as jnp
        import numpy as np
        WIN = 9
        N, L, C = x.shape
        n_w = L - WIN + 1
        idx = jnp.arange(n_w)[:, None] + jnp.arange(WIN)[None, :]
        x_win = x[:, idx]
        x_ctr = x[:, WIN // 2:WIN // 2 + n_w]
        key = jnp.einsum('nwsc,cu->nwsu', x_win, W_key)
        qry = jnp.einsum('nwc,cu->nwu', x_ctr, W_qry)
        score = jnp.einsum('nwsu,u->nws', jnp.tanh(qry[:, :, None, :] + key + b), v)
        weight = jax.nn.softmax(score, axis=2)
        out = jnp.einsum('nwsc,nws->nwc', x_win, weight)
        return out

    def _L0_attn_ref(inputs, m_u, m_phi, m_y, eig_vals, eig_vecs):
        import jax, jax.numpy as jnp
        import numpy as np
        B, L, D, K, KU, KY = (4, 512, 64, 24, 3, 2)

        def _hankel_eigh(l, k):
            i = np.arange(1, l + 1, dtype=np.float64)
            s = i[:, None] + i[None, :]
            Z = 2.0 / (s ** 3 - s)
            vals, vecs = np.linalg.eigh(Z)
            return (jnp.asarray(vals[-k:], jnp.float32), jnp.asarray(vecs[:, -k:], jnp.float32))

        def _stu_forward(inputs, m_u, m_phi, m_y, eig_vals, eig_vecs):
            b, l, d = inputs.shape
            k = eig_vals.shape[0]
            n = 2 * l
            V = jnp.fft.rfft(eig_vecs, n=n, axis=0)
            U = jnp.fft.rfft(inputs, n=n, axis=1)
            conv = jnp.fft.irfft(V[None, :, :, None] * U[:, :, None, :], n=n, axis=1)[:, :l]
            x_tilde = conv * (eig_vals ** 0.25)[None, None, :, None]
            delta_phi = x_tilde.reshape(b, l, k * d) @ m_phi
            ar = jnp.zeros_like(delta_phi)
            for i in range(m_u.shape[-1]):
                c = jnp.einsum('oi,bli->blo', m_u[:, :, i], inputs)
                ar = ar + jnp.pad(c, ((0, 0), (i, 0), (0, 0)))[:, :l]
            deltas = delta_phi + ar
            ky = m_y.shape[1]

            def step(carry, delta_t):
                out = jnp.einsum('okd,bkd->bo', m_y, carry) + delta_t
                carry = jnp.concatenate([out[:, None, :], carry[:, :-1, :]], axis=1)
                return (carry, out)
            _, ys = jax.lax.scan(step, jnp.zeros((b, ky, d), deltas.dtype), jnp.swapaxes(deltas, 0, 1))
            return jnp.swapaxes(ys, 0, 1)
        return _stu_forward(inputs, m_u, m_phi, m_y, eig_vals, eig_vecs)

    def _L0_ffn_ref(x, Wr, br, W1, b1, W2, b2, gamma, beta):
        import math
        import jax, jax.numpy as jnp
        import numpy as np
        CAPACITY_FACTOR = 1.25
        TOP_K = 2
        LN_EPS = 1e-05

        def _layer_norm(x, gamma, beta):
            mu = jnp.mean(x, axis=-1, keepdims=True)
            var = jnp.var(x, axis=-1, keepdims=True)
            return (x - mu) * jax.lax.rsqrt(var + LN_EPS) * gamma + beta
        B, S, D = x.shape
        E = Wr.shape[1]
        N = B * S
        K = TOP_K
        logits = jnp.mean(x, axis=1) @ Wr + br
        routing_weights = jax.nn.softmax(logits, axis=-1)
        capacity = float(math.ceil(N * CAPACITY_FACTOR / E))
        expected_loads = routing_weights.sum(axis=0) * (N / B)
        scale = jnp.where(expected_loads > capacity, capacity / expected_loads, 1.0)
        routing_weights = jax.nn.softmax(routing_weights * scale, axis=-1)
        rw_tok = jnp.broadcast_to(routing_weights[:, None, :], (B, S, E)).reshape(N, E)
        top_w, top_i = jax.lax.top_k(rw_tok, K)
        top_w = jax.nn.softmax(top_w, axis=-1)
        xf = x.reshape(N, D)
        h = jax.nn.gelu(jnp.einsum('nd,edf->enf', xf, W1) + b1[:, None, :], approximate=False)
        y = jnp.einsum('enf,efd->end', h, W2) + b2[:, None, :]
        w_dense = jnp.zeros((N, E), x.dtype).at[jnp.arange(N)[:, None], top_i].add(top_w)
        out = jnp.einsum('ne,end->nd', w_dense, y).reshape(B, S, D)
        out = _layer_norm(out + x, gamma, beta)
        return out

    def _L1_attn_ref(x, Wi, Wp, W1, b1, W2, b2, Wc, bc, Wm, bm, palette, Wo):
        import jax, jax.numpy as jnp
        import numpy as np
        D_MODEL = 64
        N_BRANCH = 4
        PH = 16
        KMAX = 15
        REL_HID = 64
        B, T = (2, 512)
        REL_IN = KMAX + 2
        SCALE_ACT = float(np.pi / np.sqrt(3.0))

        def _rope_tables(t_len, dim):
            inv = 1.0 / 10000.0 ** (np.arange(0, dim, 2, dtype=np.float32) / dim)
            f = np.outer(np.arange(t_len, dtype=np.float32), inv)
            return (jnp.asarray(np.cos(f)), jnp.asarray(np.sin(f)))

        def _rope(x, cos, sin):
            x1 = x[..., 0::2]
            x2 = x[..., 1::2]
            y1 = x1 * cos - x2 * sin
            y2 = x1 * sin + x2 * cos
            return jnp.stack((y1, y2), axis=-1).reshape(x.shape)

        def _l2n(v):
            n = jnp.linalg.norm(v, axis=-1, keepdims=True)
            return v / jnp.maximum(n, 1e-12)

        def _mlp(x, W1, b1, W2, b2):
            h = x @ W1 + b1
            h = h * jax.nn.sigmoid(SCALE_ACT * h)
            return h @ W2 + b2

        def _grid_sample_border(pal, g):
            D, H, W = pal.shape
            gx = jnp.clip((g[..., 0] + 1.0) * 0.5 * (W - 1), 0.0, W - 1.0)
            gy = jnp.clip((g[..., 1] + 1.0) * 0.5 * (H - 1), 0.0, H - 1.0)
            x0 = jnp.floor(gx)
            y0 = jnp.floor(gy)
            wx = gx - x0
            wy = gy - y0
            x0i = x0.astype(jnp.int32)
            y0i = y0.astype(jnp.int32)
            x1i = jnp.minimum(x0i + 1, W - 1)
            y1i = jnp.minimum(y0i + 1, H - 1)
            v00 = pal[:, y0i, x0i]
            v01 = pal[:, y0i, x1i]
            v10 = pal[:, y1i, x0i]
            v11 = pal[:, y1i, x1i]
            out = v00 * (1 - wx) * (1 - wy) + v01 * wx * (1 - wy) + v10 * (1 - wx) * wy + v11 * wx * wy
            return jnp.moveaxis(out, 0, -1)
        Bn, Tn, D = x.shape
        BR = Wo.shape[0]
        K = KMAX
        scale = D ** (-0.5)
        cos, sin = _rope_tables(Tn, D)
        I = (x @ Wi).reshape(Bn, Tn, BR, D).transpose(0, 2, 1, 3)
        P = x @ Wp
        I = _rope(I, cos, sin)
        P = _rope(P, cos, sin)
        logits = jnp.einsum('brtd,bsd->brts', I, P) * scale
        causal = jnp.tril(jnp.ones((Tn, Tn), bool))
        logits = jnp.where(causal, logits, -jnp.inf)
        topk_val, topk_idx = jax.lax.top_k(logits, K)
        keep = jnp.isfinite(topk_val)
        keep_f = keep.astype(x.dtype)
        P_sel = jax.vmap(lambda p, i: p[i])(P, topk_idx)
        P_sel_n = _l2n(P_sel) * keep_f[..., None]
        I_n = _l2n(I)[:, :, :, None, :]
        feat_a = jnp.clip(jnp.sum(I_n * P_sel_n, -1), -1.0, 1.0) * keep_f
        G = jnp.clip(jnp.einsum('brtkd,brtjd->brtkj', P_sel_n, P_sel_n), -1.0, 1.0)
        G = G * keep_f[..., :, None] * keep_f[..., None, :]
        t_rng = jnp.arange(Tn)[None, None, :, None]
        delta = jnp.maximum((t_rng - topk_idx).astype(x.dtype), 0.0) / max(1.0, float(Tn))
        delta = delta * keep_f
        rel = jnp.concatenate([G, feat_a[..., None], delta[..., None]], -1)
        h = _mlp(rel, W1, b1, W2, b2)
        z = jnp.tanh(h @ Wc + bc)
        mix = jnp.where(keep, (h @ Wm + bm)[..., 0], -jnp.inf)
        w = jnp.nan_to_num(jax.nn.softmax(mix, axis=-1), nan=0.0)
        samples = _grid_sample_border(palette, z)
        V = jnp.sum(samples * w[..., None], axis=3)
        y = jnp.einsum('brtd,rdm->brtm', V, Wo).mean(axis=1)
        return y

    def _L1_ffn_ref(x, hl_w, hl_b, wq, wk, wv, gate_w, gate_b, ln_g, ln_b, fc1_w, fc1_b, fc2_w, fc2_b, fnorm_g, fnorm_b, fgate_w):
        import jax, jax.numpy as jnp
        import numpy as np
        B, S, H, NH, NE = (4, 256, 64, 4, 4)
        D = H // NH
        EPS = 1e-08

        def layernorm(x, g, b):
            m = jnp.mean(x, axis=-1, keepdims=True)
            v = jnp.mean((x - m) ** 2, axis=-1, keepdims=True)
            return (x - m) / jnp.sqrt(v + EPS) * g + b
        b, s, h = x.shape
        nh, d, _ = wk.shape
        ne = wq.shape[1]
        sx = jnp.einsum('bsh,ndh->bnsd', x, hl_w) + hl_b[None, :, None, :]
        pad = sx == 0
        q = jnp.einsum('bnsd,neod->bneso', sx, wq)
        k = jnp.einsum('bnsd,nod->bnso', sx, wk)
        v = jnp.einsum('bnsd,nod->bnso', sx, wv)
        causal = jnp.where(jnp.tril(jnp.ones((s, s), bool)), 0.0, -jnp.inf).astype(x.dtype)
        scores = jnp.einsum('bnesd,bntd->bnest', q, k) * d ** 0.5 + causal
        att = jax.nn.softmax(scores, axis=-1)
        qkv = jnp.einsum('bnest,bntd->bnesd', att, v)
        qkv = jnp.where(pad[:, :, None], 0.0, qkv)
        out = jnp.transpose(qkv, (0, 1, 3, 2, 4)).reshape(b, nh, s, ne * d)
        gs = jax.nn.softmax(jnp.einsum('bnsf,nef->bnse', out, gate_w) + gate_b[None, :, None, :], axis=-1)
        mixed = jnp.einsum('bnsed,bnse->bnsd', out.reshape(b, nh, s, ne, d), gs)
        resid = sx[jnp.arange(nh), jnp.arange(nh)]
        hn = layernorm(mixed + resid, ln_g, ln_b)
        f_n = jnp.transpose(hn, (0, 2, 1, 3)).reshape(b, s, h)
        fx = f_n.reshape(b, s, nh, d)
        pm = fx == 0
        hx = jnp.where(pm, 0.0, fx @ fc1_w.T + fc1_b)
        hx = jax.nn.relu(hx)
        hx = jnp.where(pm, 0.0, hx @ fc2_w.T + fc2_b)
        hx = layernorm(hx + fx, fnorm_g, fnorm_b)
        fout = hx.reshape(b, s, h)
        fg = jax.nn.softmax(fout @ fgate_w.T, axis=-1)
        return (fout.reshape(b, s, nh, d) * fg[..., None]).reshape(b, s, h)
    h = _L0_tok_ref(x, L0_tok_W_qry, L0_tok_W_key, L0_tok_v, L0_tok_b)
    h = h + _L0_attn_ref(_layernorm(h, axis=-1), L0_attn_m_u, L0_attn_m_phi, L0_attn_m_y, L0_attn_eig_vals, L0_attn_eig_vecs)
    h = h + _L0_ffn_ref(_layernorm(h, axis=-1), L0_ffn_Wr, L0_ffn_br, L0_ffn_W1, L0_ffn_b1, L0_ffn_W2, L0_ffn_b2, L0_ffn_gamma, L0_ffn_beta)
    h = h + _L1_attn_ref(_layernorm(h, axis=-1), L1_attn_Wi, L1_attn_Wp, L1_attn_W1, L1_attn_b1, L1_attn_W2, L1_attn_b2, L1_attn_Wc, L1_attn_bc, L1_attn_Wm, L1_attn_bm, L1_attn_palette, L1_attn_Wo)
    h = h + _L1_ffn_ref(_layernorm(h, axis=-1), L1_ffn_hl_w, L1_ffn_hl_b, L1_ffn_wq, L1_ffn_wk, L1_ffn_wv, L1_ffn_gate_w, L1_ffn_gate_b, L1_ffn_ln_g, L1_ffn_ln_b, L1_ffn_fc1_w, L1_ffn_fc1_b, L1_ffn_fc2_w, L1_ffn_fc2_b, L1_ffn_fnorm_g, L1_ffn_fnorm_b, L1_ffn_fgate_w)
    return h

_drawn_inputs = setup_inputs


def setup_inputs(seed=0):
    import zlib

    import numpy as np

    out = dict(_drawn_inputs(seed))
    spreads = {'L0_tok_b': (0.0, 0.8),
     'L0_ffn_br': (0.0, 0.1),
     'L0_ffn_b1': (0.0, 0.519),
     'L0_ffn_b2': (0.0, 0.366),
     'L0_ffn_gamma': (1.0, 0.2),
     'L0_ffn_beta': (0.0, 0.1),
     'L1_attn_b1': (0.0, 0.8),
     'L1_attn_b2': (0.0, 0.8),
     'L1_attn_bc': (0.0, 0.8),
     'L1_ffn_ln_g': (1.0, 0.6),
     'L1_ffn_ln_b': (0.0, 0.8),
     'L1_ffn_fnorm_g': (1.0, 0.6),
     'L1_ffn_fnorm_b': (0.0, 0.8)}
    factors = {'L1_attn_Wi': 8.0,
     'L1_attn_Wp': 8.0,
     'L1_attn_W1': 8.0,
     'L1_attn_W2': 8.0,
     'L1_attn_Wc': 8.0,
     'L1_attn_Wm': 8.0,
     'L1_attn_palette': 8.0,
     'L1_attn_Wo': 8.0,
     'L1_ffn_hl_b': 4.656,
     'L1_ffn_wq': 8.0,
     'L1_ffn_wk': 8.0,
     'L1_ffn_wv': 7.154,
     'L1_ffn_gate_w': 8.0,
     'L1_ffn_gate_b': 64.0,
     'L1_ffn_fc1_w': 8.0,
     'L1_ffn_fc1_b': 31.566,
     'L1_ffn_fc2_w': 8.0,
     'L1_ffn_fc2_b': 22.629}
    for name, (base, spread) in spreads.items():
        noise = np.random.default_rng([zlib.crc32(name.encode()), seed]).standard_normal(out[name].shape)
        drawn = base * np.exp(spread * noise) if base else spread * noise
        out[name] = jnp.asarray(drawn.astype(out[name].dtype))
    for name, factor in factors.items():
        out[name] = (out[name] * factor).astype(out[name].dtype)
    return out
```

```python
import math
from contextlib import ExitStack

import numpy as np
import concourse.bass as bass
from concourse import mybir

ALU = mybir.AluOpType
ACT = mybir.ActivationFunctionType
AX = mybir.AxisListType
F32 = mybir.dt.float32
BF16 = mybir.dt.bfloat16
U32 = mybir.dt.uint32

B, L, C = 32, 256, 64
WIN = 9
T = L - WIN + 1
H = T // 2


class Phase:

    def __init__(self, nc, tag):
        self.nc, self.tag, self.stack, self.sems = nc, tag, ExitStack(), []

    def __enter__(self):
        self.stack.__enter__()
        return self

    def __exit__(self, *e):
        self.stack.__exit__(*e)
        self.nc.clear_and_free_semaphores(self.sems)
        self.nc.all_engine_barrier()

    def sb(self, name, shape, dt=F32):
        return self.stack.enter_context(self.nc.sbuf_tensor(f"{self.tag}_{name}", shape, dt))

    def ps(self, name, shape, dt=F32):
        return self.stack.enter_context(self.nc.psum_tensor(f"{self.tag}_{name}", shape, dt))

    def sem(self, name):
        self.sems.append(self.nc.alloc_semaphore(name=f"{self.tag}_{name}"))
        return self.sems[-1]

    def block(self):
        return self.stack.enter_context(self.nc.Block())


def bcast(ap, at, n):
    steps = [list(x) for x in ap.ap]
    return bass.AP(tensor=ap.tensor, offset=ap.offset, ap=steps[:at] + [[0, n]] + steps[at:])


def on_partitions(ap, n):
    return bass.AP(tensor=ap.tensor, offset=ap.offset, ap=[[0, n]] + [list(x) for x in ap.ap])


def token_attention(nc, d):
    with Phase(nc, "tok") as m:
        ident = m.sb("ident", [128, 128])
        w_key = m.sb("w_key", [128, 128])
        w_qry = m.sb("w_qry", [128, 128])
        v_two = m.sb("v_two", [128, 2])
        b_col = m.sb("b_col", [128, 1])
        x_rows = [m.sb(f"x_rows{p}", [128, 2, 2, C]) for p in range(2)]
        x_win = [m.sb(f"x_win{p}", [H, 4, WIN * C]) for p in range(2)]
        x_t = m.sb("x_t", [128, L])
        key = m.sb("key", [128, L])
        qry = m.sb("qry", [128, T])
        pre = [m.sb(f"pre{p}", [128, WIN, T]) for p in range(2)]
        th = [m.sb(f"th{p}", [128, WIN, T]) for p in range(2)]
        top = m.sb("top", [H, 4])
        low = m.sb("low", [H, 4, WIN])
        exps = m.sb("exps", [H, 4, WIN])
        tot = m.sb("tot", [H, 4])
        wt = m.sb("wt", [H, 4, WIN])
        h0 = [m.sb(f"h0{p}", [H, 4, C]) for p in range(2)]
        p_xt = m.ps("p_xt", [128, 512])
        p_key = m.ps("p_key", [128, 512])
        p_qry = m.ps("p_qry", [128, 512])
        p_score = m.ps("p_score", [128, 512])
        cleared, consts = m.sem("cleared"), m.sem("consts")
        rows_in = [m.sem(f"rows_in{p}") for p in range(2)]
        win_in = [m.sem(f"win_in{p}") for p in range(2)]
        xt_done, xt_sb, kq_done, kq_sb = m.sem("xt_done"), m.sem("xt_sb"), m.sem("kq_done"), m.sem("kq_sb")
        pre_dve, pre_pool, th_done = m.sem("pre_dve"), m.sem("pre_pool"), m.sem("th_done")
        score_done, low_done, exps_done = m.sem("score_done"), m.sem("low_done"), m.sem("exps_done")
        h0_done = m.sem("h0_done")
        stored = [m.sem(f"stored{p}") for p in range(2)]
        score = p_score[0:H, 0:4 * WIN].rearrange("p (g s) -> p g s", s=WIN)
        DVE_S = 4
        N = B // 2
        blk = m.block()

        @blk.sync
        def _(sp):
            sp.wait_ge(cleared, 3)
            for a in range(2):
                half = slice(64 * a, 64 * a + 64)
                sp.dma_start(w_key[half, half], d["L0_tok_W_key"]).then_inc(consts, 16)
                sp.dma_start(w_qry[half, half], d["L0_tok_W_qry"]).then_inc(consts, 16)
                sp.dma_start(v_two[half, a:a + 1], d["L0_tok_v"].rearrange("(p a) -> p a", a=1)).then_inc(consts, 16)
                sp.dma_start(b_col[half, :], d["L0_tok_b"].rearrange("(p a) -> p a", a=1)).then_inc(consts, 16)
            sp.dma_start(ident[:, :], d["c_ident"]).then_inc(consts, 16)
            with sp.Fori(0, N // 2) as i:
                for p in range(2):
                    n = i * 2 + p
                    pair = d["x"][bass.ds(n * 2, 2), :, :]
                    sp.wait_ge(xt_done, n + 1)
                    sp.dma_start(x_rows[p][:, 0, :, :], pair[:, 0:128, :].rearrange("a p c -> p a c")).then_inc(rows_in[p], 16)
                    sp.dma_start(x_rows[p][:, 1, :, :], pair[:, 128:256, :].rearrange("a p c -> p a c")).then_inc(rows_in[p], 16)
                    sp.wait_ge(h0_done, n + 1)
                    for g in range(4):
                        src = bass.AP(tensor=pair.tensor, offset=pair.offset + ((g % 2) * L + (g // 2) * H) * C,
                                      ap=[[C, H], [1, WIN * C]])
                        sp.dma_start(x_win[p][:, g, :], src).then_inc(win_in[p], 16)
            for p in range(2):
                sp.wait_ge(stored[p], 32 * (N // 2) + 32)

        @blk.gpsimd
        def _(pool):
            for t in (w_key, w_qry, v_two):
                pool.memset(t[:, :], 0.0).then_inc(cleared, 1)
            with pool.Fori(0, N // 2) as i:
                for p in range(2):
                    n = i * 2 + p
                    pool.wait_ge(kq_sb, n * 2 + 2)
                    pool.wait_ge(th_done, n + 1)
                    for s in range(DVE_S, WIN):
                        ins = pool.tensor_tensor(pre[p][:, s, :], key[:, s:s + T], qry[:, :], ALU.add)
                    ins.then_inc(pre_pool, 1)

        @blk.scalar
        def _(act):
            act.wait_ge(consts, 16 * 9)
            act.sem_inc(xt_done, 2)
            act.sem_inc(h0_done, 2)
            act.sem_inc(th_done, 2)
            act.sem_inc(pre_dve, 1)
            act.sem_inc(pre_pool, 1)
            with act.Fori(0, N // 2) as i:
                for p in range(2):
                    n = i * 2 + p
                    act.wait_ge(xt_done, n + 3)
                    act.activation(x_t[:, :], p_xt[:, 0:L], ACT.Copy).then_inc(xt_sb, 1)
                    act.wait_ge(kq_done, n + 1)
                    act.wait_ge(pre_dve, n + 1)
                    act.wait_ge(pre_pool, n + 1)
                    act.activation(key[:, :], p_key[:, 0:L], ACT.Copy).then_inc(kq_sb, 1)
                    act.activation(qry[:, :], p_qry[:, 0:T], ACT.Identity, bias=b_col[:, 0:1]).then_inc(kq_sb, 1)
                    act.wait_ge(pre_dve, n + 2)
                    act.wait_ge(pre_pool, n + 2)
                    act.activation(th[p][:, :, :], pre[p][:, :, :], ACT.Tanh).then_inc(th_done, 1)
                    act.wait_ge(low_done, n + 1)
                    act.activation(exps[:, :, :], low[:, :, :], ACT.Exp).then_inc(exps_done, 1)
                    act.wait_ge(h0_done, n + 3)
                    act.dma_start(d["h0"][bass.ds(n * 2, 2), 0:H, :].rearrange("a p c -> p a c"), h0[p][:, 0:2, :]).then_inc(stored[p], 16)
                    act.dma_start(d["h0"][bass.ds(n * 2, 2), H:T, :].rearrange("a p c -> p a c"), h0[p][:, 2:4, :]).then_inc(stored[p], 16)

        @blk.tensor
        def _(pe):
            pe.wait_ge(consts, 16 * 9)
            with pe.Fori(0, N // 2) as i:
                for p in range(2):
                    n = i * 2 + p
                    pe.wait_ge(rows_in[p], i * 32 + 32)
                    for h in range(2):
                        ins = pe.transpose(p_xt[:, 128 * h:128 * h + 128], x_rows[p][:, h, :, :].rearrange("p a c -> p (a c)"), ident[:, :])
                    ins.then_inc(xt_done, 1)
                    pe.wait_ge(xt_sb, n + 1)
                    pe.matmul(p_key[:, 0:L], w_key[:, :], x_t[:, :], start=True, stop=True)
                    pe.matmul(p_qry[:, 0:T], w_qry[:, :], x_t[:, WIN // 2:WIN // 2 + T], start=True, stop=True).then_inc(kq_done, 1)
                    pe.wait_ge(th_done, n + 3)
                    for t in range(2):
                        for s in range(WIN):
                            ins = pe.matmul(score[:, 2 * t:2 * t + 2, s], th[p][:, s, H * t:H * t + H], v_two[:, :], start=True, stop=True)
                    ins.then_inc(score_done, 1)

        @blk.vector
        def _(dve):
            for p in range(2):
                dve.sem_inc(stored[p], 32)
            with dve.Fori(0, N // 2) as i:
                for p in range(2):
                    n = i * 2 + p
                    dve.wait_ge(kq_sb, n * 2 + 2)
                    dve.wait_ge(th_done, n + 1)
                    for s in range(DVE_S):
                        ins = dve.tensor_tensor(pre[p][:, s, :], key[:, s:s + T], qry[:, :], ALU.add)
                    ins.then_inc(pre_dve, 1)
                    dve.wait_ge(score_done, n + 1)
                    dve.tensor_reduce(top[:, :], score, AX.X, ALU.max)
                    dve.drain()
                    dve.tensor_tensor(low[:, :, :], score, bcast(top[:, :], 2, WIN), ALU.subtract).then_inc(low_done, 1)
                    dve.wait_ge(exps_done, n + 1)
                    dve.tensor_reduce(tot[:, :], exps[:, :, :], AX.X, ALU.add)
                    dve.drain()
                    dve.reciprocal(tot[:, :], tot[:, :])
                    dve.drain()
                    dve.tensor_tensor(wt[:, :, :], exps[:, :, :], bcast(tot[:, :], 2, WIN), ALU.mult)
                    dve.drain()
                    dve.wait_ge(win_in[p], i * 64 + 64)
                    xw = x_win[p][:, :, :].rearrange("p g (s c) -> p (g s) c", c=C)
                    dve.tensor_tensor(xw, xw, bcast(wt[:, :, :].rearrange("p g s -> p (g s)"), 2, C), ALU.mult)
                    dve.drain()
                    dve.wait_ge(stored[p], i * 32 + 32)
                    dve.tensor_reduce(h0[p][:, :, :], x_win[p][:, :, :].rearrange("p g (s c) -> p g c s", c=C), AX.X, ALU.add).then_inc(h0_done, 1)


NF = T + 1
FQ = [(0, 125), (125, 124)]
NK, NU = 24, 3
CH, NCH = 8, T // 8


def stu_constants():
    n = 2 * T
    f = np.arange(NF)
    ang = 2 * np.pi * ((np.arange(n)[:, None] * f[None, :]) % n) / n
    cos, sin = np.cos(ang), np.sin(ang)
    fwd = np.concatenate([cos, -sin], 1).reshape(4, H, 2 * NF).transpose(1, 0, 2)
    rot = np.concatenate([sin, cos], 1).reshape(4, H, 2 * NF).transpose(1, 0, 2)
    taps = np.zeros((59, 2 * NF))
    taps[24:27] = np.concatenate([cos, -sin], 1)[:NU]
    taps[56:59] = np.concatenate([sin, cos], 1)[:NU]
    w = np.where((f == 0) | (f == T), 1.0, 2.0)[:, None] / n
    inv = np.zeros((125, 2, 2, T))
    for a, (f0, nf) in enumerate(FQ):
        inv[:nf, a, 0] = (w * cos.T[:, :T])[f0:f0 + nf]
        inv[:nf, a, 1] = (-w * sin.T[:, :T])[f0:f0 + nf]
    low = np.concatenate([np.eye(64), np.zeros((64, 64))], 1)
    return {"c_fwd": fwd, "c_rot": rot, "c_taps": taps, "c_inv": inv, "c_low": low}


def spectral_unit(nc, d):
    with Phase(nc, "stu") as m:
        ident = m.sb("ident", [128, 128])
        u = m.sb("u", [H, 2, B, C])
        spec_in = m.sb("spec_in", [128, NF, B])
        spec_out = m.sb("spec_out", [128, NF, B])
        mix = m.sb("mix", [128, 125, 128])
        filt_w = m.sb("filt_w", [128, 2, C, C])
        fwd = m.sb("fwd", [H, 4, 2 * NF])
        rot = m.sb("rot", [H, 4, 2 * NF])
        inv = m.sb("inv", [125, 2, 2, T])
        spec_t = [m.sb(f"spec_t{p}", [125, 2, 128]) for p in range(2)]
        filt = m.sb("filt", [128, 2 * NF])
        eig = m.sb("eig", [H, 4, NK])
        lam = m.sb("lam", [64, 3])
        st = m.sb("st", [H, 4, 64])
        comp = m.sb("comp", [128, 128])
        power = m.sb("power", [128, CH, 64])
        step8 = m.sb("step8", [128, 128])
        rows = spec_out[:, :, :].rearrange("p f b -> p (f b)")[0:H, 0:2 * B * C].rearrange("p (t b c) -> p t b c", t=2, b=B)
        sq = mix[:, :, :].rearrange("p f b -> p (f b)")[0:H, 0:2 * B * C].rearrange("p (t b c) -> p t b c", t=2, b=B)
        flat = mix[:, :, :].rearrange("p f b -> p (f b)")
        loc = flat[:, 0:CH * NCH * B].rearrange("p (j c b) -> p j c b", j=CH, b=B)
        state = flat[:, CH * NCH * B:CH * NCH * B + NCH * B].rearrange("p (c b) -> p c b", b=B)
        res = filt_w[:, :, :, :].rearrange("p a d o -> p (a d o)")[0:H, 0:2 * B * C].rearrange("p (t b c) -> p t b c", t=2, b=B)
        bank = [m.ps(f"bank{k}", [128, 512]) for k in range(8)]
        S = {n: m.sem(n) for n in "cleared consts rows_in small_in ln ln_act v_done v_sb dft dft_dve dft_act hmat hmat_dve hmat_act freq freq_sb back back_sb delta delta_sb pw pw_sb locmm loc_add loc_copy chain chain_sb carry carry_sb res_in fin fin_sb out scan0".split()}
        rsv = lambda a: a.rearrange("p t b c -> p (t b) c")
        blk = m.block()

        @blk.sync
        def _(sp):
            for t in range(2):
                sp.dma_start(rows[:, t, :, :], d["h0"][:, H * t:H * t + H, :].rearrange("b p c -> p b c")).then_inc(S["rows_in"], 16)
            sp.dma_start(fwd[:, :, :], d["c_fwd"]).then_inc(S["consts"], 16)
            sp.dma_start(rot[:, :, :], d["c_rot"]).then_inc(S["consts"], 16)
            sp.dma_start(inv[:, :, :, :], d["c_inv"]).then_inc(S["consts"], 16)
            sp.dma_start(ident[:, :], d["c_ident"]).then_inc(S["consts"], 16)
            sp.dma_start(filt[0:59, :], d["c_taps"]).then_inc(S["consts"], 16)
            sp.dma_start(eig[:, :, :], d["L0_attn_eig_vecs"][0:2 * T, :].rearrange("(a p) k -> p a k", p=H)).then_inc(S["consts"], 16)
            for a in range(2):
                sp.dma_start(lam[32 * a:32 * a + NK, 0:1], d["L0_attn_eig_vals"].rearrange("(p a) -> p a", a=1)).then_inc(S["consts"], 16)
            sp.dma_start(comp[0:64, :], d["L0_attn_m_y"].rearrange("o k d -> o (k d)")).then_inc(S["consts"], 16)
            sp.dma_start(comp[64:128, :], d["c_low"]).then_inc(S["consts"], 16)
            sp.wait_ge(S["cleared"], 1)
            for a in range(2):
                sp.dma_start(filt_w[32 * a:32 * a + NK, a, :, :], d["L0_attn_m_phi"].rearrange("(k d) o -> k d o", k=NK)).then_inc(S["consts"], 16)
                sp.dma_start(filt_w[32 * a + NK:32 * a + NK + NU, a, :, :], d["m_u_taps"]).then_inc(S["consts"], 16)
            sp.wait_ge(S["hmat"], 128)
            h0_steps = d["h0"].rearrange("b (c t j) o -> t j c b o", t=2, j=4)
            h1_steps = d["h1"].rearrange("b (c t j) o -> t j c b o", t=2, j=4)
            for t in range(2):
                for j in range(4):
                    sp.dma_start(res[NCH * j:NCH * j + NCH, t, :, :], h0_steps[t, j]).then_inc(S["res_in"], 16)
            for t in range(2):
                sp.wait_ge(S["fin_sb"], 4 * t + 4)
                for j in range(4):
                    sp.dma_start(h1_steps[t, j], res[NCH * j:NCH * j + NCH, t, :, :]).then_inc(S["out"], 16)
            sp.wait_ge(S["out"], 128)

        @blk.gpsimd
        def _(pool):
            pool.memset(filt_w[0:64, :, :, :], 0.0).then_inc(S["cleared"], 1)

        @blk.scalar
        def _(act):
            act.wait_ge(S["consts"], 16 * 14)
            for a in range(2):
                q = slice(32 * a, 32 * a + NK)
                act.activation(lam[q, 1:2], lam[q, 0:1], ACT.Sqrt)
            act.drain()
            for a in range(2):
                q = slice(32 * a, 32 * a + NK)
                act.activation(lam[q, 2:3], lam[q, 1:2], ACT.Sqrt)
            act.drain()
            act.wait_ge(S["ln"], 1)
            act.activation(st[:, 2, :], st[:, 1, :], ACT.Sqrt).then_inc(S["ln_act"], 1)
            act.wait_ge(S["v_done"], 1)
            for a in range(2):
                q = slice(32 * a, 32 * a + NK)
                act.activation(filt[q, :], bank[a][q, 0:2 * NF], ACT.Copy, scale=lam[q, 2:3]).then_inc(S["v_sb"], 1)
            for k in range(1, B, 2):
                act.wait_ge(S["dft"], k + 1)
                act.activation(spec_in[:, :, k], bank[2 + k % 4][:, 0:NF], ACT.Copy).then_inc(S["dft_act"], 1)
            for t, (f0, nf) in enumerate(FQ):
                if t:
                    act.wait_ge(S["freq"], 8)
                for o in range(1, 64, 2):
                    act.wait_ge(S["hmat"], 64 * t + o + 1)
                    act.activation(mix[:, 0:nf, :].rearrange("p f (r o) -> p r f o", r=2)[:, :, :, o],
                                   bank[o % 4][:, 0:2 * nf].rearrange("p (r f) -> p r f", r=2), ACT.Copy).then_inc(S["hmat_act"], 1)
            for k in range(B):
                act.wait_ge(S["back"], k + 1)
                if k >= 2:
                    act.wait_ge(S["delta"], k - 1)
                for t, (f0, nf) in enumerate(FQ):
                    ins = act.activation(spec_t[k % 2][0:nf, t, :], bank[k % 2][0:nf, 128 * t:128 * t + 128], ACT.Copy)
                ins.then_inc(S["back_sb"], 1)
            for j in range(1, CH):
                if j > 1:
                    act.wait_ge(S["loc_add"], 2 * (j - 1))
                else:
                    act.wait_ge(S["delta_sb"], B)
                act.activation(loc[64:128, j, :, :], loc[0:64, j - 1, :, :], ACT.Copy).then_inc(S["loc_copy"], 1)

        @blk.tensor
        def _(pe):
            pe.wait_ge(S["consts"], 16 * 14)
            for a, table in enumerate((fwd, rot)):
                for t in range(4):
                    ins = pe.matmul(bank[a][32 * a:32 * a + NK, 0:2 * NF], eig[:, t, :], table[:, t, :], start=(t == 0), stop=(t == 3))
            ins.then_inc(S["v_done"], 1)
            pe.transpose(bank[7][:, 0:64], comp[0:64, :], ident[0:64, 0:64]).then_inc(S["pw"], 1)
            for j in range(1, CH):
                pe.wait_ge(S["pw_sb"], j)
                pe.matmul(bank[7][:, 64 * j:64 * j + 64], comp[:, :], power[:, j - 1, :], start=True, stop=True).then_inc(S["pw"], 1)
            pe.wait_ge(S["ln"], 2)
            for k in range(B):
                if k >= 4:
                    pe.wait_ge(S["dft_act" if k % 2 else "dft_dve"], (k - 4) // 2 + 1)
                for r in range(2):
                    for t in range(2):
                        ins = pe.matmul(bank[2 + k % 4][64 * r:64 * r + 64, 0:NF], u[:, t, k, :], fwd[:, t, NF * r:NF * r + NF], start=(t == 0), stop=(t == 1))
                ins.then_inc(S["dft"], 1)
            pe.wait_ge(S["v_sb"], 2)
            for t, (f0, nf) in enumerate(FQ):
                for o in range(64):
                    g = 64 * t + o
                    if g == 0:
                        pe.wait_ge(S["dft_dve"], B // 2)
                        pe.wait_ge(S["dft_act"], B // 2)
                    if g >= 4:
                        pe.wait_ge(S["hmat_act" if g % 2 else "hmat_dve"], (g - 4) // 2 + 1)
                    pe.matmul(bank[o % 4][:, 0:2 * nf], filt_w[0:59, :, :, o],
                              filt[0:59, :].rearrange("p (r f) -> p r f", r=2)[:, :, f0:f0 + nf], start=True, stop=True).then_inc(S["hmat"], 1)
                pe.wait_ge(S["hmat_dve"], 32 * t + 32)
                pe.wait_ge(S["hmat_act"], 32 * t + 32)
                for k in range((nf + 15) // 16):
                    if k >= 4 or t:
                        pe.wait_ge(S["freq_sb"], 8 * t + k - 3)
                    for f in range(16 * k, min(nf, 16 * k + 16)):
                        ins = pe.matmul(bank[4 + k % 4][:, 32 * (f - 16 * k):32 * (f - 16 * k) + 32], mix[:, f, :], spec_in[:, f0 + f, :], start=True, stop=True)
                    ins.then_inc(S["freq"], 1)
            pe.wait_ge(S["freq_sb"], 16)
            for k in range(B):
                if k >= 2:
                    pe.wait_ge(S["back_sb"], k - 1)
                for t, (f0, nf) in enumerate(FQ):
                    ins = pe.transpose(bank[k % 2][0:nf, 128 * t:128 * t + 128], spec_out[:, f0:f0 + nf, k], ident[:, :])
                ins.then_inc(S["back"], 1)
                pe.wait_ge(S["back_sb"], k + 1)
                if k >= 2:
                    pe.wait_ge(S["delta_sb"], k - 1)
                for t, (f0, nf) in enumerate(FQ):
                    for r in range(2):
                        ins = pe.matmul(bank[2 + k % 2][0:64, 0:T], spec_t[k % 2][0:nf, t, 64 * r:64 * r + 64], inv[0:nf, t, r, :],
                                        start=(t == 0 and r == 0), stop=(t == 1 and r == 1))
                ins.then_inc(S["delta"], 1)
            half = loc.rearrange("p j c b -> p j (c b)")
            NH = NCH * B // 2
            for j in range(1, CH):
                pe.wait_ge(S["scan0"], 1)
                if j > 1:
                    pe.wait_ge(S["loc_copy"], j - 1)
                for a in range(2):
                    if j > 1:
                        pe.wait_ge(S["loc_add"], 2 * (j - 2) + a + 1)
                    else:
                        pe.wait_ge(S["delta_sb"], B)
                    pe.matmul(bank[4 + a][0:64, 0:NH], power[:, 0, :], half[:, j - 1, NH * a:NH * a + NH], start=True, stop=True).then_inc(S["locmm"], 1)
            for c in range(NCH - 1):
                if c == 0:
                    pe.wait_ge(S["loc_copy"], CH - 1)
                pe.wait_ge(S["chain_sb"], c + 1)
                pe.matmul(bank[c % 2][:, 0:B], step8[:, :], state[:, c, :], start=True, stop=True).then_inc(S["chain"], 1)
            pe.wait_ge(S["chain_sb"], NCH)
            st2 = state.rearrange("p c b -> p (c b)")
            for j in range(CH):
                for a in range(2):
                    if 2 * j + a >= 4:
                        pe.wait_ge(S["carry_sb"], 2 * j + a - 3)
                    pe.matmul(bank[4 + (2 * j + a) % 4][0:64, 0:NH], power[:, j, :], st2[:, NH * a:NH * a + NH], start=True, stop=True).then_inc(S["carry"], 1)
            pe.wait_ge(S["carry_sb"], 2 * CH)
            for k in range(8):
                t, b0 = k // 4, 8 * (k % 4)
                if k >= 4:
                    pe.wait_ge(S["fin_sb"], k - 3)
                for b in range(8):
                    ins = pe.transpose(bank[k % 4][0:H, 64 * b:64 * b + 64], loc[0:64, 4 * t:4 * t + 4, :, b0 + b], ident[0:64, 0:64])
                ins.then_inc(S["fin"], 1)

        @blk.vector
        def _(dve):
            dve.wait_ge(S["rows_in"], 32)
            dve.tensor_reduce(st[:, 0, :], rsv(rows), AX.X, ALU.add)
            dve.drain()
            dve.tensor_scalar(st[:, 0, :], st[:, 0, :], 1.0 / C, None, ALU.mult)
            dve.drain()
            dve.tensor_tensor(rsv(rows), rsv(rows), bcast(st[:, 0, :], 2, C), ALU.subtract)
            dve.drain()
            dve.tensor_tensor(rsv(sq), rsv(rows), rsv(rows), ALU.mult)
            dve.drain()
            dve.tensor_reduce(st[:, 1, :], rsv(sq), AX.X, ALU.add)
            dve.drain()
            dve.tensor_scalar(st[:, 1, :], st[:, 1, :], 1.0 / C, 1e-5, ALU.mult, ALU.add).then_inc(S["ln"], 1)
            for j in range(CH):
                dve.wait_ge(S["pw"], j + 1)
                dve.tensor_copy(power[:, j, :], bank[7][:, 64 * j:64 * j + 64]).then_inc(S["pw_sb"], 1)
            dve.drain()
            dve.tensor_copy(step8[:, 0:64], power[:, CH - 1, :])
            dve.tensor_copy(step8[:, 64:128], power[:, CH - 2, :])
            dve.wait_ge(S["ln_act"], 1)
            dve.reciprocal(st[:, 3, :], st[:, 2, :])
            dve.drain()
            dve.tensor_tensor(u[:, :, :, :].rearrange("p t b c -> p (t b) c"), rsv(rows), bcast(st[:, 3, :], 2, C), ALU.mult).then_inc(S["ln"], 1)
            dve.drain()
            for k in range(0, B, 2):
                dve.wait_ge(S["dft"], k + 1)
                dve.tensor_copy(spec_in[:, :, k], bank[2 + k % 4][:, 0:NF]).then_inc(S["dft_dve"], 1)
            for t, (f0, nf) in enumerate(FQ):
                if t:
                    dve.wait_ge(S["freq"], 8)
                for o in range(0, 64, 2):
                    dve.wait_ge(S["hmat"], 64 * t + o + 1)
                    dve.tensor_copy(mix[:, 0:nf, :].rearrange("p f (r o) -> p r f o", r=2)[:, :, :, o],
                                    bank[o % 4][:, 0:2 * nf].rearrange("p (r f) -> p r f", r=2)).then_inc(S["hmat_dve"], 1)
                for k in range((nf + 15) // 16):
                    dve.wait_ge(S["freq"], 8 * t + k + 1)
                    n = min(nf - 16 * k, 16)
                    dve.tensor_copy(spec_out[:, f0 + 16 * k:f0 + 16 * k + n, :], bank[4 + k % 4][:, 0:32 * n].rearrange("p (f b) -> p f b", b=B)).then_inc(S["freq_sb"], 1)
            dve.memset(loc[64:128, 0, :, :], 0.0)
            dve.memset(state[:, 0, :], 0.0)
            for k in range(B):
                dve.wait_ge(S["delta"], k + 1)
                dve.tensor_copy(loc[0:64, :, :, k].rearrange("p j c -> p c j"), bank[2 + k % 2][0:64, 0:T].rearrange("p (c j) -> p c j", j=CH)).then_inc(S["delta_sb"], 1)
            dve.drain()
            dve.memset(st[:, 0, 0:1], 0.0).then_inc(S["scan0"], 1)
            half = loc.rearrange("p j c b -> p j (c b)")
            NH = NCH * B // 2
            for j in range(1, CH):
                for a in range(2):
                    dve.wait_ge(S["locmm"], 2 * (j - 1) + a + 1)
                    s = half[0:64, j, NH * a:NH * a + NH]
                    dve.tensor_tensor(s, bank[4 + a][0:64, 0:NH], s, ALU.add).then_inc(S["loc_add"], 1)
            dve.memset(st[:, 0, 0:1], 0.0).then_inc(S["chain_sb"], 1)
            dve.wait_ge(S["loc_copy"], CH - 1)
            for c in range(NCH - 1):
                dve.wait_ge(S["chain"], c + 1)
                dve.tensor_tensor(state[:, c + 1, :], bank[c % 2][:, 0:B], loc[:, CH - 1, c, :], ALU.add).then_inc(S["chain_sb"], 1)
            for j in range(CH):
                for a in range(2):
                    g = 2 * j + a
                    dve.wait_ge(S["carry"], g + 1)
                    s = half[0:64, j, NH * a:NH * a + NH]
                    dve.tensor_tensor(s, bank[4 + g % 4][0:64, 0:NH], s, ALU.add).then_inc(S["carry_sb"], 1)
            dve.wait_ge(S["res_in"], 128)
            for k in range(8):
                t, b0 = k // 4, 8 * (k % 4)
                dve.wait_ge(S["fin"], k + 1)
                s = res[:, t, b0:b0 + 8, :]
                dve.tensor_tensor(s, bank[k % 4][0:H, :].rearrange("p (b c) -> p b c", b=8), s, ALU.add).then_inc(S["fin_sb"], 1)


NE, FF = 8, 128
CAPACITY = float(math.ceil(B * T * 1.25 / NE))


def routing(nc, d):
    with Phase(nc, "route") as m:
        rows = m.sb("rows", [H, 2, B, C])
        sq = m.sb("sq", [H, 2, B, C])
        u = m.sb("u", [H, 2, B, C])
        st = m.sb("st", [H, 4, 64])
        mean_w = m.sb("mean_w", [H, 1])
        means = m.sb("means", [C, B])
        w_r = m.sb("w_r", [C, NE])
        b_r = m.sb("b_r", [B, NE])
        ones = m.sb("ones", [B, B])
        iota8 = m.sb("iota8", [B, NE])
        lg = m.sb("lg", [B, NE])
        ex = m.sb("ex", [B, NE])
        col = m.sb("col", [B, 8])
        best = m.sb("best", [B, 8])
        best_i = m.sb("best_i", [B, 8], U32)
        best_f = m.sb("best_f", [B, 8])
        hot = m.sb("hot", [B, 2, NE])
        wd = m.sb("wd", [B, NE])
        p_mean = m.ps("p_mean", [128, 512])
        p_log = m.ps("p_log", [128, 512])
        p_load = m.ps("p_load", [128, 512])
        S = {n: m.sem(n) for n in "rows_in consts ln ln_act u_done mean mean_sb log low ex1 rw load s2 ex2 tops ex3 wd out".split()}
        rsv = lambda a: a[:, :, :, :].rearrange("p t b c -> p (t b) c")
        blk = m.block()

        @blk.sync
        def _(sp):
            for t in range(2):
                sp.dma_start(rows[:, t, :, :], d["h1"][:, H * t:H * t + H, :].rearrange("b p c -> p b c")).then_inc(S["rows_in"], 16)
            sp.dma_start(w_r[:, :], d["L0_ffn_Wr"]).then_inc(S["consts"], 16)
            sp.dma_start(b_r[:, :], on_partitions(d["L0_ffn_br"], B)).then_inc(S["consts"], 16)
            sp.dma_start(iota8[:, :], on_partitions(d["c_iota"][0:NE], B)).then_inc(S["consts"], 16)
            sp.wait_ge(S["u_done"], 1)
            for t in range(2):
                sp.dma_start(d["u"][:, H * t:H * t + H, :].rearrange("b p c -> p b c"), u[:, t, :, :]).then_inc(S["out"], 16)
            sp.wait_ge(S["wd"], 1)
            sp.dma_start(d["w_route"], wd[:, :]).then_inc(S["out"], 16)
            sp.wait_ge(S["out"], 48)

        @blk.scalar
        def _(act):
            act.wait_ge(S["ln"], 1)
            act.activation(st[:, 2, :], st[:, 1, :], ACT.Sqrt).then_inc(S["ln_act"], 1)
            act.wait_ge(S["low"], 1)
            act.activation(ex[:, :], lg[:, :], ACT.Exp).then_inc(S["ex1"], 1)
            act.wait_ge(S["s2"], 1)
            act.activation(ex[:, :], lg[:, :], ACT.Exp).then_inc(S["ex2"], 1)
            act.wait_ge(S["tops"], 1)
            act.activation(col[:, 4:5], col[:, 3:4], ACT.Exp).then_inc(S["ex3"], 1)

        @blk.tensor
        def _(pe):
            pe.wait_ge(S["u_done"], 1)
            for b in range(B):
                for t in range(2):
                    ins = pe.matmul(p_mean[0:C, b:b + 1], u[:, t, b, :], mean_w[:, :], start=(t == 0), stop=(t == 1))
            ins.then_inc(S["mean"], 1)
            pe.wait_ge(S["consts"], 48)
            pe.wait_ge(S["mean_sb"], 1)
            pe.matmul(p_log[0:B, 0:NE], means[:, :], w_r[:, :], start=True, stop=True).then_inc(S["log"], 1)
            pe.wait_ge(S["rw"], 1)
            pe.matmul(p_load[0:B, 0:NE], ones[:, :], ex[:, :], start=True, stop=True).then_inc(S["load"], 1)

        @blk.vector
        def _(dve):
            dve.memset(mean_w[:, :], 1.0 / T)
            dve.memset(ones[:, :], 1.0)
            dve.wait_ge(S["rows_in"], 32)
            dve.tensor_reduce(st[:, 0, :], rsv(rows), AX.X, ALU.add)
            dve.drain()
            dve.tensor_scalar(st[:, 0, :], st[:, 0, :], 1.0 / C, None, ALU.mult)
            dve.drain()
            dve.tensor_tensor(rsv(rows), rsv(rows), bcast(st[:, 0, :], 2, C), ALU.subtract)
            dve.drain()
            dve.tensor_tensor(rsv(sq), rsv(rows), rsv(rows), ALU.mult)
            dve.drain()
            dve.tensor_reduce(st[:, 1, :], rsv(sq), AX.X, ALU.add)
            dve.drain()
            dve.tensor_scalar(st[:, 1, :], st[:, 1, :], 1.0 / C, 1e-5, ALU.mult, ALU.add).then_inc(S["ln"], 1)
            dve.wait_ge(S["ln_act"], 1)
            dve.reciprocal(st[:, 3, :], st[:, 2, :])
            dve.drain()
            dve.tensor_tensor(rsv(u), rsv(rows), bcast(st[:, 3, :], 2, C), ALU.mult).then_inc(S["u_done"], 1)
            dve.wait_ge(S["mean"], 1)
            dve.tensor_copy(means[:, :], p_mean[0:C, 0:B]).then_inc(S["mean_sb"], 1)
            dve.wait_ge(S["consts"], 48)

            def softmax_low(done):
                dve.drain()
                dve.tensor_reduce(col[:, 0:1], lg[:, :], AX.X, ALU.max)
                dve.drain()
                dve.tensor_scalar(lg[:, :], lg[:, :], col[:, 0:1], None, ALU.subtract).then_inc(done, 1)

            def softmax_norm():
                dve.tensor_reduce(col[:, 1:2], ex[:, :], AX.X, ALU.add)
                dve.drain()
                dve.reciprocal(col[:, 2:3], col[:, 1:2])
                dve.drain()

            dve.wait_ge(S["log"], 1)
            dve.tensor_tensor(lg[:, :], p_log[0:B, 0:NE], b_r[:, :], ALU.add)
            softmax_low(S["low"])
            dve.wait_ge(S["ex1"], 1)
            softmax_norm()
            dve.tensor_scalar(ex[:, :], ex[:, :], col[:, 2:3], None, ALU.mult).then_inc(S["rw"], 1)
            dve.drain()
            dve.wait_ge(S["load"], 1)
            dve.tensor_scalar(lg[:, :], p_load[0:B, 0:NE], float(T), None, ALU.mult)
            dve.drain()
            dve.reciprocal(lg[:, :], lg[:, :])
            dve.drain()
            dve.tensor_scalar(lg[:, :], lg[:, :], CAPACITY, 1.0, ALU.mult, ALU.min)
            dve.drain()
            dve.tensor_tensor(lg[:, :], lg[:, :], ex[:, :], ALU.mult)
            softmax_low(S["s2"])
            dve.wait_ge(S["ex2"], 1)
            softmax_norm()
            dve.tensor_scalar(ex[:, :], ex[:, :], col[:, 2:3], None, ALU.mult)
            dve.drain()
            dve.max(best[:, :], ex[:, :])
            dve.drain()
            dve.max_index(best_i[:, :], best[:, :], ex[:, :])
            dve.drain()
            dve.tensor_copy(best_f[:, :], best_i[:, :])
            dve.tensor_tensor(col[:, 3:4], best[:, 1:2], best[:, 0:1], ALU.subtract).then_inc(S["tops"], 1)
            dve.wait_ge(S["ex3"], 1)
            dve.tensor_scalar(col[:, 5:6], col[:, 4:5], 1.0, None, ALU.add)
            dve.drain()
            dve.reciprocal(col[:, 6:7], col[:, 5:6])
            dve.drain()
            dve.tensor_tensor(col[:, 7:8], col[:, 6:7], col[:, 4:5], ALU.mult)
            dve.drain()
            dve.tensor_scalar(hot[:, 0, :], iota8[:, :], best_f[:, 0:1], col[:, 6:7], ALU.is_equal, ALU.mult)
            dve.tensor_scalar(hot[:, 1, :], iota8[:, :], best_f[:, 1:2], col[:, 7:8], ALU.is_equal, ALU.mult)
            dve.drain()
            dve.tensor_tensor(wd[:, :], hot[:, 0, :], hot[:, 1, :], ALU.add).then_inc(S["wd"], 1)


def experts(nc, d):
    with Phase(nc, "moe") as m:
        ident = m.sb("ident", [128, 128])
        w1 = m.sb("w1", [128, NE, FF])
        b1 = m.sb("b1", [FF, NE])
        w2 = m.sb("w2", [FF, NE, C])
        b2 = m.sb("b2", [NE, C])
        gamma = m.sb("gamma", [H, C])
        beta = m.sb("beta", [H, C])
        ones = m.sb("ones", [NE, H])
        half_neg = m.sb("half_neg", [H, 4])
        u = [m.sb(f"u{p}", [H, 4, C]) for p in range(2)]
        h1 = [m.sb(f"h1{p}", [H, 4, C]) for p in range(2)]
        we = [m.sb(f"we{p}", [128, 2, NE]) for p in range(2)]
        we_t = [m.sb(f"we_t{p}", [NE, 2]) for p in range(2)]
        w_rep = [m.sb(f"w_rep{p}", [NE, 2, H]) for p in range(2)]
        u_t = [m.sb(f"u_t{p}", [128, T]) for p in range(2)]
        hid = [m.sb(f"hid{k}", [FF, 2, T]) for k in range(4)]
        y = m.sb("y", [H, 4, C])
        sq = m.sb("sq", [H, 4, C])
        st = m.sb("st", [H, 4, 4])
        h2 = [m.sb(f"h2{p}", [H, 4, C]) for p in range(2)]
        p_t = m.ps("p_t", [128, 512])
        p_h = [m.ps(f"p_h{k}", [128, 2, 512]) for k in range(2)]
        p_y = [m.ps(f"p_y{p}", [128, 512]) for p in range(2)]
        S = {n: m.sem(n) for n in "consts ones_set ut ut_sb hid_mm gelu hid_w y_mm rep var rstd fin_used h2_done".split()}
        loaded = [m.sem(f"loaded{p}") for p in range(2)]
        stored = [m.sem(f"stored{p}") for p in range(2)]
        N = B // 2
        blk = m.block()

        @blk.sync
        def _(sp):
            for a in range(2):
                sp.dma_start(w1[64 * a:64 * a + 64, :, :], d["L0_ffn_W1"].rearrange("e c f -> c e f")).then_inc(S["consts"], 16)
            sp.dma_start(b1[:, :], d["b1_cols"]).then_inc(S["consts"], 16)
            sp.dma_start(w2[:, :, :], d["L0_ffn_W2"].rearrange("e f c -> f e c")).then_inc(S["consts"], 16)
            sp.dma_start(b2[:, :], d["L0_ffn_b2"]).then_inc(S["consts"], 16)
            sp.dma_start(gamma[:, :], on_partitions(d["L0_ffn_gamma"], H)).then_inc(S["consts"], 16)
            sp.dma_start(beta[:, :], on_partitions(d["L0_ffn_beta"], H)).then_inc(S["consts"], 16)
            sp.dma_start(ident[:, :], d["c_ident"]).then_inc(S["consts"], 16)
            with sp.Fori(0, N // 2) as i:
                for p in range(2):
                    n = i * 2 + p
                    pair = bass.ds(n * 2, 2)
                    sp.wait_ge(S["h2_done"], n + 1)
                    for t in range(2):
                        rows = slice(H * t, H * t + H)
                        sp.dma_start(u[p][:, 2 * t:2 * t + 2, :], d["u"][pair, rows, :].rearrange("a p c -> p a c")).then_inc(loaded[p], 16)
                        sp.dma_start(h1[p][:, 2 * t:2 * t + 2, :], d["h1"][pair, rows, :].rearrange("a p c -> p a c")).then_inc(loaded[p], 16)
                    sp.dma_start(we[p][:, :, :], on_partitions(d["w_route"][pair, :], 128)).then_inc(loaded[p], 16)
                    sp.dma_start(we_t[p][:, :], d["w_route"][pair, :].rearrange("a e -> e a"), allow_slow_non_contiguous=True).then_inc(loaded[p], 16)
            for p in range(2):
                sp.wait_ge(stored[p], 32 * (N // 2))

        @blk.gpsimd
        def _(pool):
            pool.memset(half_neg[:, :], -0.5).then_inc(S["ones_set"], 1)
            pool.memset(ones[:, :], 1.0).then_inc(S["ones_set"], 1)
            pool.wait_ge(S["ones_set"], 2)
            with pool.Fori(0, N // 2) as i:
                for p in range(2):
                    n = i * 2 + p
                    pool.wait_ge(S["var"], n + 1)
                    pool.tensor_tensor(st[:, 3, :], st[:, 2, :], half_neg[:, :], ALU.pow).then_inc(S["rstd"], 1)
                    pool.wait_ge(S["h2_done"], n + 3)
                    for t in range(2):
                        pool.dma_start(d["h2"][bass.ds(n * 2, 2), H * t:H * t + H, :].rearrange("a p c -> p a c"),
                                       h2[p][:, 2 * t:2 * t + 2, :]).then_inc(stored[p], 16)
                    pool.wait_ge(stored[p], i * 32 + 32)

        @blk.scalar
        def _(act):
            act.wait_ge(S["consts"], 16 * 8)
            act.sem_inc(S["gelu"], 2)
            with act.Fori(0, N // 2) as i:
                for p in range(2):
                    n = i * 2 + p
                    act.wait_ge(S["ut"], n + 1)
                    act.activation(u_t[p][:, :], p_t[:, 0:T], ACT.Copy).then_inc(S["ut_sb"], 1)
                    for e in range(NE):
                        act.wait_ge(S["hid_mm"], n * NE + e + 1)
                        act.wait_ge(S["y_mm"], n * NE + e + 1)
                        act.activation(hid[e % 4][:, :, :], p_h[e % 2][:, :, 0:T], ACT.Gelu,
                                       bias=b1[:, e:e + 1]).then_inc(S["gelu"], 1)

        @blk.tensor
        def _(pe):
            pe.wait_ge(S["consts"], 16 * 8)
            pe.sem_inc(S["y_mm"], 4)
            with pe.Fori(0, N // 2) as i:
                for p in range(2):
                    n = i * 2 + p
                    pe.wait_ge(loaded[p], i * 96 + 96)
                    pe.wait_ge(S["ut_sb"], n + 1)
                    for t in range(2):
                        ins = pe.transpose(p_t[:, H * t:H * t + H], u[p][:, 2 * t:2 * t + 2, :].rearrange("p a c -> p (a c)"), ident[0:H, 0:H])
                    ins.then_inc(S["ut"], 1)
                    pe.wait_ge(S["ut_sb"], n + 2)

                    def up(e):
                        pe.wait_ge(S["gelu"], n * NE + e + 1)
                        for a in range(2):
                            q = slice(64 * a, 64 * a + 64)
                            ins = pe.matmul(p_h[e % 2][:, a, 0:T], w1[q, e, :], u_t[p][q, :], start=True, stop=True)
                        ins.then_inc(S["hid_mm"], 1)

                    def down(e):
                        pe.wait_ge(S["hid_w"], n * NE + e + 1)
                        for t in range(2):
                            for a in range(2):
                                g = 2 * t + a
                                ins = pe.matmul(p_y[p][0:H, C * g:C * g + C], hid[e % 4][:, a, H * t:H * t + H], w2[:, e, :],
                                                start=False, stop=False, skip_group_check=True)
                        ins.then_inc(S["y_mm"], 1)

                    up(0)
                    up(1)
                    pe.wait_ge(S["rep"], n + 1)
                    pe.wait_ge(S["fin_used"], n + 1)
                    for t in range(2):
                        for a in range(2):
                            g = 2 * t + a
                            pe.matmul(p_y[p][0:H, C * g:C * g + C], w_rep[p][:, a, :], b2[:, :], start=(g == 0), stop=False, skip_group_check=True)
                    for e in range(NE):
                        if e + 2 < NE:
                            up(e + 2)
                        down(e)

        @blk.vector
        def _(dve):
            dve.wait_ge(S["consts"], 16 * 8)
            dve.wait_ge(S["ones_set"], 2)
            dve.sem_inc(S["h2_done"], 2)
            dve.sem_inc(S["fin_used"], 2)
            dve.sem_inc(S["ut_sb"], 1)
            with dve.Fori(0, N // 2) as i:
                for p in range(2):
                    n = i * 2 + p
                    dve.wait_ge(loaded[p], i * 96 + 96)
                    for a in range(2):
                        ins = dve.tensor_scalar(w_rep[p][:, a, :], ones[:, :], we_t[p][:, a:a + 1], None, ALU.mult)
                    ins.then_inc(S["rep"], 1)
                    for e in range(NE):
                        dve.wait_ge(S["gelu"], n * NE + e + 3)
                        for a in range(2):
                            ins = dve.tensor_scalar(hid[e % 4][:, a, :], hid[e % 4][:, a, :], we[p][:, a, e:e + 1], None, ALU.mult)
                        ins.then_inc(S["hid_w"], 1)
                    dve.wait_ge(S["y_mm"], n * NE + 12)
                    dve.tensor_tensor(y[:, :, :], p_y[p][0:H, 0:4 * C].rearrange("p (g c) -> p g c", g=4), u[p][:, :, :], ALU.add).then_inc(S["fin_used"], 1)
                    dve.drain()
                    dve.tensor_reduce(st[:, 0, :], y[:, :, :], AX.X, ALU.add)
                    dve.drain()
                    dve.tensor_scalar(st[:, 0, :], st[:, 0, :], 1.0 / C, None, ALU.mult)
                    dve.drain()
                    dve.tensor_tensor(y[:, :, :], y[:, :, :], bcast(st[:, 0, :], 2, C), ALU.subtract)
                    dve.drain()
                    dve.tensor_tensor(sq[:, :, :], y[:, :, :], y[:, :, :], ALU.mult)
                    dve.drain()
                    dve.tensor_reduce(st[:, 1, :], sq[:, :, :], AX.X, ALU.add)
                    dve.drain()
                    dve.tensor_scalar(st[:, 2, :], st[:, 1, :], 1.0 / C, 1e-5, ALU.mult, ALU.add).then_inc(S["var"], 1)
                    dve.wait_ge(S["rstd"], n + 1)
                    dve.tensor_tensor(y[:, :, :], y[:, :, :], bcast(st[:, 3, :], 2, C), ALU.mult)
                    dve.drain()
                    dve.tensor_tensor(y[:, :, :], y[:, :, :], bcast(gamma[:, :], 1, 4), ALU.mult)
                    dve.drain()
                    dve.tensor_tensor(y[:, :, :], y[:, :, :], bcast(beta[:, :], 1, 4), ALU.add)
                    dve.drain()
                    dve.tensor_tensor(h2[p][:, :, :], y[:, :, :], h1[p][:, :, :], ALU.add).then_inc(S["h2_done"], 1)


NR, KM = 4, 15
ROWS = NR * T
TOK = ROWS * KM
QUAD = 32 * KM
Q_LOW = H // 8
Q_HIGH = ROWS // 32 - Q_LOW
T_LOW = 8 * Q_LOW
NONE = 300.0
FILL, GONE = -3.0e38, -3.3e38


def select_constants():
    inv = 1.0 / 10000.0 ** (np.arange(0, C, 2, dtype=np.float32) / C)
    f = np.outer(np.arange(T, dtype=np.float32), inv)
    two = lambda a: np.repeat(a, 2, 1).reshape(2, H, C).transpose(1, 0, 2)
    t = np.arange(T)
    keep = (np.arange(KM)[None, :] <= t[:, None]).astype(np.float32)
    keep = np.repeat(keep[:, None, :], NR, 1).reshape(2, H, NR * KM).transpose(1, 0, 2)
    ahead = np.triu(np.ones((H, H)), 1) * FILL
    return {"c_cos": two(np.cos(f)), "c_sin": two(np.sin(f)), "c_keep": keep, "c_none": (1 - keep) * NONE,
            "c_time": t.reshape(2, H).T, "c_ahead": ahead}


def pipelined(eng, n, front, back, back_first=False):
    order = lambda i, p, more: (
        (back(i, p), more and front(i + 1, 1 - p)) if back_first else (more and front(i + 1, 1 - p), back(i, p)))
    front(0, 0)
    with eng.Fori(0, n // 2 - 1) as k:
        for p in range(2):
            order(k * 2 + p, p, True)
    order(n - 2, 0, True)
    order(n - 1, 1, False)


def select_keys(nc, d):
    with Phase(nc, "sel") as m:
        ident = m.sb("ident", [128, 128])
        ident_b = m.sb("ident_b", [H, H], BF16)
        ahead_b = m.sb("ahead_b", [H, H], BF16)
        ahead = m.sb("ahead", [H, H])
        w = m.sb("w", [C, 6, C])
        w_rot = m.sb("w_rot", [C, 6, C])
        cos = m.sb("cos", [H, 2, C])
        sin = m.sb("sin", [H, 2, C])
        keep = m.sb("keep", [H, 2, NR * KM])
        none = m.sb("none", [H, 2, NR * KM])
        time = m.sb("time", [H, 2])
        rows = [m.sb(f"rows{p}", [H, 2, C]) for p in range(2)]
        sq = m.sb("sq", [H, 2, C])
        st = m.sb("st", [H, 4, 2])
        u = m.sb("u", [H, 2, 2, C])
        pad = m.sb("pad", [H, 1])
        u_t = m.sb("u_t", [C, T])
        by_cos = m.sb("by_cos", [H, 2, 6, C])
        by_sin = m.sb("by_sin", [H, 2, 6, C])
        rope = m.sb("rope", [H, 2, 6, C])
        sq2 = m.sb("sq2", [H, 2, 5, C])
        ss = m.sb("ss", [H, 3, 2, 5])
        nrm = m.sb("nrm", [H, 2, 5, C])
        rope_t = [m.sb(f"rope_t{p}", [128, 3, T]) for p in range(2)]
        q_n = m.sb("q_n", [C, T, NR])
        part = [m.sb(f"part{p}", [H, 2, 3, C], BF16) for p in range(2)]
        rest = m.sb("rest", [H, 2, 2, C])
        vals = m.sb("vals", [H, 2, NR, 16])
        nums = m.sb("nums", [H, 2, NR, 16], U32)
        left = m.sb("left", [H, 2, T])
        num_f = m.sb("num_f", [H, 2, NR, KM])
        num_k = m.sb("num_k", [H, 2, NR * KM])
        dist_f = m.sb("dist_f", [H, 2, NR * KM])
        num_o = [m.sb(f"num_o{p}", [H, 2, NR * KM], BF16) for p in range(2)]
        dist_o = [m.sb(f"dist_o{p}", [H, 2, NR * KM], BF16) for p in range(2)]
        p_t = m.ps("p_t", [128, 512])
        p_q = m.ps("p_q", [128, 512])
        p_a = m.ps("p_a", [128, 512])
        p_b = m.ps("p_b", [128, 512])
        p_low = [m.ps(f"p_low{k}", [128, 512]) for k in range(2)]
        p_high = [m.ps(f"p_high{k}", [128, 512]) for k in range(2)]
        S = {n: m.sem(n) for n in "consts w_set ready var std u_done ut ut_sb proj proj_used rope ss norm nrm rt rt_sb nt q_done q_stored part_done logit picked chosen".split()}
        rows_in = [m.sem(f"rows_in{p}") for p in range(2)]
        stored = [m.sem(f"stored{p}") for p in range(2)]
        blk = m.block()

        @blk.sync
        def _(sp):
            for dst, src in ((ident[:, :], "c_ident"), (ahead[:, :], "c_ahead"), (cos[:, :, :], "c_cos"), (sin[:, :, :], "c_sin"),
                             (keep[:, :, :], "c_keep"), (none[:, :, :], "c_none"), (time[:, :], "c_time")):
                sp.dma_start(dst, d[src]).then_inc(S["consts"], 16)
            sp.dma_start(w[:, 0:4, :], d["L1_attn_Wi"].rearrange("c (r o) -> c r o", r=NR)).then_inc(S["consts"], 16)
            for k in (4, 5):
                sp.dma_start(w[:, k, :], d["L1_attn_Wp"]).then_inc(S["consts"], 16)

            def front(n, p):
                sp.wait_ge(S["nrm"], n + 1)
                sp.dma_start(rows[p][:, :, :], d["h2"][bass.ds(n, 1), :, :].rearrange("a (t p) c -> p (a t) c", t=2)).then_inc(rows_in[p], 16)

            def back(n, p):
                one = bass.ds(n, 1)
                sp.wait_ge(S["part_done"], n + 3)
                sp.dma_start(d["key_parts"][one, :, :].rearrange("a (t p) c -> p (a t) c", t=2), part[p][:, :, :, :].rearrange("p t k c -> p t (k c)")).then_inc(stored[p], 16)
                sp.wait_ge(S["chosen"], n + 3)
                half = bass.ds((n - p) // 2, 1)
                for name, tile in (("num", num_o[p]), ("dist", dist_o[p])):
                    low, high = d[name + "_low"][p][half, :], d[name + "_high"][p][half, :]
                    row = NR * KM
                    sp.dma_start(low.rearrange("a (t k) -> (a t) k", k=row), tile[0:T_LOW, 0, :]).then_inc(stored[p], 16)
                    sp.dma_start(high[:, 0:(H - T_LOW) * row].rearrange("a (t k) -> (a t) k", k=row), tile[T_LOW:H, 0, :]).then_inc(stored[p], 16)
                    sp.dma_start(high[:, (H - T_LOW) * row:].rearrange("a (t k) -> (a t) k", k=row), tile[:, 1, :]).then_inc(stored[p], 16)

            pipelined(sp, B, front, back)
            for p in range(2):
                sp.wait_ge(stored[p], 112 * (B // 2) + 112)
            sp.wait_ge(S["q_stored"], 16 * B + 16)

        @blk.gpsimd
        def _(pool):
            def front(n, p):
                for t in range(2):
                    pool.wait_ge(S["proj_used"], n * 2 + t + 2)
                    if t == 0:
                        pool.wait_ge(S["rt"], n + 1)
                        pool.wait_ge(S["nrm"], n + 2)
                    pool.tensor_tensor(rope[:, t, :, :], by_cos[:, t, :, :], by_sin[:, t, :, :], ALU.add).then_inc(S["rope"], 1)

            pipelined(pool, B, front, lambda n, p: None)

        @blk.scalar
        def _(act):
            act.wait_ge(S["consts"], 160)
            act.activation(ident_b[:, :], ident[0:H, 0:H], ACT.Copy).then_inc(S["w_set"], 1)
            act.activation(ahead_b[:, :], ahead[:, :], ACT.Copy).then_inc(S["w_set"], 1)
            wp = lambda a, k: a[:, :, :].rearrange("c g (o k) -> c (g o) k", k=2)[:, :, k]
            act.activation(wp(w_rot, 0), wp(w, 1), ACT.Copy, scale=-1.0).then_inc(S["w_set"], 1)
            act.activation(wp(w_rot, 1), wp(w, 0), ACT.Copy).then_inc(S["w_set"], 1)
            act.sem_inc(S["q_stored"], 16)
            act.sem_inc(S["rt_sb"], 2)
            act.sem_inc(S["ut_sb"], 1)
            act.sem_inc(S["q_done"], 1)

            def front(n, p):
                act.wait_ge(S["var"], n + 1)
                act.activation(st[:, 2, :], st[:, 1, :], ACT.Sqrt).then_inc(S["std"], 1)
                act.wait_ge(S["ut"], n + 2)
                act.activation(u_t[:, :], p_t[0:C, 0:T], ACT.Copy).then_inc(S["ut_sb"], 1)
                act.wait_ge(S["ss"], n + 1)
                act.activation(ss[:, 1, :, :], ss[:, 0, :, :], ACT.Sqrt).then_inc(S["norm"], 1)
                act.wait_ge(S["rt"], n + 2)
                act.wait_ge(S["logit"], n + 1)
                act.activation(rope_t[p][:, 0:2, :], p_q[:, 0:2 * T].rearrange("p (g t) -> p g t", g=2), ACT.Copy)
                act.activation(rope_t[p][:, 2, :], p_t[:, 0:T], ACT.Copy).then_inc(S["rt_sb"], 1)
                act.wait_ge(S["nt"], n + 2)
                act.wait_ge(S["q_stored"], n * 16 + 16)
                for r in range(NR):
                    half, col = 64 * (r % 2), T * (r // 2)
                    ins = act.activation(q_n[:, :, r], p_a[half:half + 64, col:col + T], ACT.Copy)
                ins.then_inc(S["q_done"], 1)
                act.wait_ge(S["q_done"], n + 2)
                act.dma_start(d["q_n"][bass.ds(n, 1), :, :].rearrange("a c q -> (a c) q"), q_n[:, :, :].rearrange("c t r -> c (t r)")).then_inc(S["q_stored"], 16)

            pipelined(act, B, front, lambda n, p: None)

        @blk.tensor
        def _(pe):
            pe.wait_ge(S["w_set"], 4)
            pe.wait_ge(S["ready"], 1)
            pe.sem_inc(S["rt"], 1)
            pe.sem_inc(S["nt"], 1)
            pe.sem_inc(S["ut"], 1)
            pe.sem_inc(S["logit"], 2)

            def front(n, p):
                pe.wait_ge(S["u_done"], n + 1)
                pe.wait_ge(S["rt_sb"], n + 2)
                for t in range(2):
                    ins = pe.transpose(p_t[:, H * t:H * t + H], u[:, t, :, :].rearrange("p g c -> p (g c)"), ident[0:H, 0:H])
                ins.then_inc(S["ut"], 1)
                pe.wait_ge(S["ut_sb"], n + 2)
                for t in range(2):
                    if t == 0:
                        pe.wait_ge(S["q_done"], n + 1)
                    pe.wait_ge(S["proj_used"], n * 2 + t + 1)
                    lhs = u_t[:, H * t:H * t + H]
                    pe.matmul(p_a[0:H, 0:6 * C], lhs, w[:, :, :], start=True, stop=True)
                    pe.matmul(p_b[0:H, 0:6 * C], lhs, w_rot[:, :, :], start=True, stop=True).then_inc(S["proj"], 1)
                pe.wait_ge(S["rope"], n * 2 + 2)
                pe.wait_ge(S["rt_sb"], n + 2)
                for g in range(3):
                    for t in range(2):
                        dst = p_t[:, H * t:H * t + H] if g == 2 else p_q[:, T * g + H * t:T * g + H * t + H]
                        ins = pe.transpose(dst, rope[:, t, 2 * g:2 * g + 2, :].rearrange("p g c -> p (g c)"), ident[0:H, 0:H])
                ins.then_inc(S["rt"], 1)
                pe.wait_ge(S["nrm"], n + 3)
                pe.wait_ge(S["proj_used"], n * 2 + 3)
                for g in range(2):
                    for t in range(2):
                        ins = pe.transpose(p_a[:, T * g + H * t:T * g + H * t + H], nrm[:, t, 2 * g:2 * g + 2, :].rearrange("p g c -> p (g c)"), ident[0:H, 0:H])
                ins.then_inc(S["nt"], 1)

            def back(n, p):
                pe.wait_ge(S["rt_sb"], n + 3)
                pe.wait_ge(S["picked"], n + 1)
                for k in range(2):
                    pe.matmul(p_low[k][0:H, 0:2 * H], ident_b[:, :], bcast(ahead_b[:, :], 1, 2), start=True, stop=False, skip_group_check=True)
                    pe.matmul(p_high[k][0:H, 0:2 * T].rearrange("p (g s) -> p g s", g=2)[:, :, H:T], ident_b[:, :], bcast(ahead_b[:, :], 1, 2), start=True, stop=False, skip_group_check=True)
                for g in range(2):
                    for k in range(2):
                        q = slice(64 * k, 64 * k + 64)
                        pe.matmul(p_low[k][0:H, H * g:H * g + H], rope_t[p][q, g, 0:H], rope_t[p][q, 2, 0:H], start=False, stop=False, skip_group_check=True)
                for g in range(2):
                    for k in range(2):
                        q = slice(64 * k, 64 * k + 64)
                        ins = pe.matmul(p_high[k][0:H, T * g:T * g + T], rope_t[p][q, g, H:T], rope_t[p][q, 2, :], start=False, stop=False, skip_group_check=True)
                ins.then_inc(S["logit"], 1)

            pipelined(pe, B, front, back, back_first=True)

        @blk.vector
        def _(dve):
            dve.wait_ge(S["consts"], 160)
            dve.sem_inc(S["ready"], 1)
            dve.sem_inc(S["nrm"], 2)
            dve.sem_inc(S["proj_used"], 1)
            dve.sem_inc(S["picked"], 1)
            dve.sem_inc(S["chosen"], 2)
            dve.sem_inc(S["part_done"], 2)
            for p in range(2):
                dve.sem_inc(stored[p], 112)

            def front(n, p):
                x = rows[p]
                dve.wait_ge(rows_in[p], (n // 2) * 16 + 16 if isinstance(n, int) else (n - p) * 8 + 16)
                dve.tensor_reduce(st[:, 0, :], x[:, :, :], AX.X, ALU.add)
                dve.drain()
                dve.tensor_scalar(st[:, 0, :], st[:, 0, :], 1.0 / C, None, ALU.mult)
                dve.drain()
                dve.tensor_tensor(x[:, :, :], x[:, :, :], bcast(st[:, 0, :], 2, C), ALU.subtract)
                dve.drain()
                dve.tensor_tensor(sq[:, :, :], x[:, :, :], x[:, :, :], ALU.mult)
                dve.drain()
                dve.tensor_reduce(st[:, 3, :], sq[:, :, :], AX.X, ALU.add)
                dve.drain()
                dve.tensor_scalar(st[:, 1, :], st[:, 3, :], 1.0 / C, 1e-5, ALU.mult, ALU.add).then_inc(S["var"], 1)
                dve.wait_ge(S["std"], n + 1)
                dve.reciprocal(st[:, 2, :], st[:, 2, :])
                dve.drain()
                dve.wait_ge(S["ut"], n + 1)
                for k in range(2):
                    ins = dve.tensor_tensor(u[:, :, k, :], x[:, :, :], bcast(st[:, 2, :], 2, C), ALU.mult)
                ins.then_inc(S["u_done"], 1)
                for t in range(2):
                    dve.wait_ge(S["proj"], n * 2 + t + 1)
                    if t == 0 and not (isinstance(n, int) and n == 0):
                        dve.wait_ge(S["rope"], n * 2)
                    view = lambda a: a[0:H, 0:6 * C].rearrange("p (g c) -> p g c", c=C)
                    dve.tensor_tensor(by_cos[:, t, :, :], view(p_a), bcast(cos[:, t, :], 1, 6), ALU.mult)
                    dve.tensor_tensor(by_sin[:, t, :, :], view(p_b), bcast(sin[:, t, :], 1, 6), ALU.mult).then_inc(S["proj_used"], 1)
                dve.wait_ge(S["rope"], n * 2 + 2)
                five = rope[:, :, 0:5, :]
                for t in range(2):
                    dve.tensor_tensor(sq2[:, t, :, :], rope[:, t, 0:5, :], rope[:, t, 0:5, :], ALU.mult)
                dve.drain()
                dve.tensor_reduce(ss[:, 0, :, :], sq2[:, :, :, :], AX.X, ALU.add).then_inc(S["ss"], 1)
                dve.wait_ge(S["norm"], n + 1)
                dve.tensor_scalar(ss[:, 2, :, :], ss[:, 1, :, :], 1e-12, None, ALU.max)
                dve.drain()
                dve.reciprocal(ss[:, 2, :, :], ss[:, 2, :, :])
                dve.drain()
                dve.wait_ge(S["nt"], n + 1)
                for t in range(2):
                    ins = dve.tensor_tensor(nrm[:, t, :, :], rope[:, t, 0:5, :], bcast(ss[:, 2, t, :], 2, C), ALU.mult)
                ins.then_inc(S["nrm"], 1)
                dve.drain()
                dve.wait_ge(stored[p], (n // 2) * 112 + 112 if isinstance(n, int) else (n - p) * 56 + 112)
                key = nrm[:, :, 4, :]
                hi, mid, lo = (part[p][:, :, k, :] for k in range(3))
                dve.tensor_copy(hi, key)
                dve.drain()
                dve.tensor_tensor(rest[:, 0, :, :], key, hi, ALU.subtract)
                dve.drain()
                dve.tensor_copy(mid, rest[:, 0, :, :])
                dve.drain()
                dve.tensor_tensor(rest[:, 1, :, :], rest[:, 0, :, :], mid, ALU.subtract)
                dve.drain()
                dve.tensor_copy(lo, rest[:, 1, :, :]).then_inc(S["part_done"], 1)

            def back(n, p):
                dve.wait_ge(S["logit"], n + 3)
                dve.memset(pad[:, :], 0.0)
                for t in range(2):
                    for r in range(NR):
                        k, g, width = r % 2, r // 2, (H, T)[t]
                        row = (p_low, p_high)[t][k][0:H, width * g:width * g + width]
                        rem = left[:, r % 2, 0:width]
                        dve.max(vals[:, t, r, 0:8], row)
                        dve.drain()
                        dve.max_index(nums[:, t, r, 0:8], vals[:, t, r, 0:8], row)
                        ins = dve.match_replace(rem, vals[:, t, r, 0:8], row, GONE)
                        if t == 1 and r == NR - 1:
                            ins.then_inc(S["picked"], 1)
                        dve.drain()
                        dve.max(vals[:, t, r, 8:16], rem)
                        dve.drain()
                        dve.max_index(nums[:, t, r, 8:16], vals[:, t, r, 8:16], rem)
                dve.drain()
                for t in range(2):
                    dve.tensor_copy(num_f[:, t, :, :], nums[:, t, :, 0:KM])
                dve.drain()
                f = num_f[:, :, :, :].rearrange("p t r k -> p t (r k)")
                dve.tensor_tensor(num_k[:, :, :], f, keep[:, :, :], ALU.mult)
                for t in range(2):
                    dve.tensor_scalar(dist_f[:, t, :], f[:, t, :], time[:, t:t + 1], 0.0, ALU.subtract, ALU.min)
                dve.drain()
                dve.tensor_tensor(num_o[p][:, :, :], num_k[:, :, :], none[:, :, :], ALU.add)
                dve.tensor_tensor(dist_o[p][:, :, :], dist_f[:, :, :], keep[:, :, :], ALU.mult).then_inc(S["chosen"], 1)

            pipelined(dve, B, front, back)


GRP = 8
TOKG = GRP * KM
SLOT = KM + 1
STEPS = {"low": (B // 2 * Q_LOW, Q_LOW, 1), "high": (B // 2 * Q_HIGH, Q_HIGH, 2)}
ACT_SCALE = float(np.pi / np.sqrt(3.0))


def relation_constants():
    r = np.arange(128)[:, None] // SLOT
    c = np.arange(TOKG)[None, :] // KM
    return {"c_own": (r == c).astype(np.float32), "c_keynum": np.stack([np.arange(H), np.arange(H) + H], 1)}


def skewed(eng, n, stages):
    deep = max(lag for lag, _ in stages)
    start = deep + deep % 2
    stop = start + (n - start) // 2 * 2

    def tick(i, p, whole):
        for lag, run in stages:
            if whole or 0 <= i - lag < n:
                run(i - lag, (p - lag) % 2)

    for i in range(start):
        tick(i, i % 2, False)
    with eng.Fori(0, (stop - start) // 2) as k:
        for p in range(2):
            tick(k * 2 + (start + p), p, True)
    for i in range(stop, n + deep):
        tick(i, i % 2, False)


def relations(nc, d, tag):
    n_steps, per_pair, tiles = STEPS[tag]
    with Phase(nc, "rel_" + tag) as m:
        ident = m.sb("ident", [128, 128])
        own = m.sb("own", [128, TOKG])
        keynum = m.sb("keynum", [H, 2])
        w1 = m.sb("w1", [128, C])
        w1_d = m.sb("w1_d", [1, C])
        w1_x = m.sb("w1_x", [1, C])
        w1_dp = m.sb("w1_dp", [1, 3, C], BF16)
        w1_d3 = m.sb("w1_d3", [3, C], BF16)
        b1 = m.sb("b1", [128, 1])
        b1_s = m.sb("b1_s", [128, 1])
        w2 = m.sb("w2", [C, C])
        w2_t = m.sb("w2_t", [C, C])
        w_cm = m.sb("w_cm", [C, 3])
        w_out = m.sb("w_out", [128, 6])
        pad = m.sb("pad", [128, 32])
        parts = [m.sb(f"parts{p}", [H, 2, tiles, 3, C], BF16) for p in range(2)]
        num = [m.sb(f"num{p}", [H, 2, QUAD], BF16) for p in range(2)]
        dist = [m.sb(f"dist{p}", [3, 2, QUAD], BF16) for p in range(2)]
        q_n = [m.sb(f"q_n{p}", [128, 32]) for p in range(2)]
        hot = [m.sb(f"hot{p}", [H, tiles, 2, QUAD], BF16) for p in range(2)]
        sel = [m.sb(f"sel{p}", [128, 32, SLOT]) for p in range(2)]
        gram = [m.sb(f"gram{p}", [128, 2, QUAD]) for p in range(2)]
        hid = [m.sb(f"hid{p}", [128, QUAD]) for p in range(2)]
        out = [m.sb(f"out{p}", [TOKG, 24]) for p in range(2)]
        p_sel = [m.ps(f"p_sel{p}", [128, 512]) for p in range(2)]
        p_gram = [m.ps(f"p_gram{a}", [128, 512]) for a in range(2)]
        p_hid = [m.ps(f"p_hid{p}", [128, 512]) for p in range(2)]
        p_out = m.ps("p_out", [128, 512])
        p_w = m.ps("p_w", [128, 512])
        S = {n: m.sem(n) for n in "consts zero padded wd wd_in w2t w2t_sb wout wout_sb hot gath sel_sb query gr mask clip hid_mm silu out_mm out_sb".split()}
        loaded = [m.sem(f"loaded{p}") for p in range(2)]
        dist_in = [m.sem(f"dist_in{p}") for p in range(2)]
        stored = [m.sem(f"stored{p}") for p in range(2)]
        per_load = 16 * (2 * tiles + 2 + 2)
        blk = m.block()

        @blk.sync
        def _(sp):
            sp.dma_start(ident[:, :], d["c_ident"]).then_inc(S["consts"], 16)
            sp.dma_start(own[:, :], d["c_own"]).then_inc(S["consts"], 16)
            sp.dma_start(keynum[:, :], d["c_keynum"]).then_inc(S["consts"], 16)
            for g in range(GRP):
                sp.dma_start(w1[SLOT * g:SLOT * g + SLOT, :], d["L1_attn_W1"][0:SLOT, :]).then_inc(S["consts"], 16)
            sp.dma_start(w1_x[:, :], d["L1_attn_W1"][SLOT:SLOT + 1, :]).then_inc(S["consts"], 16)
            for a in range(2):
                sp.dma_start(b1[64 * a:64 * a + 64, :], d["L1_attn_b1"].rearrange("(p a) -> p a", a=1)).then_inc(S["consts"], 16)
            sp.dma_start(w2[:, :], d["L1_attn_W2"]).then_inc(S["consts"], 16)
            sp.dma_start(w_cm[:, 0:2], d["L1_attn_Wc"]).then_inc(S["consts"], 16)
            sp.dma_start(w_cm[:, 2:3], d["L1_attn_Wm"], allow_slow_non_contiguous=True).then_inc(S["consts"], 16)
            sp.wait_ge(S["wd"], 1)
            for k in range(3):
                sp.dma_start(w1_d3[k:k + 1, :], w1_dp[:, k, :]).then_inc(S["wd_in"], 16)

            def load(s, p):
                pair, quad = s // per_pair, s % per_pair
                sp.wait_ge(S["hot"], s + 1)
                sp.wait_ge(S["gath"], s + 1)
                sp.wait_ge(S["query"], s + 1)
                for a in range(2):
                    batch = bass.ds(pair * 2 + a, 1)
                    for t in range(tiles):
                        sp.dma_start(parts[p][:, a, t, :, :].rearrange("p k c -> p (k c)"),
                                     d["key_parts"][batch, H * t:H * t + H, :].rearrange("a p c -> (a p) c")).then_inc(loaded[p], 16)
                    numbers = d["num_" + tag][a].rearrange("b (q c) -> (b q) c", c=QUAD)[bass.ds(s, 1), :]
                    sp.dma_start(num[p][:, a, :], on_partitions(numbers.rearrange("a c -> (a c)"), H)).then_inc(loaded[p], 16)
                    first = quad * 32 + (0 if tag == "low" else 32 * Q_LOW)
                    sp.dma_start(q_n[p][64 * a:64 * a + 64, :], d["q_n"][batch, :, bass.ds(first, 32)].rearrange("a c q -> (a c) q")).then_inc(loaded[p], 16)

            def load_dist(s, p):
                sp.wait_ge(S["hid_mm"], s + 1)
                for a in range(2):
                    distances = d["dist_" + tag][a].rearrange("b (q c) -> (b q) c", c=QUAD)[bass.ds(s, 1), :]
                    sp.dma_start(dist[p][:, a, :], on_partitions(distances.rearrange("a c -> (a c)"), 3)).then_inc(dist_in[p], 16)

            skewed(sp, n_steps, [(0, load), (2, load_dist)])
            for p in range(2):
                sp.wait_ge(stored[p], 16 * ((n_steps - p + 1) // 2) + 16)

        @blk.gpsimd
        def _(pool):
            pool.memset(w_out[:, :], 0.0).then_inc(S["zero"], 1)
            pool.memset(pad[:, :], 0.0).then_inc(S["padded"], 1)
            pool.wait_ge(S["padded"], 1)
            pool.sem_inc(S["query"], 2)
            pool.sem_inc(S["clip"], 2)

            def masked(s, p):
                pool.wait_ge(S["mask"], s + 2)

            def query(s, p):
                pool.wait_ge(loaded[p], (s - p) // 2 * per_load + per_load)
                pool.wait_ge(S["gr"], s + 1)
                pool.tensor_tensor(sel[p][:, :, KM], q_n[p][:, :], pad[:, :], ALU.add).then_inc(S["query"], 1)

            def clip(s, p):
                pool.tensor_scalar(gram[p][:, :, :], gram[p][:, :, :], -1.0, None, ALU.max).then_inc(S["clip"], 1)

            skewed(pool, n_steps, [(1, masked), (0, query), (1, clip)])

        @blk.scalar
        def _(act):
            act.wait_ge(S["consts"], 16 * 17)
            act.activation(b1_s[:, :], b1[:, :], ACT.Copy, scale=ACT_SCALE)
            act.wait_ge(S["w2t"], 1)
            act.activation(w2_t[:, :], p_w[0:C, 0:C], ACT.Copy).then_inc(S["w2t_sb"], 1)
            act.wait_ge(S["zero"], 1)
            act.wait_ge(S["wout"], 1)
            for a in range(2):
                q = slice(64 * a, 64 * a + 64)
                act.activation(w_out[q, 3 * a:3 * a + 3], p_w[q, 64:67], ACT.Copy, scale=1.0 / ACT_SCALE).then_inc(S["wout_sb"], 1)
            act.drain()
            act.sem_inc(S["sel_sb"], 2)
            act.sem_inc(S["silu"], 2)

            def copy_sel(s, p):
                act.wait_ge(S["gath"], s + 3)
                act.wait_ge(S["gr"], s + 1)
                act.activation(sel[p][:, :, 0:KM], p_sel[p][:, 0:QUAD].rearrange("p (q k) -> p q k", k=KM), ACT.Copy).then_inc(S["sel_sb"], 1)

            def silu(s, p):
                act.wait_ge(S["hid_mm"], s + 3)
                act.wait_ge(S["out_mm"], s + 1)
                act.activation(hid[p][:, :], p_hid[p][:, 0:QUAD], ACT.Silu, scale=ACT_SCALE, bias=b1_s[:, 0:1]).then_inc(S["silu"], 1)

            def store(s, p):
                act.wait_ge(S["out_sb"], s + 2)
                act.dma_start(d["heads_" + tag][bass.ds(s, 1), :, :].rearrange("a p c -> (a p) c"), out[p][:, :]).then_inc(stored[p], 16)

            skewed(act, n_steps, [(0, copy_sel), (2, silu), (4, store)])

        @blk.tensor
        def _(pe):
            pe.wait_ge(S["consts"], 16 * 17)
            pe.transpose(p_w[0:C, 0:C], w2[:, :], ident[0:C, 0:C]).then_inc(S["w2t"], 1)
            pe.wait_ge(S["w2t_sb"], 1)
            for a in range(2):
                ins = pe.matmul(p_w[64 * a:64 * a + 64, 64:67], w2_t[:, :], w_cm[:, :], start=True, stop=True)
            ins.then_inc(S["wout"], 1)
            pe.wait_ge(S["wout_sb"], 2)
            pe.wait_ge(S["wd_in"], 48)
            pe.sem_inc(S["gath"], 2)
            pe.sem_inc(S["gr"], 2)
            pe.sem_inc(S["hid_mm"], 2)
            pe.sem_inc(S["out_mm"], 2)

            def gather(s, p):
                pe.wait_ge(S["hot"], s + 3)
                pe.wait_ge(S["sel_sb"], s + 1)
                for a in range(2):
                    last = 3 * tiles - 1
                    for k in range(3):
                        for t in range(tiles):
                            ins = pe.matmul(p_sel[p][64 * a:64 * a + 64, 0:QUAD], parts[p][:, a, t, k, :], hot[p][:, t, a, :],
                                            start=(k == 0 and t == 0), stop=(k * tiles + t == last))
                ins.then_inc(S["gath"], 1)

            def grams(s, p):
                pe.wait_ge(S["sel_sb"], s + 3)
                pe.wait_ge(S["query"], s + 3)
                pe.wait_ge(S["mask"], s + 1)
                for g in range(4):
                    for a in range(2):
                        q = slice(64 * a, 64 * a + 64)
                        ins = pe.matmul(p_gram[a][:, TOKG * g:TOKG * g + TOKG].rearrange("p (q k) -> p q k", k=KM), sel[p][q, GRP * g:GRP * g + GRP, :].rearrange("p q k -> p (q k)"),
                                        sel[p][q, GRP * g:GRP * g + GRP, 0:KM], start=True, stop=True)
                ins.then_inc(S["gr"], 1)

            def first_layer(s, p):
                pe.wait_ge(S["clip"], s + 3)
                pe.wait_ge(dist_in[p], (s - p) // 2 * 32 + 32)
                pe.wait_ge(S["silu"], s + 1)
                for a in range(2):
                    dst = p_hid[p][64 * a:64 * a + 64, 0:QUAD]
                    pe.matmul(dst, w1_d3[:, :], dist[p][:, a, :], start=True, stop=False)
                    ins = pe.matmul(dst, w1[:, :], gram[p][:, a, :], start=False, stop=True)
                ins.then_inc(S["hid_mm"], 1)

            def heads(s, p):
                pe.wait_ge(S["silu"], s + 3)
                pe.wait_ge(S["out_sb"], s + 1)
                for g in range(4):
                    ins = pe.matmul(p_out[0:TOKG, 6 * g:6 * g + 6], hid[p][:, TOKG * g:TOKG * g + TOKG], w_out[:, :], start=True, stop=True)
                ins.then_inc(S["out_mm"], 1)

            skewed(pe, n_steps, [(0, gather), (1, grams), (2, first_layer), (3, heads)])

        @blk.vector
        def _(dve):
            dve.wait_ge(S["consts"], 16 * 17)
            dve.tensor_scalar(w1_d[:, :], w1_x[:, :], 1.0 / -T, None, ALU.mult)
            dve.drain()
            dve.tensor_copy(w1_dp[:, 0, :], w1_d[:, :])
            for k in (1, 2):
                dve.drain()
                dve.tensor_tensor(w1_d[:, :], w1_d[:, :], w1_dp[:, k - 1, :], ALU.subtract)
                dve.drain()
                ins = dve.tensor_copy(w1_dp[:, k, :], w1_d[:, :])
            ins.then_inc(S["wd"], 1)
            dve.sem_inc(S["hot"], 2)
            dve.sem_inc(S["out_sb"], 1)
            dve.sem_inc(S["mask"], 1)
            for p in range(2):
                dve.sem_inc(stored[p], 16)

            def one_hot(s, p):
                dve.wait_ge(loaded[p], (s - p) // 2 * per_load + per_load)
                dve.wait_ge(S["gath"], s + 1)
                for t in range(tiles):
                    ins = dve.tensor_scalar(hot[p][:, t, :, :], num[p][:, :, :], keynum[:, t:t + 1], None, ALU.is_equal)
                ins.then_inc(S["hot"], 1)

            def mask(s, p):
                dve.wait_ge(S["gr"], s + 3)
                dve.wait_ge(S["hid_mm"], s + 1)
                for a in range(2):
                    ins = dve.scalar_tensor_tensor(out=gram[p][:, a, :].rearrange("p (g c) -> p g c", c=TOKG), in0=p_gram[a][:, 0:QUAD].rearrange("p (g c) -> p g c", c=TOKG),
                                                   scalar=1.0, in1=bcast(own[:, :], 1, 4), op0=ALU.min, op1=ALU.mult)
                ins.then_inc(S["mask"], 1)

            def copy_out(s, p):
                dve.wait_ge(S["out_mm"], s + 3)
                dve.wait_ge(stored[p], (s - p) // 2 * 16 + 16)
                dve.tensor_copy(out[p][:, :], p_out[0:TOKG, 0:24]).then_inc(S["out_sb"], 1)

            skewed(dve, n_steps, [(0, one_hot), (1, mask), (3, copy_out)])


NG = T // 2
GRID = 16
CK = 31
NCK = NG // CK


def sample_constants():
    p = np.arange(TOKG)
    own = (p[:, None] // KM == np.arange(GRP)[None, :]).astype(np.float32)
    g = np.arange(NG)[:, None]
    r = np.arange(TOKG)[None, :]
    shut = np.where(r % KM <= 2 * g + r // KM // NR, 0.0, -1e30)
    return {"c_row": own, "c_shut": shut, "c_cells": np.repeat(-np.arange(GRID)[None, :], TOKG, 0)}


def sample(nc, d):
    with Phase(nc, "smp") as m:
        ident = m.sb("ident", [128, 128])
        row = m.sb("row", [TOKG, GRP])
        shut = m.sb("shut", [NG, TOKG])
        cells = m.sb("cells", [TOKG, GRID])
        ones = m.sb("ones", [C, TOKG])
        b2 = m.sb("b2", [C, 1])
        b2_rep = m.sb("b2_rep", [C, TOKG])
        w_cm = m.sb("w_cm", [C, 3])
        b_cm = m.sb("b_cm", [TOKG, 3])
        b_all = m.sb("b_all", [TOKG, 3])
        wo = m.sb("wo", [C, NR, C])
        pal = m.sb("pal", [C, NR, NR, GRID, GRID])
        pal_w = m.sb("pal_w", [128, GRID, 128])
        heads = [m.sb(f"heads{p}", [TOKG, NG, 2, 3]) for p in range(2)]
        h2 = [m.sb(f"h2{p}", [NG, 2, 128]) for p in range(2)]
        z = m.sb("z", [TOKG, 2, 2, NG])
        pos = m.sb("pos", [TOKG, 2, 2, NG])
        mix = m.sb("mix", [TOKG, 2, NG])
        low = m.sb("low", [NG, 2, GRP, KM])
        red = m.sb("red", [NG, 3, 2, GRP])
        exps = m.sb("exps", [NG, 2, GRP, KM])
        wn = m.sb("wn", [NG, 2, GRP, KM])
        w = m.sb("w", [TOKG, 2, NG])
        far = m.sb("far", [TOKG, 2, NG, GRID])
        hat_y = m.sb("hat_y", [TOKG, 2, NG, GRID])
        hat_x = [m.sb(f"hat_x{p}", [TOKG, 2, NG, GRID]) for p in range(2)]
        wy = [m.sb(f"wy{p}", [TOKG, 2, NG, GRID]) for p in range(2)]
        own = [m.sb(f"own{k}", [TOKG, CK, GRP, GRID]) for k in range(2)]
        cell = m.sb("cell", [128, GRID, 2, NG])
        y_t = m.sb("y_t", [128, 2 * NG])
        p_w = m.ps("p_w", [128, 512])
        p_mix = m.ps("p_mix", [128, 512])
        p_wt = m.ps("p_wt", [128, 512])
        p_cell = [m.ps(f"p_cell{k}", [128, 512]) for k in range(2)]
        p_y = m.ps("p_y", [128, 512])
        p_r = m.ps("p_r", [128, 512])
        S = {n: m.sem(n) for n in "consts zero ones_set rep bias palw palw_sb b_done tanh mix mix_t low exps wn w_t w_sb pos hats wy own cells_mm cell_sb y_mm y_sb y_r h3".split()}
        loaded = [m.sem(f"loaded{p}") for p in range(2)]
        stored = [m.sem(f"stored{p}") for p in range(2)]
        N = B // 2
        blk = m.block()

        @blk.sync
        def _(sp):
            sp.wait_ge(S["zero"], 2)
            for dst, src in ((ident[:, :], d["c_ident"]), (row[:, :], d["c_row"]), (shut[:, :], d["c_shut"]), (cells[:, :], d["c_cells"]),
                             (b2[:, :], d["L1_attn_b2"].rearrange("(p a) -> p a", a=1)), (w_cm[:, 0:2], d["L1_attn_Wc"]),
                             (b_cm[:, 0:2], on_partitions(d["L1_attn_bc"], TOKG)), (b_cm[:, 2:3], on_partitions(d["L1_attn_bm"], TOKG)),
                             (wo[:, :, :], d["L1_attn_Wo"].rearrange("r c o -> c r o"))):
                sp.dma_start(dst, src).then_inc(S["consts"], 16)
            sp.dma_start(w_cm[:, 2:3], d["L1_attn_Wm"], allow_slow_non_contiguous=True).then_inc(S["consts"], 16)
            for r in range(NR):
                sp.dma_start(pal[:, r, r, :, :], d["L1_attn_palette"]).then_inc(S["consts"], 16)

            def front(n, p):
                sp.wait_ge(S["mix"], n + 1)
                sp.wait_ge(S["h3"], n + 1)
                if not (isinstance(n, int) and n < 2):
                    sp.wait_ge(stored[p], (n - p) // 2 * 16)
                lo, hi = 4 * Q_LOW, 4 * Q_HIGH
                sp.dma_start(heads[p][:, 0:lo, :, :].rearrange("p (s g) a c -> p s (g a c)", g=4),
                             d["heads_low"][bass.ds(n * Q_LOW, Q_LOW), :, :].rearrange("s p c -> p s c")).then_inc(loaded[p], 16)
                sp.dma_start(heads[p][:, lo:lo + hi, :, :].rearrange("p (s g) a c -> p s (g a c)", g=4),
                             d["heads_high"][bass.ds(n * Q_HIGH, Q_HIGH), :, :].rearrange("s p c -> p s c")).then_inc(loaded[p], 16)
                sp.dma_start(h2[p][:, :, :], d["h2"][bass.ds(n * 2, 2), :, :].rearrange("a (g t) c -> g a (t c)", t=2)).then_inc(loaded[p], 16)

            def back(n, p):
                sp.wait_ge(S["h3"], n + 3)
                sp.dma_start(d["h3"][bass.ds(n * 2, 2), :, :].rearrange("a (g t) c -> g a (t c)", t=2), h2[p][:, :, :]).then_inc(stored[p], 16)

            pipelined(sp, N, front, back)
            for p in range(2):
                sp.wait_ge(stored[p], 16 * (N // 2))

        @blk.gpsimd
        def _(pool):
            pool.memset(pal[:, :, :, :, :], 0.0).then_inc(S["zero"], 1)
            pool.memset(pal_w[:, :, :], 0.0).then_inc(S["zero"], 1)
            pool.memset(ones[:, :], 1.0).then_inc(S["ones_set"], 1)

        @blk.scalar
        def _(act):
            act.wait_ge(S["palw"], 1)
            for a in range(2):
                for k in range(2):
                    q = slice(64 * a, 64 * a + 64)
                    act.activation(pal_w[q, 8 * k:8 * k + 8, 64 * a:64 * a + 64], p_cell[k][q, :].rearrange("p (x c) -> p x c", c=C),
                                   ACT.Copy, scale=1.0 / NR).then_inc(S["palw_sb"], 1)
            act.wait_ge(S["b_done"], 1)
            act.sem_inc(S["mix"], 2)
            act.sem_inc(S["hats"], 1)

            def front(n, p):
                act.wait_ge(loaded[p], (n - p) // 2 * 48 + 48)
                act.wait_ge(S["pos"], n + 1)
                act.wait_ge(S["mix_t"], n + 1)
                for c in range(2):
                    act.activation(z[:, c, :, :], heads[p][:, :, :, c].rearrange("p g a -> p a g"), ACT.Tanh, bias=b_all[:, c:c + 1]).then_inc(S["tanh"], 1)
                act.activation(mix[:, :, :], heads[p][:, :, :, 2].rearrange("p g a -> p a g"), ACT.Identity, bias=b_all[:, 2:3]).then_inc(S["mix"], 1)
                act.wait_ge(S["low"], n + 2)
                act.activation(exps[:, :, :, :], low[:, :, :, :], ACT.Exp).then_inc(S["exps"], 1)
                act.wait_ge(S["pos"], n + 2)
                for c in range(2):
                    if c:
                        act.drain()
                    for x in range(GRID):
                        act.activation(far[:, :, :, x], pos[:, c, :, :], ACT.Abs, bias=cells[:, x:x + 1])
                    act.drain()
                    if c == 0:
                        act.wait_ge(S["cells_mm"], 8 * n + 1)
                    else:
                        act.wait_ge(S["wy"], n + 1)
                    dst = (hat_x[p], hat_y)[c]
                    ins = act.activation(dst[:, :, :, :], far[:, :, :, :], ACT.Relu, scale=-1.0, bias=1.0)
                ins.then_inc(S["hats"], 1)

            def back(n, p):
                for k in range(2 * NCK):
                    a, c = k // NCK, k % NCK
                    act.wait_ge(S["cells_mm"], 2 * NCK * n + k + 17)
                    if k == 0:
                        act.wait_ge(S["y_mm"], n + 1)
                    act.activation(cell[:, :, a, CK * c:CK * c + CK], p_cell[k % 2][:, 0:CK * GRID].rearrange("p (g x) -> p x g", x=GRID), ACT.Copy).then_inc(S["cell_sb"], 1)

            pipelined(act, N, front, back)

        @blk.tensor
        def _(pe):
            pe.wait_ge(S["consts"], 16 * 14)
            for k in range(2):
                for a in range(2):
                    for x in range(8):
                        for r in range(NR):
                            ins = pe.matmul(p_cell[k][64 * a:64 * a + 64, C * x:C * x + C], pal[:, r, :, :, 8 * k + x].rearrange("p r y -> p (r y)"), wo[:, r, :],
                                            start=(r == 0), stop=(r == NR - 1))
            ins.then_inc(S["palw"], 1)
            pe.wait_ge(S["rep"], 1)
            pe.matmul(p_w[0:TOKG, 0:3], b2_rep[:, :], w_cm[:, :], start=True, stop=True).then_inc(S["bias"], 1)
            pe.wait_ge(S["palw_sb"], 4)
            pe.sem_inc(S["mix_t"], 1)
            pe.sem_inc(S["w_t"], 1)
            pe.sem_inc(S["cells_mm"], 16)
            pe.sem_inc(S["y_mm"], 1)

            def front(n, p):
                pe.wait_ge(S["mix"], n + 3)
                pe.wait_ge(S["low"], n + 1)
                for a in range(2):
                    ins = pe.transpose(p_mix[0:NG, TOKG * a:TOKG * a + TOKG], mix[:, a, :], ident[0:TOKG, 0:TOKG])
                ins.then_inc(S["mix_t"], 1)
                pe.wait_ge(S["wn"], n + 1)
                pe.wait_ge(S["w_sb"], n + 1)
                for a in range(2):
                    ins = pe.transpose(p_wt[0:TOKG, NG * a:NG * a + NG], wn[:, a, :, :].rearrange("p r k -> p (r k)"), ident[0:NG, 0:NG])
                ins.then_inc(S["w_t"], 1)

            def back(n, p):
                for k in range(2 * NCK):
                    a, c = k // NCK, k % NCK
                    pe.wait_ge(S["own"], 2 * NCK * n + k + 1)
                    pe.wait_ge(S["cell_sb"], 2 * NCK * n + k + 1)
                    for g in range(CK):
                        ins = pe.matmul(p_cell[k % 2][:, GRID * g:GRID * g + GRID], own[k % 2][:, g, :, :].rearrange("p r y -> p (r y)"), hat_x[p][:, a, CK * c + g, :], start=True, stop=True)
                    ins.then_inc(S["cells_mm"], 1)
                pe.wait_ge(S["cell_sb"], 2 * NCK * n + 2 * NCK + 2)
                pe.wait_ge(S["y_sb"], n + 1)
                for x in range(GRID):
                    ins = pe.matmul(p_y[:, 0:2 * NG], pal_w[:, x, :], cell[:, x, :, :].rearrange("p a g -> p (a g)"), start=(x == 0), stop=(x == GRID - 1))
                ins.then_inc(S["y_mm"], 1)
                pe.wait_ge(S["y_sb"], n + 2)
                pe.wait_ge(S["h3"], n + 2)
                for a in range(2):
                    ins = pe.transpose(p_r[0:NG, 128 * a:128 * a + 128], y_t[:, NG * a:NG * a + NG], ident[:, :])
                ins.then_inc(S["y_r"], 1)

            pipelined(pe, N, front, back)

        @blk.vector
        def _(dve):
            dve.wait_ge(S["consts"], 16 * 14)
            dve.wait_ge(S["ones_set"], 1)
            dve.tensor_scalar(b2_rep[:, :], ones[:, :], b2[:, 0:1], None, ALU.mult).then_inc(S["rep"], 1)
            dve.wait_ge(S["bias"], 1)
            dve.tensor_tensor(b_all[:, :], p_w[0:TOKG, 0:3], b_cm[:, :], ALU.add).then_inc(S["b_done"], 1)
            dve.sem_inc(S["pos"], 1)
            dve.sem_inc(S["w_sb"], 1)
            dve.sem_inc(S["low"], 1)
            dve.sem_inc(S["wy"], 1)
            dve.sem_inc(S["cell_sb"], 2)
            dve.sem_inc(S["y_sb"], 1)
            dve.sem_inc(S["h3"], 2)

            def front(n, p):
                dve.wait_ge(S["tanh"], n * 2 + 2)
                dve.tensor_scalar(pos[:, :, :, :], z[:, :, :, :], 1.0, 0.5 * (GRID - 1), ALU.add, ALU.mult)
                dve.drain()
                dve.tensor_scalar(pos[:, :, :, :], pos[:, :, :, :], 0.0, float(GRID - 1), ALU.max, ALU.min).then_inc(S["pos"], 1)
                dve.wait_ge(S["mix_t"], n + 2)
                pm = p_mix[0:NG, 0:2 * TOKG].rearrange("p (a r) -> p a r", a=2)
                flat = lambda t: t[:, :, :, :].rearrange("p a r k -> p (a r) k")
                dve.tensor_tensor(low[:, :, :, :].rearrange("p a r k -> p a (r k)"), pm, bcast(shut[:, :], 1, 2), ALU.add)
                dve.drain()
                dve.tensor_reduce(red[:, 0, :, :].rearrange("p a r -> p (a r)"), flat(low), AX.X, ALU.max)
                dve.drain()
                dve.tensor_tensor(flat(low), flat(low), bcast(red[:, 0, :, :].rearrange("p a r -> p (a r)"), 2, KM), ALU.subtract).then_inc(S["low"], 1)
                dve.wait_ge(S["exps"], n + 1)
                dve.tensor_reduce(red[:, 1, :, :].rearrange("p a r -> p (a r)"), flat(exps), AX.X, ALU.add)
                dve.drain()
                dve.reciprocal(red[:, 2, :, :], red[:, 1, :, :])
                dve.drain()
                dve.wait_ge(S["w_t"], n + 1)
                dve.tensor_tensor(flat(wn), flat(exps), bcast(red[:, 2, :, :].rearrange("p a r -> p (a r)"), 2, KM), ALU.mult).then_inc(S["wn"], 1)
                dve.wait_ge(S["w_t"], n + 2)
                dve.tensor_copy(w[:, :, :], p_wt[0:TOKG, 0:2 * NG].rearrange("p (a g) -> p a g", a=2)).then_inc(S["w_sb"], 1)
                dve.drain()
                dve.wait_ge(S["hats"], n + 2)
                g16 = lambda t: t[:, :, :, :].rearrange("p a g y -> p (a g) y")
                dve.tensor_tensor(g16(wy[p]), g16(hat_y), bcast(w[:, :, :].rearrange("p a g -> p (a g)"), 2, GRID), ALU.mult).then_inc(S["wy"], 1)
                dve.drain()

            def back(n, p):
                for k in range(2 * NCK):
                    a, c = k // NCK, k % NCK
                    dve.wait_ge(S["cells_mm"], 2 * NCK * n + k + 15)
                    for r in range(GRP):
                        ins = dve.tensor_scalar(own[k % 2][:, :, r, :], wy[p][:, a, CK * c:CK * c + CK, :], row[:, r:r + 1], None, ALU.mult)
                    ins.then_inc(S["own"], 1)
                dve.wait_ge(S["y_mm"], n + 2)
                dve.wait_ge(S["y_r"], n) if not (isinstance(n, int) and n == 0) else None
                dve.tensor_copy(y_t[:, :], p_y[:, 0:2 * NG]).then_inc(S["y_sb"], 1)
                dve.wait_ge(S["y_r"], n + 1)
                dve.tensor_tensor(h2[p][:, :, :], p_r[0:NG, 0:256].rearrange("p (a c) -> p a c", a=2), h2[p][:, :, :], ALU.add).then_inc(S["h3"], 1)

            pipelined(dve, N, front, back)


NH, NX, DH = 4, 4, 16
FAR = -1.0e30


def ffn_constants():
    minus = np.zeros((128, 1))
    minus[::32] = -1.0
    return {"c_ahead30": np.triu(np.ones((H, H)), 1) * FAR, "c_behind30": np.tril(np.ones((H, H)), -1) * FAR, "c_minus": minus}


def normed(dve, x, sq, mean, ssum, var, width, eps, then):
    g = x.shape[1]
    dve.tensor_reduce(mean, x, AX.X, ALU.add)
    dve.drain()
    dve.tensor_scalar(mean, mean, 1.0 / width, None, ALU.mult)
    dve.drain()
    dve.tensor_tensor(x, x, bcast(mean, 2, width), ALU.subtract)
    dve.drain()
    dve.tensor_tensor(sq, x, x, ALU.mult)
    dve.drain()
    dve.tensor_reduce(ssum, sq, AX.X, ALU.add)
    dve.drain()
    dve.tensor_scalar(var, ssum, 1.0 / width, eps, ALU.mult, ALU.add).then_inc(then, 1)


def head_residual(nc, d):
    with Phase(nc, "hres") as m:
        ident = m.sb("ident", [128, 128])
        b_h = m.sb("b_h", [H, C])
        rows = m.sb("rows", [H, 2, NH, C])
        sq = m.sb("sq", [H, 2, NH, C])
        st = m.sb("st", [H, 5, 2 * NH])
        u_t = m.sb("u_t", [128, 2, T])
        res = m.sb("res", [H, 2, C])
        p_t = m.ps("p_t", [128, 512])
        p_s = [m.ps(f"p_s{a}", [128, 512]) for a in range(2)]
        S = {n: m.sem(n) for n in "rows_in consts var std u_done ut ut_sb s_mm done out".split()}
        w2 = m.sb("w2", [128, C])
        blk = m.block()

        @blk.sync
        def _(sp):
            for b in range(NH):
                sp.dma_start(rows[:, :, b, :], d["h3"][b, :, :].rearrange("(t p) c -> p t c", t=2)).then_inc(S["rows_in"], 16)
            for a in range(2):
                sp.dma_start(w2[64 * a:64 * a + 64, :], d["hl_w_t"]).then_inc(S["consts"], 16)
            sp.dma_start(b_h[:, :], on_partitions(d["L1_ffn_hl_b"].rearrange("n d -> (n d)"), H)).then_inc(S["consts"], 16)
            sp.dma_start(ident[:, :], d["c_ident"]).then_inc(S["consts"], 16)
            sp.wait_ge(S["done"], 4)
            sp.dma_start(d["resid"].rearrange("(t p) c -> p t c", t=2), res[:, :, :]).then_inc(S["out"], 16)
            sp.wait_ge(S["out"], 16)

        @blk.scalar
        def _(act):
            act.wait_ge(S["var"], 1)
            act.activation(st[:, 3, :], st[:, 2, :], ACT.Sqrt).then_inc(S["std"], 1)
            for b in range(0, NH, 2):
                act.wait_ge(S["ut"], 2)
                act.activation(u_t[:, b // 2, :], p_t[:, 248 * (b // 2):248 * (b // 2) + T], ACT.Copy).then_inc(S["ut_sb"], 1)

        @blk.tensor
        def _(pe):
            pe.wait_ge(S["consts"], 64)
            pe.wait_ge(S["u_done"], 1)
            for k in range(2):
                for t in range(2):
                    ins = pe.transpose(p_t[:, T * k + H * t:T * k + H * t + H], rows[:, t, 2 * k:2 * k + 2, :].rearrange("p b c -> p (b c)"), ident[0:H, 0:H])
                ins.then_inc(S["ut"], 1)
            pe.wait_ge(S["ut_sb"], 2)
            for b in range(NH):
                q = slice(64 * (b % 2), 64 * (b % 2) + 64)
                for t in range(2):
                    ins = pe.matmul(p_s[b % 2][0:H, 128 * (b // 2) + 64 * t:128 * (b // 2) + 64 * t + 64], u_t[q, b // 2, H * t:H * t + H], w2[q, :], start=True, stop=True)
            ins.then_inc(S["s_mm"], 1)

        @blk.vector
        def _(dve):
            dve.wait_ge(S["rows_in"], 64)
            x = rows[:, :, :, :].rearrange("p t b c -> p (t b) c")
            normed(dve, x, sq[:, :, :, :].rearrange("p t b c -> p (t b) c"), st[:, 0, :], st[:, 1, :], st[:, 2, :], C, 1e-5, S["var"])
            dve.wait_ge(S["std"], 1)
            dve.reciprocal(st[:, 4, :], st[:, 3, :])
            dve.drain()
            dve.tensor_tensor(x, x, bcast(st[:, 4, :], 2, C), ALU.mult).then_inc(S["u_done"], 1)
            dve.wait_ge(S["s_mm"], 1)
            for b in range(NH):
                at = 128 * (b // 2)
                dve.tensor_tensor(res[:, :, DH * b:DH * b + DH], p_s[b % 2][0:H, at:at + 128].rearrange("p (t c) -> p t c", t=2)[:, :, DH * b:DH * b + DH],
                                  bcast(b_h[:, DH * b:DH * b + DH], 1, 2), ALU.add).then_inc(S["done"], 1)


def head_mixture(nc, d):
    with Phase(nc, "mix") as m:
        ident = m.sb("ident", [128, 128])
        ident_b = m.sb("ident_b", [H, H], BF16)
        tri = m.sb("tri", [H, 2, H])
        ahead_b = m.sb("ahead_b", [H, H], BF16)
        behind_b = m.sb("behind_b", [H, H], BF16)
        w_h = m.sb("w_h", [C, 128])
        b_h = m.sb("b_h", [H, C])
        b_hc = m.sb("b_hc", [C, 1])
        w_q = m.sb("w_q", [C, NX, 128])
        w_k = m.sb("w_k", [C, 128])
        w_v = m.sb("w_v", [C, C])
        minus = m.sb("minus", [128, 1])
        w_g = m.sb("w_g", [128, 2, 2, NX])
        b_g = m.sb("b_g", [H, NH * NX])
        w_1 = m.sb("w_1", [128, 128])
        w_2 = m.sb("w_2", [128, 128])
        b_1 = m.sb("b_1", [128, 1])
        b_2 = m.sb("b_2", [H, DH])
        ln_g, ln_b, fn_g, fn_b = (m.sb(n, [H, DH]) for n in ("ln_g", "ln_b", "fn_g", "fn_b"))
        w_f = m.sb("w_f", [128, 2, NH])
        resid = m.sb("resid", [H, 2, C])
        half_neg = m.sb("half_neg", [H, 8])
        rows = [m.sb(f"rows{p}", [H, 2, C]) for p in range(2)]
        kept = [m.sb(f"kept{p}", [H, 2, C]) for p in range(2)]
        sq = m.sb("sq", [H, 2, C])
        st = m.sb("st", [H, 4, 2])
        u = m.sb("u", [H, 2, 2, C])
        u_t = m.sb("u_t", [C, T])
        sx_t = m.sb("sx_t", [C, T])
        sx = m.sb("sx", [H, 2, C])
        full = [m.sb(f"full{p}", [H, 2, C]) for p in range(2)]
        q_t = m.sb("q_t", [128, NX, T])
        q_m = [m.sb(f"q_m{p}", [128, NX, T]) for p in range(2)]
        k_t = [m.sb(f"k_t{p}", [128, T]) for p in range(2)]
        v_1 = [m.sb(f"v_1{p}", [H, 2, NH, DH + 1]) for p in range(2)]
        tops = m.sb("tops", [H, 2, NX, 128])
        e_0 = [m.sb(f"e_0{k}", [H, NX, T]) for k in range(2)]
        e_1 = [m.sb(f"e_1{k}", [H, NX, H]) for k in range(2)]
        den = m.sb("den", [H, 2, 16])
        qkv = m.sb("qkv", [H, 2, 16, DH])
        qkv_p = m.sb("qkv_p", [H, 2, 16, DH])
        qkv_t = m.sb("qkv_t", [128, 4, H])
        gate = m.sb("gate", [H, 2 * NH, NX])
        gate_e = m.sb("gate_e", [H, 2 * NH, NX])
        red = m.sb("red", [H, 4, 2 * NH])
        prod = m.sb("prod", [H, 2, NH, NX, DH])
        fx = m.sb("fx", [H, 2 * NH, DH])
        sq16 = m.sb("sq16", [H, 2 * NH, DH])
        vs = m.sb("vs", [H, 6, 2 * NH])
        fx_t = m.sb("fx_t", [128, H])
        hx_t = m.sb("hx_t", [128, H])
        hm_t = m.sb("hm_t", [128, H])
        hx = m.sb("hx", [H, 2 * NH, DH])
        fo = m.sb("fo", [H, 2 * NH, DH])
        fo_t = m.sb("fo_t", [128, H])
        fg = m.sb("fg", [H, 2, NH])
        fg_e = m.sb("fg_e", [H, 2, NH])
        fr = m.sb("fr", [H, 3, 2])
        res = [m.sb(f"res{p}", [H, 2, C]) for p in range(2)]
        p_f = m.ps("p_f", [128, 512])
        p_b = m.ps("p_b", [128, 512])
        ring = [m.ps(f"ring{k}", [128, 512]) for k in range(4)]
        p_av = [m.ps(f"p_av{t}", [128, 512]) for t in range(2)]
        S = {n: m.sem(n) for n in ("zero consts cast ready var rstd u_done fmm fev sx_read max_mm q_used s_used key_mm st_used "
                                   "av av_used masked bmm bact bdve var1 rstd1 fo_done done").split()}
        loaded = [m.sem(f"loaded{p}") for p in range(2)]
        stored = [m.sem(f"stored{p}") for p in range(2)]
        NCONST = 32
        bank = lambda k, n: ring[k % 4][0:n, 0:496]
        e2 = lambda ap: ap.rearrange("p (e s) -> p e s", e=2)
        blk = m.block()

        @blk.sync
        def _(sp):
            sp.wait_ge(S["zero"], 9)
            col = lambda v: v.rearrange("(p a) -> p a", a=1)
            loads = [(ident[:, :], d["c_ident"]), (tri[:, 0, :], d["c_ahead30"]), (tri[:, 1, :], d["c_behind30"]), (minus[:, :], d["c_minus"]),
                     (w_h[:, 0:C], d["hl_w_t"]), (b_h[:, :], on_partitions(d["L1_ffn_hl_b"].rearrange("n d -> (n d)"), H)),
                     (b_hc[:, :], col(d["L1_ffn_hl_b"].rearrange("n d -> (n d)"))),
                     (b_g[:, :], on_partitions(d["L1_ffn_gate_b"].rearrange("n e -> (n e)"), H)), (b_2[:, :], on_partitions(d["L1_ffn_fc2_b"], H)),
                     (w_f[0:C, 0, :], d["fgate_t"]), (w_f[C:128, 1, :], d["fgate_t"]), (resid[:, :, :], d["resid"].rearrange("(t p) c -> p t c", t=2))]
            loads += [(t[:, :], on_partitions(d["L1_ffn_" + n], H)) for t, n in ((ln_g, "ln_g"), (ln_b, "ln_b"), (fn_g, "fnorm_g"), (fn_b, "fnorm_b"))]
            for n in range(NH):
                q = slice(DH * n, DH * n + DH)
                loads += [(w_q[q, :, 32 * n + 1:32 * n + 1 + DH], d["wq_t"][n]), (w_k[q, 32 * n + 1:32 * n + 1 + DH], d["wk_t"][n]),
                          (w_v[q, q], d["wv_t"][n]), (w_g[64 * (n % 2):64 * (n % 2) + 64, n // 2, n % 2, :], d["gate_t"][n])]
            assert len(loads) == NCONST
            for dst, src in loads:
                sp.dma_start(dst, src).then_inc(S["consts"], 16)
            for n in range(2 * NH):
                q = slice(DH * n, DH * n + DH)
                for dst, src in ((w_1[q, q], d["fc1_t"]), (w_2[q, q], d["fc2_t"]), (b_1[q, :], col(d["L1_ffn_fc1_b"]))):
                    sp.dma_start(dst, src).then_inc(S["consts"], 16)

            def front(n, p):
                sp.wait_ge(S["done"], n + 1)
                src = d["h3"][bass.ds(n, 1), :, :].rearrange("a (t p) c -> p (a t) c", t=2)
                sp.dma_start(rows[p][:, :, :], src).then_inc(loaded[p], 16)
                sp.dma_start(kept[p][:, :, :], src).then_inc(loaded[p], 16)

            def back(n, p):
                sp.wait_ge(S["done"], n + 3)
                sp.dma_start(d["out"][bass.ds(n, 1), :, :].rearrange("a (t p) c -> p (a t) c", t=2), res[p][:, :, :]).then_inc(stored[p], 16)

            pipelined(sp, B, front, back)
            for p in range(2):
                sp.wait_ge(stored[p], 16 * (B // 2) + 16)

        ALL = 16 * (NCONST + 3 * 2 * NH)

        @blk.gpsimd
        def _(pool):
            for t in (w_h[:, :], w_f[:, :, :], w_q[:, :, :], w_k[:, :], w_v[:, :], w_g[:, :, :, :], w_1[:, :], w_2[:, :], tops[:, :, :, :]):
                pool.memset(t, 0.0).then_inc(S["zero"], 1)
            pool.memset(half_neg[:, :], -0.5).then_inc(S["ready"], 1)
            for p in range(2):
                pool.memset(v_1[p][:, :, :, DH:DH + 1], 1.0).then_inc(S["ready"], 1)
            pool.wait_ge(S["ready"], 3)
            pool.sem_inc(S["masked"], 1)

            def front(n, p):
                pool.wait_ge(S["var"], n + 1)
                pool.tensor_tensor(st[:, 3, :], st[:, 2, :], half_neg[:, 0:2], ALU.pow).then_inc(S["rstd"], 1)

            def back(n, p):
                pool.wait_ge(S["av_used"], 2 * n + 4)
                pool.wait_ge(S["bmm"], 7 * n + 7)
                for t in range(2):
                    ins = pool.tensor_tensor(qkv_p[:, t, :, :].rearrange("p (n e) d -> p n e d", n=NH), qkv[:, t, :, :].rearrange("p (n e) d -> p n e d", n=NH),
                                             bcast(full[p][:, t, :].rearrange("p (n d) -> p n d", n=NH), 2, NX), ALU.mult)
                ins.then_inc(S["masked"], 1)
                for k in range(2):
                    pool.wait_ge(S["var1"], 2 * n + k + 1)
                    pool.tensor_tensor(vs[:, 3, :], vs[:, 2, :], half_neg[:, :], ALU.pow).then_inc(S["rstd1"], 1)

            pipelined(pool, B, front, back)

        @blk.scalar
        def _(act):
            act.wait_ge(S["consts"], ALL)
            act.activation(ident_b[:, :], ident[0:H, 0:H], ACT.Copy).then_inc(S["cast"], 1)
            act.activation(ahead_b[:, :], tri[:, 0, :], ACT.Copy).then_inc(S["cast"], 1)
            act.activation(behind_b[:, :], tri[:, 1, :], ACT.Copy).then_inc(S["cast"], 1)
            act.wait_ge(S["ready"], 3)
            act.sem_inc(S["st_used"], 24)
            act.sem_inc(S["fev"], 1)

            def front(n, p):
                def copy(k, dst, src, **kw):
                    act.wait_ge(S["fmm"], 4 * n + k + 1)
                    return act.activation(dst, src, ACT.Identity if "bias" in kw else ACT.Copy, **kw)
                copy(0, u_t[:, :], p_f[0:C, 0:T]).then_inc(S["fev"], 1)
                copy(1, sx_t[:, :], p_f[0:C, 256:256 + T], bias=b_hc[:, 0:1]).then_inc(S["fev"], 1)
                act.wait_ge(S["key_mm"], 12 * n + 12)
                act.wait_ge(S["av"], 4 * n + 4)
                copy(3, k_t[p][:, :], p_f[:, 0:T], bias=minus[:, 0:1])
                copy(3, v_1[p][:, :, :, 0:DH], p_f[0:H, 256:384].rearrange("p (t n o) -> p t n o", t=2, n=NH)).then_inc(S["fev"], 1)
                for k in range(2):
                    act.wait_ge(S["max_mm"], 16 * n + k + 1)
                    act.activation(q_t[:, 2 * k:2 * k + 2, :], e2(bank(k, 128)), ACT.Copy).then_inc(S["q_used"], 1)

            def back(n, p):
                for h in range(NH):
                    act.wait_ge(S["av"], 4 * n + h + 7)
                    for k in range(3):
                        v = 3 * h + k
                        act.wait_ge(S["key_mm"], 12 * n + v + 25)
                        if k < 2:
                            dst, src = e_0[h % 2][:, 2 * k:2 * k + 2, :], e2(bank(v, H))
                        else:
                            dst, src = e_1[h % 2][:, :, :], bank(v, H).rearrange("p (e s) -> p e s", e=4)
                        act.activation(dst, src, ACT.Exp, scale=float(DH) ** 0.5).then_inc(S["st_used"], 1)
                act.wait_ge(S["bmm"], 7 * n + 8)
                act.activation(qkv_t[:, :, :], p_b[:, 0:4 * H].rearrange("p (g s) -> p g s", g=4), ACT.Copy).then_inc(S["bact"], 1)
                act.wait_ge(S["bdve"], 4 * n + 1)
                act.activation(gate_e[:, :, :], gate[:, :, :], ACT.Exp).then_inc(S["bact"], 1)
                act.wait_ge(S["bmm"], 7 * n + 10)
                act.activation(fx_t[:, :], p_b[:, 0:H], ACT.Copy).then_inc(S["bact"], 1)
                act.wait_ge(S["bmm"], 7 * n + 13)
                act.activation(fo_t[:, :], p_b[:, 0:H], ACT.Copy).then_inc(S["bact"], 1)
                act.wait_ge(S["bdve"], 4 * n + 4)
                act.activation(fg_e[:, :, :], fg[:, :, :], ACT.Exp).then_inc(S["bact"], 1)

            pipelined(act, B, front, back)

        @blk.tensor
        def _(pe):
            pe.wait_ge(S["cast"], 3)
            pe.wait_ge(S["ready"], 3)
            pe.sem_inc(S["key_mm"], 24)
            pe.sem_inc(S["av"], 8)
            pe.sem_inc(S["bmm"], 7)

            def front(n, p):
                pe.wait_ge(S["u_done"], n + 1)
                pe.wait_ge(S["fev"], 3 * n + 1)
                pe.wait_ge(S["sx_read"], n + 1)
                for t in range(2):
                    ins = pe.transpose(p_f[:, H * t:H * t + H], u[:, t, :, :].rearrange("p g c -> p (g c)"), ident[0:H, 0:H])
                ins.then_inc(S["fmm"], 1)
                pe.wait_ge(S["fev"], 3 * n + 2)
                pe.matmul(p_f[:, 256:256 + T], w_h[:, :], u_t[:, :], start=True, stop=True).then_inc(S["fmm"], 1)
                pe.wait_ge(S["fev"], 3 * n + 3)
                pe.matmul(p_f[:, 0:T], w_k[:, :], sx_t[:, :], start=True, stop=True).then_inc(S["fmm"], 1)
                for t in range(2):
                    pe.matmul(p_f[0:H, 256 + 64 * t:320 + 64 * t], sx_t[:, H * t:H * t + H], w_v[:, :], start=True, stop=True)
                for t in range(2):
                    ins = pe.matmul(p_f[0:H, 384 + 64 * t:448 + 64 * t], u_t[:, H * t:H * t + H], w_h[:, 0:C], start=True, stop=True)
                ins.then_inc(S["fmm"], 1)

                def turn(v):
                    if v < 4:
                        pe.wait_ge(S["st_used"], 12 * n + 9 + v)
                        pe.wait_ge(S["s_used"], 14 * n + 14)
                    elif v < 6:
                        pe.wait_ge(S["q_used"], 2 * n + v - 3)
                    else:
                        pe.wait_ge(S["s_used"], 14 * n + 14 + v - 5)

                for k in range(2):
                    turn(k)
                    for e in range(2):
                        ins = pe.matmul(bank(k, 128)[:, T * e:T * e + T], w_q[:, 2 * k + e, :], sx_t[:, :], start=True, stop=True)
                    ins.then_inc(S["max_mm"], 1)
                pe.wait_ge(S["q_used"], 2 * n + 2)
                pe.wait_ge(S["fev"], 3 * n + 4)
                for h in range(NH):
                    q = slice(32 * h, 32 * h + 1 + DH)
                    for k in range(3):
                        v = 2 + 3 * h + k
                        turn(v)
                        dst = bank(v, H)
                        if k == 0:
                            dst = dst.rearrange("p (e s) -> p e s", e=4)
                            pe.matmul(dst, ident_b[:, :], bcast(ahead_b[:, :], 1, 4), start=True, stop=False, skip_group_check=True)
                            for e in range(4):
                                ins = pe.matmul(dst[:, e, :], q_t[q, e, 0:H], k_t[p][q, 0:H], start=False, stop=False, skip_group_check=True)
                        else:
                            dst = e2(dst)
                            pe.matmul(dst[:, :, H:T], ident_b[:, :], bcast(ahead_b[:, :], 1, 2), start=True, stop=False, skip_group_check=True)
                            for e in range(2):
                                ins = pe.matmul(dst[:, e, :], q_t[q, 2 * (k - 1) + e, H:T], k_t[p][q, :], start=False, stop=False, skip_group_check=True)
                        ins.then_inc(S["max_mm"], 1)
                for k in range(2):
                    turn(14 + k)
                    pe.wait_ge(S["s_used"], 14 * n + 26)
                    for e in range(2):
                        for t in range(2):
                            ins = pe.matmul(bank(14 + k, 128)[:, T * e + H * t:T * e + H * t + H], tops[:, t, 2 * k + e, :], ident[0:H, 0:H], start=True, stop=True)
                    ins.then_inc(S["max_mm"], 1)

            def back(n, p):
                last = isinstance(n, int) and n == B - 1

                def scores(h):
                    q = slice(32 * h, 32 * h + 1 + DH)
                    for k in range(3):
                        v = 3 * h + k
                        if v < 4:
                            pe.wait_ge(S["st_used"], 12 * n + 21 + v)
                            if not last:
                                pe.wait_ge(S["s_used"], 14 * n + 14 + 14 + 11 + v)
                        else:
                            pe.wait_ge(S["st_used"], 12 * n + 21 + v)
                        dst = bank(v, H)
                        if k < 2:
                            dst = e2(dst)
                            pe.matmul(dst[:, :, 0:H], ident_b[:, :], bcast(behind_b[:, :], 1, 2), start=True, stop=False, skip_group_check=True)
                            ins = pe.matmul(dst, k_t[p][q, 0:H], q_m[p][q, 2 * k:2 * k + 2, :], start=False, stop=False, skip_group_check=True)
                        else:
                            dst = dst.rearrange("p (e s) -> p e s", e=4)
                            pe.matmul(dst, ident_b[:, :], bcast(behind_b[:, :], 1, 4), start=True, stop=False, skip_group_check=True)
                            ins = pe.matmul(dst, k_t[p][q, H:T], q_m[p][q, :, H:T], start=False, stop=False, skip_group_check=True)
                        ins.then_inc(S["key_mm"], 1)

                def values(h):
                    pe.wait_ge(S["st_used"], 12 * n + 24 + 3 * h + 3)
                    if h == 0:
                        pe.wait_ge(S["av_used"], 2 * n + 2)
                    for e in range(NX):
                        at = slice((4 * h + e) * (DH + 1), (4 * h + e + 1) * (DH + 1))
                        pe.matmul(p_av[0][0:H, at], e_0[h % 2][:, e, 0:H], v_1[p][:, 0, h, :], start=True, stop=True)
                        pe.matmul(p_av[1][0:H, at], e_0[h % 2][:, e, H:T], v_1[p][:, 0, h, :], start=True, stop=False)
                        ins = pe.matmul(p_av[1][0:H, at], e_1[h % 2][:, e, :], v_1[p][:, 1, h, :], start=False, stop=True)
                    ins.then_inc(S["av"], 1)

                pe.wait_ge(S["s_used"], 14 * n + 28)
                scores(0)
                for h in range(NH):
                    if h + 1 < NH:
                        scores(h + 1)
                    values(h)
                pe.wait_ge(S["masked"], n + 2)
                pe.wait_ge(S["done"], n + 2)
                for g in range(4):
                    ins = pe.transpose(p_b[:, H * g:H * g + H], qkv_p[:, g // 2, 8 * (g % 2):8 * (g % 2) + 8, :].rearrange("p e d -> p (e d)"), ident[0:H, 0:H])
                ins.then_inc(S["bmm"], 1)
                pe.wait_ge(S["bact"], 5 * n + 1)
                for g in range(4):
                    ins = pe.matmul(p_b[0:H, 8 * g:8 * g + 8], qkv_t[:, g, :], w_g[:, g % 2, :, :].rearrange("p a e -> p (a e)"), start=True, stop=True)
                ins.then_inc(S["bmm"], 1)
                pe.wait_ge(S["bdve"], 4 * n + 2)
                pe.transpose(p_b[:, 0:H], fx[:, :, :].rearrange("p n d -> p (n d)"), ident[0:H, 0:H]).then_inc(S["bmm"], 1)
                pe.wait_ge(S["bact"], 5 * n + 3)
                pe.matmul(p_b[:, 256:256 + H], w_1[:, :], fx_t[:, :], start=True, stop=True).then_inc(S["bmm"], 1)
                pe.wait_ge(S["bdve"], 4 * n + 3)
                pe.matmul(p_b[0:H, 0:128], hm_t[:, :], w_2[:, :], start=True, stop=True).then_inc(S["bmm"], 1)
                pe.wait_ge(S["rstd1"], 2 * n + 2)
                pe.wait_ge(S["fo_done"], n + 1)
                pe.transpose(p_b[:, 0:H], fo[:, :, :].rearrange("p n d -> p (n d)"), ident[0:H, 0:H]).then_inc(S["bmm"], 1)
                pe.wait_ge(S["bact"], 5 * n + 4)
                pe.matmul(p_b[0:H, 256:264], fo_t[:, :], w_f[:, :, :].rearrange("p t h -> p (t h)"), start=True, stop=True).then_inc(S["bmm"], 1)

            pipelined(pe, B, front, back)

        @blk.vector
        def _(dve):
            dve.wait_ge(S["consts"], ALL)
            dve.wait_ge(S["ready"], 3)
            dve.sem_inc(S["s_used"], 14)
            dve.sem_inc(S["sx_read"], 1)
            dve.sem_inc(S["av_used"], 2)
            dve.sem_inc(S["done"], 2)
            for p in range(2):
                dve.sem_inc(stored[p], 16)

            def front(n, p):
                x = rows[p]
                dve.wait_ge(loaded[p], (n - p) // 2 * 32 + 32)
                normed(dve, x[:, :, :], sq[:, :, :], st[:, 0, :], st[:, 1, :], st[:, 2, :], C, 1e-5, S["var"])
                dve.wait_ge(S["rstd"], n + 1)
                for k in range(2):
                    ins = dve.tensor_tensor(u[:, :, k, :], x[:, :, :], bcast(st[:, 3, :], 2, C), ALU.mult)
                ins.then_inc(S["u_done"], 1)
                dve.wait_ge(S["fev"], 3 * n + 4)
                dve.wait_ge(S["masked"], n)
                dve.tensor_tensor(sx[:, :, :], p_f[0:H, 384:512].rearrange("p (t c) -> p t c", t=2), bcast(b_h[:, :], 1, 2), ALU.add).then_inc(S["sx_read"], 1)
                dve.drain()
                dve.tensor_scalar(full[p][:, :, :], sx[:, :, :], 0.0, None, ALU.not_equal)
                for h in range(NH):
                    for k in range(3):
                        v = 2 + 3 * h + k
                        dve.wait_ge(S["max_mm"], 16 * n + v + 1)
                        if k == 0:
                            ins = dve.tensor_reduce(tops[:, 0, :, 32 * h], bank(v, H).rearrange("p (e s) -> p e s", e=4), AX.X, ALU.max)
                        else:
                            ins = dve.tensor_reduce(tops[:, 1, 2 * (k - 1):2 * k, 32 * h], e2(bank(v, H)), AX.X, ALU.max)
                        ins.then_inc(S["s_used"], 1)
                for k in range(2):
                    dve.wait_ge(S["max_mm"], 16 * n + 15 + k)
                    dve.wait_ge(S["key_mm"], 12 * n + 12)
                    dve.tensor_tensor(q_m[p][:, 2 * k:2 * k + 2, :], e2(bank(14 + k, 128)), q_t[:, 2 * k:2 * k + 2, :], ALU.add).then_inc(S["s_used"], 1)

            def back(n, p):
                for t in range(2):
                    dve.wait_ge(S["av"], 4 * n + 12)
                    o = p_av[t][0:H, 0:16 * (DH + 1)].rearrange("p (g d) -> p g d", d=DH + 1)
                    dve.reciprocal(den[:, t, :], o[:, :, DH])
                    dve.drain()
                    if t == 0:
                        dve.wait_ge(S["masked"], n + 1)
                    dve.tensor_tensor(qkv[:, t, :, :], o[:, :, 0:DH], bcast(den[:, t, :], 2, DH), ALU.mult).then_inc(S["av_used"], 1)
                dve.wait_ge(S["bmm"], 7 * n + 9)
                dve.tensor_tensor(gate[:, :, :].rearrange("p (t n) e -> p t (n e)", t=2), p_b[0:H, 0:32].rearrange("p (t g) -> p t g", t=2), bcast(b_g[:, :], 1, 2), ALU.add)
                dve.drain()
                dve.tensor_reduce(red[:, 0, :], gate[:, :, :], AX.X, ALU.max)
                dve.drain()
                dve.tensor_tensor(gate[:, :, :], gate[:, :, :], bcast(red[:, 0, :], 2, NX), ALU.subtract).then_inc(S["bdve"], 1)
                dve.wait_ge(S["bact"], 5 * n + 2)
                dve.tensor_reduce(red[:, 1, :], gate_e[:, :, :], AX.X, ALU.add)
                dve.drain()
                dve.reciprocal(red[:, 2, :], red[:, 1, :])
                dve.drain()
                dve.tensor_tensor(gate[:, :, :], gate_e[:, :, :], bcast(red[:, 2, :], 2, NX), ALU.mult)
                dve.drain()
                g32 = prod[:, :, :, :, :].rearrange("p t n e d -> p (t n e) d")
                dve.tensor_tensor(g32, qkv_p[:, :, :, :].rearrange("p t g d -> p (t g) d"), bcast(gate[:, :, :].rearrange("p g e -> p (g e)"), 2, DH), ALU.mult)
                dve.drain()
                dve.tensor_reduce(fx[:, :, :], prod[:, :, :, :, :].rearrange("p t n e d -> p (t n) d e"), AX.X, ALU.add)
                dve.drain()
                x = fx[:, :, :]
                dve.tensor_tensor(x, x, resid[:, :, :].rearrange("p t (n d) -> p (t n) d", n=NH), ALU.add)
                dve.drain()

                def norm16(y, k, gain, shift, out, done):
                    normed(dve, y, sq16[:, :, :], vs[:, 0, :], vs[:, 1, :], vs[:, 2, :], DH, 1e-8, S["var1"])
                    dve.wait_ge(S["rstd1"], 2 * n + k + 1)
                    dve.tensor_tensor(y, y, bcast(vs[:, 3, :], 2, DH), ALU.mult)
                    dve.drain()
                    dve.tensor_tensor(y, y, bcast(gain[:, :], 1, 2 * NH), ALU.mult)
                    dve.drain()
                    dve.tensor_tensor(out, y, bcast(shift[:, :], 1, 2 * NH), ALU.add).then_inc(done, 1)

                norm16(x, 0, ln_g, ln_b, x, S["bdve"])
                dve.wait_ge(S["bmm"], 7 * n + 11)
                dve.tensor_scalar(hx_t[:, :], p_b[:, 256:256 + H], b_1[:, 0:1], 0.0, ALU.add, ALU.max)
                dve.drain()
                dve.scalar_tensor_tensor(out=hm_t[:, :], in0=fx_t[:, :], scalar=0.0, in1=hx_t[:, :], op0=ALU.not_equal, op1=ALU.mult).then_inc(S["bdve"], 1)
                dve.wait_ge(S["bmm"], 7 * n + 12)
                dve.tensor_tensor(hx[:, :, :], p_b[0:H, 0:128].rearrange("p (g d) -> p g d", d=DH), bcast(b_2[:, :], 1, 2 * NH), ALU.add)
                dve.drain()
                dve.scalar_tensor_tensor(out=hx[:, :, :], in0=x, scalar=0.0, in1=hx[:, :, :], op0=ALU.not_equal, op1=ALU.mult)
                dve.drain()
                dve.tensor_tensor(hx[:, :, :], hx[:, :, :], x, ALU.add)
                dve.drain()
                norm16(hx[:, :, :], 1, fn_g, fn_b, fo[:, :, :], S["fo_done"])
                dve.wait_ge(S["bmm"], 7 * n + 14)
                logits = p_b[0:H, 256:264].rearrange("p (t h) -> p t h", t=2)
                dve.tensor_reduce(fr[:, 0, :], logits, AX.X, ALU.max)
                dve.drain()
                dve.tensor_tensor(fg[:, :, :], logits, bcast(fr[:, 0, :], 2, NH), ALU.subtract).then_inc(S["bdve"], 1)
                dve.wait_ge(S["bact"], 5 * n + 5)
                dve.tensor_reduce(fr[:, 1, :], fg_e[:, :, :], AX.X, ALU.add)
                dve.drain()
                dve.reciprocal(fr[:, 2, :], fr[:, 1, :])
                dve.drain()
                dve.tensor_tensor(fg[:, :, :], fg_e[:, :, :], bcast(fr[:, 2, :], 2, NH), ALU.mult)
                dve.drain()
                dve.tensor_tensor(fo[:, :, :], fo[:, :, :], bcast(fg[:, :, :].rearrange("p t h -> p (t h)"), 2, DH), ALU.mult)
                dve.drain()
                dve.wait_ge(stored[p], (n - p) // 2 * 16 + 16)
                dve.tensor_tensor(res[p][:, :, :], fo[:, :, :].rearrange("p (t n) d -> p t (n d)", t=2), kept[p][:, :, :], ALU.add).then_inc(S["done"], 1)

            pipelined(dve, B, front, back)


def constants():
    tables = {"c_ident": np.eye(128), "c_iota": np.arange(256.0)}
    for made in (stu_constants(), select_constants(), relation_constants(), sample_constants(), ffn_constants()):
        tables.update(made)
    return {k: np.ascontiguousarray(v, np.float32) for k, v in tables.items()}


LAYOUTS = {
    "m_u_taps": ("L0_attn_m_u", (2, 1, 0)),
    "b1_cols": ("L0_ffn_b1", (1, 0)),
    "wq_t": ("L1_ffn_wq", (0, 3, 1, 2)),
    "wk_t": ("L1_ffn_wk", (0, 2, 1)),
    "wv_t": ("L1_ffn_wv", (0, 2, 1)),
    "gate_t": ("L1_ffn_gate_w", (0, 2, 1)),
    "fc1_t": ("L1_ffn_fc1_w", (1, 0)),
    "fc2_t": ("L1_ffn_fc2_w", (1, 0)),
    "fgate_t": ("L1_ffn_fgate_w", (1, 0)),
}

SCRATCH = {
    "h0": ([B, T, C], F32), "h1": ([B, T, C], F32), "u": ([B, T, C], F32), "w_route": ([B, NE], F32), "h2": ([B, T, C], F32),
    "num_low": ([2, B // 2, T_LOW * NR * KM], BF16), "dist_low": ([2, B // 2, T_LOW * NR * KM], BF16),
    "num_high": ([2, B // 2, (T - T_LOW) * NR * KM], BF16), "dist_high": ([2, B // 2, (T - T_LOW) * NR * KM], BF16),
    "q_n": ([B, C, ROWS], F32), "key_parts": ([B, T, 3 * C], BF16),
    "heads_low": ([STEPS["low"][0], TOKG, 24], F32), "heads_high": ([STEPS["high"][0], TOKG, 24], F32),
    "h3": ([B, T, C], F32), "resid": ([T, C], F32),
}


def tower(nc, d):
    for name, (shape, dt) in SCRATCH.items():
        d[name] = nc.dram_tensor("scratch_" + name, shape, dt, kind="Internal").ap()
    token_attention(nc, d)
    spectral_unit(nc, d)
    routing(nc, d)
    experts(nc, d)
    select_keys(nc, d)
    relations(nc, d, "low")
    relations(nc, d, "high")
    sample(nc, d)
    head_residual(nc, d)
    head_mixture(nc, d)


def kernel(**inputs):
    import concourse.bacc as bacc
    from concourse.bass_utils import run_bass_kernel_spmd

    arrays = {k: np.ascontiguousarray(v) for k, v in inputs.items()}
    for name, (source, axes) in LAYOUTS.items():
        arrays[name] = np.ascontiguousarray(np.transpose(arrays[source], axes))
    arrays["hl_w_t"] = np.ascontiguousarray(arrays["L1_ffn_hl_w"].reshape(C, C).T)
    arrays.update(constants())
    nc = bacc.Bacc("TRN2", target_bir_lowering=False, num_devices=1)
    d = {k: nc.dram_tensor(f"in_{k}_dram", a.shape, mybir.dt.from_np(a.dtype), kind="ExternalInput").ap() for k, a in arrays.items()}
    d["out"] = nc.dram_tensor("out_0_dram", (B, T, C), F32, kind="ExternalOutput").ap()
    tower(nc, d)
    r = run_bass_kernel_spmd(nc, [{f"in_{k}_dram": a for k, a in arrays.items()}], core_ids=[0])
    return r.results[0]["out_0_dram"]
```

```python
import math
from contextlib import ExitStack

import numpy as np
import concourse.bass as bass
from concourse import mybir

ALU = mybir.AluOpType
ACT = mybir.ActivationFunctionType
AX = mybir.AxisListType
F32 = mybir.dt.float32
BF16 = mybir.dt.bfloat16
U32 = mybir.dt.uint32

B, L, C = 32, 256, 64
WIN = 9
T = L - WIN + 1
H = T // 2


class Phase:

    def __init__(self, nc, tag):
        self.nc, self.tag, self.stack, self.sems = nc, tag, ExitStack(), []

    def __enter__(self):
        self.stack.__enter__()
        return self

    def __exit__(self, *e):
        self.stack.__exit__(*e)
        self.nc.clear_and_free_semaphores(self.sems)
        self.nc.all_engine_barrier()

    def sb(self, name, shape, dt=F32):
        return self.stack.enter_context(self.nc.sbuf_tensor(f"{self.tag}_{name}", shape, dt))

    def ps(self, name, shape, dt=F32):
        return self.stack.enter_context(self.nc.psum_tensor(f"{self.tag}_{name}", shape, dt))

    def sem(self, name):
        self.sems.append(self.nc.alloc_semaphore(name=f"{self.tag}_{name}"))
        return self.sems[-1]

    def block(self):
        return self.stack.enter_context(self.nc.Block())


def bcast(ap, at, n):
    steps = [list(x) for x in ap.ap]
    return bass.AP(tensor=ap.tensor, offset=ap.offset, ap=steps[:at] + [[0, n]] + steps[at:])


def on_partitions(ap, n):
    return bass.AP(tensor=ap.tensor, offset=ap.offset, ap=[[0, n]] + [list(x) for x in ap.ap])


def in_ticks(eng, n, tick, peeled=0):
    tick(-1, 1, True, False, False)
    tick(0, 0, True, True, False)
    with eng.Fori(0, (n - peeled) // 2 - 1) as k:
        for p in range(2):
            tick(k * 2 + (1 + p), 1 - p, True, True, True)
    for i in range(n - 1 - peeled, n - 1):
        tick(i, i % 2, True, True, True)
    tick(n - 1, 1, False, True, True)
    tick(n, 0, False, False, True)


def token_attention(nc, d):
    with Phase(nc, "tok") as m:
        ident = m.sb("ident", [128, 128])
        w_key = m.sb("w_key", [128, 128])
        w_qry = m.sb("w_qry", [128, 128])
        v_two = m.sb("v_two", [128, 2])
        b_col = m.sb("b_col", [128, 1])
        x_rows = [m.sb(f"x_rows{p}", [128, 2, 2, C]) for p in range(2)]
        x_win = [m.sb(f"x_win{p}", [H, 4, WIN * C]) for p in range(2)]
        x_t = m.sb("x_t", [128, L])
        key = m.sb("key", [128, L])
        qry = m.sb("qry", [128, T])
        pre = [m.sb(f"pre{p}", [128, WIN, T]) for p in range(2)]
        th = [m.sb(f"th{p}", [128, WIN, T]) for p in range(2)]
        top = m.sb("top", [H, 4])
        low = m.sb("low", [H, 4, WIN])
        exps = m.sb("exps", [H, 4, WIN])
        tot = m.sb("tot", [H, 4])
        wt = m.sb("wt", [H, 4, WIN])
        h0 = [m.sb(f"h0{p}", [H, 4, C]) for p in range(2)]
        p_xt = m.ps("p_xt", [128, 512])
        p_key = m.ps("p_key", [128, 512])
        p_qry = m.ps("p_qry", [128, 512])
        p_score = m.ps("p_score", [128, 512])
        cleared, consts = m.sem("cleared"), m.sem("consts")
        rows_in = [m.sem(f"rows_in{p}") for p in range(2)]
        win_in = [m.sem(f"win_in{p}") for p in range(2)]
        xt_done, xt_sb, kq_done, kq_sb = m.sem("xt_done"), m.sem("xt_sb"), m.sem("kq_done"), m.sem("kq_sb")
        pre_dve, pre_pool, th_done = m.sem("pre_dve"), m.sem("pre_pool"), m.sem("th_done")
        score_done, low_done, exps_done = m.sem("score_done"), m.sem("low_done"), m.sem("exps_done")
        h0_done = m.sem("h0_done")
        stored = [m.sem(f"stored{p}") for p in range(2)]
        score = p_score[0:H, 0:4 * WIN].rearrange("p (g s) -> p g s", s=WIN)
        DVE_S = 4
        N = B // 2
        blk = m.block()

        @blk.sync
        def _(sp):
            sp.wait_ge(cleared, 3)
            for a in range(2):
                half = slice(64 * a, 64 * a + 64)
                sp.dma_start(w_key[half, half], d["L0_tok_W_key"]).then_inc(consts, 16)
                sp.dma_start(w_qry[half, half], d["L0_tok_W_qry"]).then_inc(consts, 16)
                sp.dma_start(v_two[half, a:a + 1], d["L0_tok_v"].rearrange("(p a) -> p a", a=1)).then_inc(consts, 16)
                sp.dma_start(b_col[half, :], d["L0_tok_b"].rearrange("(p a) -> p a", a=1)).then_inc(consts, 16)
            sp.dma_start(ident[:, :], d["c_ident"]).then_inc(consts, 16)
            with sp.Fori(0, N // 2) as i:
                for p in range(2):
                    n = i * 2 + p
                    pair = d["x"][bass.ds(n * 2, 2), :, :]
                    sp.wait_ge(xt_done, n + 1)
                    sp.dma_start(x_rows[p][:, 0, :, :], pair[:, 0:128, :].rearrange("a p c -> p a c")).then_inc(rows_in[p], 16)
                    sp.dma_start(x_rows[p][:, 1, :, :], pair[:, 128:256, :].rearrange("a p c -> p a c")).then_inc(rows_in[p], 16)
                    sp.wait_ge(h0_done, n + 1)
                    for g in range(4):
                        src = bass.AP(tensor=pair.tensor, offset=pair.offset + ((g % 2) * L + (g // 2) * H) * C,
                                      ap=[[C, H], [1, WIN * C]])
                        sp.dma_start(x_win[p][:, g, :], src).then_inc(win_in[p], 16)
            for p in range(2):
                sp.wait_ge(stored[p], 32 * (N // 2) + 32)

        @blk.gpsimd
        def _(pool):
            for t in (w_key, w_qry, v_two):
                pool.memset(t[:, :], 0.0).then_inc(cleared, 1)

            def tick(i, p, front, back, tail):
                if front:
                    pool.wait_ge(kq_sb, i * 2 + 6)
                    pool.wait_ge(th_done, i + 2)
                    for s in range(DVE_S, WIN):
                        ins = pool.tensor_tensor(pre[1 - p][:, s, :], key[:, s:s + T], qry[:, :], ALU.add)
                    ins.then_inc(pre_pool, 1)

            in_ticks(pool, N, tick)

        @blk.scalar
        def _(act):
            act.wait_ge(consts, 16 * 9)
            act.sem_inc(xt_done, 2)
            act.sem_inc(h0_done, 2)
            act.sem_inc(th_done, 2)
            act.sem_inc(pre_dve, 1)
            act.sem_inc(pre_pool, 1)
            act.sem_inc(kq_sb, 2)

            def front_of(n, p):
                act.wait_ge(xt_done, n + 3)
                act.activation(x_t[:, :], p_xt[:, 0:L], ACT.Copy).then_inc(xt_sb, 1)
                act.wait_ge(kq_done, n + 1)
                act.wait_ge(pre_dve, n + 1)
                act.wait_ge(pre_pool, n + 1)
                act.activation(key[:, :], p_key[:, 0:L], ACT.Copy).then_inc(kq_sb, 1)
                act.activation(qry[:, :], p_qry[:, 0:T], ACT.Identity, bias=b_col[:, 0:1]).then_inc(kq_sb, 1)

            def tick(i, p, front, back, tail):
                n = i + 1
                if front:
                    front_of(n, 1 - p)
                if tail:
                    act.wait_ge(h0_done, i + 2)
                    for t in range(2):
                        act.dma_start(d["h0"][bass.ds(i * 2 - 2, 2), H * t:H * t + H, :].rearrange("a p c -> p a c"), h0[1 - p][:, 2 * t:2 * t + 2, :]).then_inc(stored[1 - p], 16)
                if back:
                    act.wait_ge(low_done, i + 2)
                    act.activation(exps[:, :, :], low[:, :, :], ACT.Exp).then_inc(exps_done, 1)
                if front:
                    act.wait_ge(pre_dve, n + 2)
                    act.wait_ge(pre_pool, n + 2)
                    act.activation(th[1 - p][:, :, :], pre[1 - p][:, :, :], ACT.Tanh).then_inc(th_done, 1)

            in_ticks(act, N, tick)

        @blk.tensor
        def _(pe):
            pe.wait_ge(consts, 16 * 9)

            def front_of(n, p):
                pe.wait_ge(rows_in[p], (n - p) // 2 * 32 + 32)
                for h in range(2):
                    ins = pe.transpose(p_xt[:, 128 * h:128 * h + 128], x_rows[p][:, h, :, :].rearrange("p a c -> p (a c)"), ident[:, :])
                ins.then_inc(xt_done, 1)
                pe.wait_ge(xt_sb, n + 1)
                pe.wait_ge(kq_sb, n * 2 + 2)
                pe.matmul(p_key[:, 0:L], w_key[:, :], x_t[:, :], start=True, stop=True)
                pe.matmul(p_qry[:, 0:T], w_qry[:, :], x_t[:, WIN // 2:WIN // 2 + T], start=True, stop=True).then_inc(kq_done, 1)

            def tick(i, p, front, back, tail):
                if front:
                    front_of(i + 1, 1 - p)
                if back:
                    pe.wait_ge(th_done, i + 3)
                    pe.wait_ge(low_done, i + 1)
                    for t in range(2):
                        for s in range(WIN):
                            ins = pe.matmul(score[:, 2 * t:2 * t + 2, s], th[p][:, s, H * t:H * t + H], v_two[:, :], start=True, stop=True)
                    ins.then_inc(score_done, 1)

            in_ticks(pe, N, tick)

        @blk.vector
        def _(dve):
            for p in range(2):
                dve.sem_inc(stored[p], 32)
            dve.sem_inc(low_done, 1)

            def front_of(n, p):
                dve.wait_ge(kq_sb, n * 2 + 4)
                dve.wait_ge(th_done, n + 1)
                for s in range(DVE_S):
                    ins = dve.tensor_tensor(pre[p][:, s, :], key[:, s:s + T], qry[:, :], ALU.add)
                ins.then_inc(pre_dve, 1)

            def back_of(n, p):
                dve.wait_ge(score_done, n + 1)
                dve.tensor_reduce(top[:, :], score, AX.X, ALU.max)
                dve.drain()
                dve.tensor_tensor(low[:, :, :], score, bcast(top[:, :], 2, WIN), ALU.subtract).then_inc(low_done, 1)
                dve.wait_ge(exps_done, n + 1)
                dve.tensor_reduce(tot[:, :], exps[:, :, :], AX.X, ALU.add)
                dve.drain()
                dve.reciprocal(tot[:, :], tot[:, :])
                dve.drain()
                dve.tensor_tensor(wt[:, :, :], exps[:, :, :], bcast(tot[:, :], 2, WIN), ALU.mult)
                dve.drain()
                dve.wait_ge(win_in[p], (n - p) // 2 * 64 + 64)
                xw = x_win[p][:, :, :].rearrange("p g (s c) -> p (g s) c", c=C)
                dve.tensor_tensor(xw, xw, bcast(wt[:, :, :].rearrange("p g s -> p (g s)"), 2, C), ALU.mult)
                dve.drain()
                dve.wait_ge(stored[p], (n - p) // 2 * 32 + 32)
                dve.tensor_reduce(h0[p][:, :, :], x_win[p][:, :, :].rearrange("p g (s c) -> p g c s", c=C), AX.X, ALU.add).then_inc(h0_done, 1)

            def tick(i, p, front, back, tail):
                if front:
                    front_of(i + 1, 1 - p)
                if back:
                    back_of(i, p)

            in_ticks(dve, N, tick)


NF = T + 1
FQ = [(0, 125), (125, 124)]
NK, NU = 24, 3
CH, NCH = 8, T // 8


def stu_constants():
    n = 2 * T
    f = np.arange(NF)
    ang = 2 * np.pi * ((np.arange(n)[:, None] * f[None, :]) % n) / n
    cos, sin = np.cos(ang), np.sin(ang)
    fwd = np.concatenate([cos, -sin], 1).reshape(4, H, 2 * NF).transpose(1, 0, 2)
    rot = np.concatenate([sin, cos], 1).reshape(4, H, 2 * NF).transpose(1, 0, 2)
    taps = np.zeros((128, 2 * NF))
    taps[24:27] = np.concatenate([cos, -sin], 1)[:NU]
    taps[56:59] = np.concatenate([sin, cos], 1)[:NU]
    w = np.where((f == 0) | (f == T), 1.0, 2.0)[:, None] / n
    inv = np.zeros((125, 2, 2, T))
    for a, (f0, nf) in enumerate(FQ):
        inv[:nf, a, 0] = (w * cos.T[:, :T])[f0:f0 + nf]
        inv[:nf, a, 1] = (-w * sin.T[:, :T])[f0:f0 + nf]
    low = np.concatenate([np.eye(64), np.zeros((64, 64))], 1)
    return {"c_fwd": fwd, "c_rot": rot, "c_taps": taps, "c_inv": inv, "c_low": low}


def spectral_unit(nc, d):
    with Phase(nc, "stu") as m:
        ident = m.sb("ident", [128, 128])
        u = m.sb("u", [H, 2, B, C])
        spec_in = m.sb("spec_in", [128, NF, B])
        spec_out = m.sb("spec_out", [128, NF, B])
        mix = m.sb("mix", [128, 125, 128])
        filt_w = m.sb("filt_w", [128, 2, C, C])
        fwd = m.sb("fwd", [H, 4, 2 * NF])
        rot = m.sb("rot", [H, 4, 2 * NF])
        inv = m.sb("inv", [125, 2, 2, T])
        spec_t = [m.sb(f"spec_t{p}", [125, 2, 128]) for p in range(2)]
        filt = m.sb("filt", [128, 2 * NF])
        eig = m.sb("eig", [H, 4, NK])
        lam = m.sb("lam", [64, 3])
        st = m.sb("st", [H, 4, 64])
        comp = m.sb("comp", [128, 128])
        power = m.sb("power", [128, CH, 64])
        step8 = m.sb("step8", [128, 128])
        rows = spec_out[:, :, :].rearrange("p f b -> p (f b)")[0:H, 0:2 * B * C].rearrange("p (t b c) -> p t b c", t=2, b=B)
        sq = mix[:, :, :].rearrange("p f b -> p (f b)")[0:H, 0:2 * B * C].rearrange("p (t b c) -> p t b c", t=2, b=B)
        flat = mix[:, :, :].rearrange("p f b -> p (f b)")
        loc = flat[:, 0:CH * NCH * B].rearrange("p (j c b) -> p j c b", j=CH, b=B)
        state = flat[:, CH * NCH * B:CH * NCH * B + NCH * B].rearrange("p (c b) -> p c b", b=B)
        res = filt_w[:, :, :, :].rearrange("p a d o -> p (a d o)")[0:H, 0:2 * B * C].rearrange("p (t b c) -> p t b c", t=2, b=B)
        bank = [m.ps(f"bank{k}", [128, 512]) for k in range(8)]
        S = {n: m.sem(n) for n in "cleared consts rows_in ln ln_act v_done v_sb dft dft_dve dft_act hmat hmat_dve hmat_act freq freq_sb back back_sb delta delta_sb pw pw_sb locmm loc_add loc_copy chain chain_sb carry carry_sb res_in fin fin_sb out scan0".split()}
        rsv = lambda a: a.rearrange("p t b c -> p (t b) c")
        blk = m.block()

        @blk.sync
        def _(sp):
            for t in range(2):
                sp.dma_start(rows[:, t, :, :], d["h0"][:, H * t:H * t + H, :].rearrange("b p c -> p b c")).then_inc(S["rows_in"], 16)
            sp.dma_start(fwd[:, :, :], d["c_fwd"]).then_inc(S["consts"], 16)
            sp.dma_start(rot[:, :, :], d["c_rot"]).then_inc(S["consts"], 16)
            sp.dma_start(inv[:, :, :, :], d["c_inv"]).then_inc(S["consts"], 16)
            sp.dma_start(ident[:, :], d["c_ident"]).then_inc(S["consts"], 16)
            sp.dma_start(filt[:, :], d["c_taps"]).then_inc(S["consts"], 16)
            sp.dma_start(eig[:, :, :], d["L0_attn_eig_vecs"][0:2 * T, :].rearrange("(a p) k -> p a k", p=H)).then_inc(S["consts"], 16)
            for a in range(2):
                sp.dma_start(lam[32 * a:32 * a + NK, 0:1], d["L0_attn_eig_vals"].rearrange("(p a) -> p a", a=1)).then_inc(S["consts"], 16)
            sp.dma_start(comp[0:64, :], d["L0_attn_m_y"].rearrange("o k d -> o (k d)")).then_inc(S["consts"], 16)
            sp.dma_start(comp[64:128, :], d["c_low"]).then_inc(S["consts"], 16)
            sp.wait_ge(S["cleared"], 1)
            for a in range(2):
                sp.dma_start(filt_w[32 * a:32 * a + NK, a, :, :], d["L0_attn_m_phi"].rearrange("(k d) o -> k d o", k=NK)).then_inc(S["consts"], 16)
                sp.dma_start(filt_w[32 * a + NK:32 * a + NK + NU, a, :, :], d["m_u_taps"]).then_inc(S["consts"], 16)
            sp.wait_ge(S["hmat"], 128)
            h0_steps = d["h0"].rearrange("b (c t j) o -> t j c b o", t=2, j=4)
            h1_steps = d["h1"].rearrange("b (c t j) o -> t j c b o", t=2, j=4)
            for t in range(2):
                for j in range(4):
                    sp.dma_start(res[NCH * j:NCH * j + NCH, t, :, :], h0_steps[t, j]).then_inc(S["res_in"], 16)
            for t in range(2):
                sp.wait_ge(S["fin_sb"], 4 * t + 4)
                for j in range(4):
                    sp.dma_start(h1_steps[t, j], res[NCH * j:NCH * j + NCH, t, :, :]).then_inc(S["out"], 16)
            sp.wait_ge(S["out"], 128)

        @blk.gpsimd
        def _(pool):
            pool.memset(filt_w[:, :, :, :], 0.0).then_inc(S["cleared"], 1)

        @blk.scalar
        def _(act):
            act.wait_ge(S["consts"], 16 * 14)
            for a in range(2):
                q = slice(32 * a, 32 * a + NK)
                act.activation(lam[q, 1:2], lam[q, 0:1], ACT.Sqrt)
            act.drain()
            for a in range(2):
                q = slice(32 * a, 32 * a + NK)
                act.activation(lam[q, 2:3], lam[q, 1:2], ACT.Sqrt)
            act.drain()
            act.wait_ge(S["ln"], 1)
            act.activation(st[:, 2, :], st[:, 1, :], ACT.Sqrt).then_inc(S["ln_act"], 1)
            act.wait_ge(S["v_done"], 1)
            for a in range(2):
                q = slice(32 * a, 32 * a + NK)
                act.activation(filt[q, :], bank[a][q, 0:2 * NF], ACT.Copy, scale=lam[q, 2:3]).then_inc(S["v_sb"], 1)
            for k in range(1, B, 2):
                act.wait_ge(S["dft"], k + 1)
                act.activation(spec_in[:, :, k], bank[2 + k % 4][:, 0:NF], ACT.Copy).then_inc(S["dft_act"], 1)
            for t, (f0, nf) in enumerate(FQ):
                if t:
                    act.wait_ge(S["freq"], 8)
                for o in range(1, 64, 2):
                    act.wait_ge(S["hmat"], 64 * t + o + 1)
                    act.activation(mix[:, 0:nf, :].rearrange("p f (r o) -> p r f o", r=2)[:, :, :, o],
                                   bank[o % 4][:, 0:2 * nf].rearrange("p (r f) -> p r f", r=2), ACT.Copy).then_inc(S["hmat_act"], 1)
            for k in range(B):
                act.wait_ge(S["back"], k + 1)
                if k >= 2:
                    act.wait_ge(S["delta"], k - 1)
                for t, (f0, nf) in enumerate(FQ):
                    ins = act.activation(spec_t[k % 2][0:nf, t, :], bank[k % 2][0:nf, 128 * t:128 * t + 128], ACT.Copy)
                ins.then_inc(S["back_sb"], 1)
            for j in range(1, CH):
                if j > 1:
                    act.wait_ge(S["loc_add"], 2 * (j - 1))
                else:
                    act.wait_ge(S["delta_sb"], B)
                act.activation(loc[64:128, j, :, :], loc[0:64, j - 1, :, :], ACT.Copy).then_inc(S["loc_copy"], 1)

        @blk.tensor
        def _(pe):
            pe.wait_ge(S["consts"], 16 * 14)
            for a, table in enumerate((fwd, rot)):
                for t in range(4):
                    ins = pe.matmul(bank[a][32 * a:32 * a + NK, 0:2 * NF], eig[:, t, :], table[:, t, :], start=(t == 0), stop=(t == 3))
            ins.then_inc(S["v_done"], 1)
            pe.transpose(bank[7][:, 0:64], comp[0:64, :], ident[0:64, 0:64]).then_inc(S["pw"], 1)
            for j in range(1, CH):
                pe.wait_ge(S["pw_sb"], j)
                pe.matmul(bank[7][:, 64 * j:64 * j + 64], comp[:, :], power[:, j - 1, :], start=True, stop=True).then_inc(S["pw"], 1)
            pe.wait_ge(S["ln"], 2)
            for k in range(B):
                if k >= 4:
                    pe.wait_ge(S["dft_act" if k % 2 else "dft_dve"], (k - 4) // 2 + 1)
                for r in range(2):
                    for t in range(2):
                        ins = pe.matmul(bank[2 + k % 4][64 * r:64 * r + 64, 0:NF], u[:, t, k, :], fwd[:, t, NF * r:NF * r + NF], start=(t == 0), stop=(t == 1))
                ins.then_inc(S["dft"], 1)
            pe.wait_ge(S["v_sb"], 2)
            for t, (f0, nf) in enumerate(FQ):
                for o in range(64):
                    g = 64 * t + o
                    if g == 0:
                        pe.wait_ge(S["dft_dve"], B // 2)
                        pe.wait_ge(S["dft_act"], B // 2)
                    if g >= 4:
                        pe.wait_ge(S["hmat_act" if g % 2 else "hmat_dve"], (g - 4) // 2 + 1)
                    pe.matmul(bank[o % 4][:, 0:2 * nf], filt_w[:, :, :, o],
                              filt[:, :].rearrange("p (r f) -> p r f", r=2)[:, :, f0:f0 + nf], start=True, stop=True).then_inc(S["hmat"], 1)
                pe.wait_ge(S["hmat_dve"], 32 * t + 32)
                pe.wait_ge(S["hmat_act"], 32 * t + 32)
                for k in range((nf + 15) // 16):
                    if k >= 4 or t:
                        pe.wait_ge(S["freq_sb"], 8 * t + k - 3)
                    for f in reversed(range(16 * k, min(nf, 16 * k + 16))):
                        e = max(16 * k, f - 2)
                        ins = pe.matmul(bank[4 + k % 4][:, 32 * (e - 16 * k):32 * (f - 16 * k) + 32], mix[:, f, :],
                                        spec_in[:, f0 + e:f0 + f + 1, :].rearrange("p f b -> p (f b)"), start=True, stop=True)
                    ins.then_inc(S["freq"], 1)
            pe.wait_ge(S["freq_sb"], 16)
            def turned(k):
                if k >= 2:
                    pe.wait_ge(S["back_sb"], k - 1)
                for t, (f0, nf) in enumerate(FQ):
                    ins = pe.transpose(bank[k % 2][0:nf, 128 * t:128 * t + 128], spec_out[:, f0:f0 + nf, k], ident[:, :])
                ins.then_inc(S["back"], 1)

            turned(0)
            for k in range(B):
                if k + 1 < B:
                    turned(k + 1)
                pe.wait_ge(S["back_sb"], k + 1)
                if k >= 2:
                    pe.wait_ge(S["delta_sb"], k - 1)
                for t, (f0, nf) in enumerate(FQ):
                    for r in range(2):
                        ins = pe.matmul(bank[2 + k % 2][0:64, 0:T], spec_t[k % 2][0:nf, t, 64 * r:64 * r + 64], inv[0:nf, t, r, :],
                                        start=(t == 0 and r == 0), stop=(t == 1 and r == 1))
                ins.then_inc(S["delta"], 1)
            half = loc.rearrange("p j c b -> p j (c b)")
            NH = NCH * B // 2
            for j in range(1, CH):
                pe.wait_ge(S["scan0"], 1)
                if j > 1:
                    pe.wait_ge(S["loc_copy"], j - 1)
                for a in range(2):
                    if j > 1:
                        pe.wait_ge(S["loc_add"], 2 * (j - 2) + a + 1)
                    else:
                        pe.wait_ge(S["delta_sb"], B)
                    pe.matmul(bank[4 + a][0:64, 0:NH], power[:, 0, :], half[:, j - 1, NH * a:NH * a + NH], start=True, stop=True).then_inc(S["locmm"], 1)
            for c in range(NCH - 1):
                if c == 0:
                    pe.wait_ge(S["loc_copy"], CH - 1)
                pe.wait_ge(S["chain_sb"], c + 1)
                pe.matmul(bank[c % 2][:, 0:B], step8[:, :], state[:, c, :], start=True, stop=True).then_inc(S["chain"], 1)
            pe.wait_ge(S["chain_sb"], NCH)
            st2 = state.rearrange("p c b -> p (c b)")
            for j in range(CH):
                for a in range(2):
                    if 2 * j + a >= 4:
                        pe.wait_ge(S["carry_sb"], 2 * j + a - 3)
                    pe.matmul(bank[4 + (2 * j + a) % 4][0:64, 0:NH], power[:, j, :], st2[:, NH * a:NH * a + NH], start=True, stop=True).then_inc(S["carry"], 1)
            pe.wait_ge(S["carry_sb"], 2 * CH)
            for k in range(8):
                t, b0 = k // 4, 8 * (k % 4)
                if k >= 4:
                    pe.wait_ge(S["fin_sb"], k - 3)
                for b in range(8):
                    ins = pe.transpose(bank[k % 4][0:H, 64 * b:64 * b + 64], loc[0:64, 4 * t:4 * t + 4, :, b0 + b], ident[0:64, 0:64])
                ins.then_inc(S["fin"], 1)

        @blk.vector
        def _(dve):
            dve.wait_ge(S["rows_in"], 32)
            dve.tensor_reduce(st[:, 0, :], rsv(rows), AX.X, ALU.add)
            dve.drain()
            dve.tensor_scalar(st[:, 0, :], st[:, 0, :], 1.0 / C, None, ALU.mult)
            dve.drain()
            dve.tensor_tensor(rsv(rows), rsv(rows), bcast(st[:, 0, :], 2, C), ALU.subtract)
            dve.drain()
            dve.tensor_tensor(rsv(sq), rsv(rows), rsv(rows), ALU.mult)
            dve.drain()
            dve.tensor_reduce(st[:, 1, :], rsv(sq), AX.X, ALU.add)
            dve.drain()
            dve.tensor_scalar(st[:, 1, :], st[:, 1, :], 1.0 / C, 1e-5, ALU.mult, ALU.add).then_inc(S["ln"], 1)
            for j in range(CH):
                dve.wait_ge(S["pw"], j + 1)
                dve.tensor_copy(power[:, j, :], bank[7][:, 64 * j:64 * j + 64]).then_inc(S["pw_sb"], 1)
            dve.drain()
            dve.tensor_copy(step8[:, 0:64], power[:, CH - 1, :])
            dve.tensor_copy(step8[:, 64:128], power[:, CH - 2, :])
            dve.wait_ge(S["ln_act"], 1)
            dve.reciprocal(st[:, 3, :], st[:, 2, :])
            dve.drain()
            dve.tensor_tensor(u[:, :, :, :].rearrange("p t b c -> p (t b) c"), rsv(rows), bcast(st[:, 3, :], 2, C), ALU.mult).then_inc(S["ln"], 1)
            dve.drain()
            for k in range(0, B, 2):
                dve.wait_ge(S["dft"], k + 1)
                dve.tensor_copy(spec_in[:, :, k], bank[2 + k % 4][:, 0:NF]).then_inc(S["dft_dve"], 1)
            for t, (f0, nf) in enumerate(FQ):
                if t:
                    dve.wait_ge(S["freq"], 8)
                for o in range(0, 64, 2):
                    dve.wait_ge(S["hmat"], 64 * t + o + 1)
                    dve.tensor_copy(mix[:, 0:nf, :].rearrange("p f (r o) -> p r f o", r=2)[:, :, :, o],
                                    bank[o % 4][:, 0:2 * nf].rearrange("p (r f) -> p r f", r=2)).then_inc(S["hmat_dve"], 1)
                for k in range((nf + 15) // 16):
                    dve.wait_ge(S["freq"], 8 * t + k + 1)
                    n = min(nf - 16 * k, 16)
                    dve.tensor_copy(spec_out[:, f0 + 16 * k:f0 + 16 * k + n, :], bank[4 + k % 4][:, 0:32 * n].rearrange("p (f b) -> p f b", b=B)).then_inc(S["freq_sb"], 1)
            dve.memset(loc[64:128, 0, :, :], 0.0)
            dve.memset(state[:, 0, :], 0.0)
            for k in range(B):
                dve.wait_ge(S["delta"], k + 1)
                dve.tensor_copy(loc[0:64, :, :, k].rearrange("p j c -> p c j"), bank[2 + k % 2][0:64, 0:T].rearrange("p (c j) -> p c j", j=CH)).then_inc(S["delta_sb"], 1)
            dve.drain()
            dve.memset(st[:, 0, 0:1], 0.0).then_inc(S["scan0"], 1)
            half = loc.rearrange("p j c b -> p j (c b)")
            NH = NCH * B // 2
            for j in range(1, CH):
                for a in range(2):
                    dve.wait_ge(S["locmm"], 2 * (j - 1) + a + 1)
                    s = half[0:64, j, NH * a:NH * a + NH]
                    dve.tensor_tensor(s, bank[4 + a][0:64, 0:NH], s, ALU.add).then_inc(S["loc_add"], 1)
            dve.memset(st[:, 0, 0:1], 0.0).then_inc(S["chain_sb"], 1)
            dve.wait_ge(S["loc_copy"], CH - 1)
            for c in range(NCH - 1):
                dve.wait_ge(S["chain"], c + 1)
                dve.tensor_tensor(state[:, c + 1, :], bank[c % 2][:, 0:B], loc[:, CH - 1, c, :], ALU.add).then_inc(S["chain_sb"], 1)
            for j in range(CH):
                for a in range(2):
                    g = 2 * j + a
                    dve.wait_ge(S["carry"], g + 1)
                    s = half[0:64, j, NH * a:NH * a + NH]
                    dve.tensor_tensor(s, bank[4 + g % 4][0:64, 0:NH], s, ALU.add).then_inc(S["carry_sb"], 1)
            dve.wait_ge(S["res_in"], 128)
            for k in range(8):
                t, b0 = k // 4, 8 * (k % 4)
                dve.wait_ge(S["fin"], k + 1)
                s = res[:, t, b0:b0 + 8, :]
                dve.tensor_tensor(s, bank[k % 4][0:H, :].rearrange("p (b c) -> p b c", b=8), s, ALU.add).then_inc(S["fin_sb"], 1)


NE, FF = 8, 128
CAPACITY = float(math.ceil(B * T * 1.25 / NE))


def routing(nc, d):
    with Phase(nc, "route") as m:
        rows = m.sb("rows", [H, 2, B, C])
        sq = m.sb("sq", [H, 2, B, C])
        u = m.sb("u", [H, 2, B, C])
        st = m.sb("st", [H, 4, 64])
        mean_w = m.sb("mean_w", [H, 1])
        means = m.sb("means", [C, B])
        w_r = m.sb("w_r", [C, NE])
        b_r = m.sb("b_r", [B, NE])
        ones = m.sb("ones", [B, B])
        iota8 = m.sb("iota8", [B, NE])
        lg = m.sb("lg", [B, NE])
        ex = m.sb("ex", [B, NE])
        col = m.sb("col", [B, 8])
        best = m.sb("best", [B, 8])
        best_i = m.sb("best_i", [B, 8], U32)
        best_f = m.sb("best_f", [B, 8])
        hot = m.sb("hot", [B, 2, NE])
        wd = m.sb("wd", [B, NE])
        p_mean = m.ps("p_mean", [128, 512])
        p_log = m.ps("p_log", [128, 512])
        p_load = m.ps("p_load", [128, 512])
        S = {n: m.sem(n) for n in "rows_in consts ln ln_act u_done mean mean_sb log low ex1 rw load s2 ex2 tops ex3 wd out".split()}
        rsv = lambda a: a[:, :, :, :].rearrange("p t b c -> p (t b) c")
        blk = m.block()

        @blk.sync
        def _(sp):
            for t in range(2):
                sp.dma_start(rows[:, t, :, :], d["h1"][:, H * t:H * t + H, :].rearrange("b p c -> p b c")).then_inc(S["rows_in"], 16)
            sp.dma_start(w_r[:, :], d["L0_ffn_Wr"]).then_inc(S["consts"], 16)
            sp.dma_start(b_r[:, :], on_partitions(d["L0_ffn_br"], B)).then_inc(S["consts"], 16)
            sp.dma_start(iota8[:, :], on_partitions(d["c_iota"][0:NE], B)).then_inc(S["consts"], 16)
            sp.wait_ge(S["u_done"], 1)
            for t in range(2):
                sp.dma_start(d["u"][:, H * t:H * t + H, :].rearrange("b p c -> p b c"), u[:, t, :, :]).then_inc(S["out"], 16)
            sp.wait_ge(S["wd"], 1)
            sp.dma_start(d["w_route"], wd[:, :]).then_inc(S["out"], 16)
            sp.wait_ge(S["out"], 48)

        @blk.scalar
        def _(act):
            act.wait_ge(S["ln"], 1)
            act.activation(st[:, 2, :], st[:, 1, :], ACT.Sqrt).then_inc(S["ln_act"], 1)
            act.wait_ge(S["low"], 1)
            act.activation(ex[:, :], lg[:, :], ACT.Exp).then_inc(S["ex1"], 1)
            act.wait_ge(S["s2"], 1)
            act.activation(ex[:, :], lg[:, :], ACT.Exp).then_inc(S["ex2"], 1)
            act.wait_ge(S["tops"], 1)
            act.activation(col[:, 4:5], col[:, 3:4], ACT.Exp).then_inc(S["ex3"], 1)

        @blk.tensor
        def _(pe):
            pe.wait_ge(S["u_done"], 1)
            for b in range(B):
                for t in range(2):
                    ins = pe.matmul(p_mean[0:C, b:b + 1], u[:, t, b, :], mean_w[:, :], start=(t == 0), stop=(t == 1))
            ins.then_inc(S["mean"], 1)
            pe.wait_ge(S["consts"], 48)
            pe.wait_ge(S["mean_sb"], 1)
            pe.matmul(p_log[0:B, 0:NE], means[:, :], w_r[:, :], start=True, stop=True).then_inc(S["log"], 1)
            pe.wait_ge(S["rw"], 1)
            pe.matmul(p_load[0:B, 0:NE], ones[:, :], ex[:, :], start=True, stop=True).then_inc(S["load"], 1)

        @blk.vector
        def _(dve):
            dve.memset(mean_w[:, :], 1.0 / T)
            dve.memset(ones[:, :], 1.0)
            dve.wait_ge(S["rows_in"], 32)
            dve.tensor_reduce(st[:, 0, :], rsv(rows), AX.X, ALU.add)
            dve.drain()
            dve.tensor_scalar(st[:, 0, :], st[:, 0, :], 1.0 / C, None, ALU.mult)
            dve.drain()
            dve.tensor_tensor(rsv(rows), rsv(rows), bcast(st[:, 0, :], 2, C), ALU.subtract)
            dve.drain()
            dve.tensor_tensor(rsv(sq), rsv(rows), rsv(rows), ALU.mult)
            dve.drain()
            dve.tensor_reduce(st[:, 1, :], rsv(sq), AX.X, ALU.add)
            dve.drain()
            dve.tensor_scalar(st[:, 1, :], st[:, 1, :], 1.0 / C, 1e-5, ALU.mult, ALU.add).then_inc(S["ln"], 1)
            dve.wait_ge(S["ln_act"], 1)
            dve.reciprocal(st[:, 3, :], st[:, 2, :])
            dve.drain()
            dve.tensor_tensor(rsv(u), rsv(rows), bcast(st[:, 3, :], 2, C), ALU.mult).then_inc(S["u_done"], 1)
            dve.wait_ge(S["mean"], 1)
            dve.tensor_copy(means[:, :], p_mean[0:C, 0:B]).then_inc(S["mean_sb"], 1)
            dve.wait_ge(S["consts"], 48)

            def softmax_low(done):
                dve.drain()
                dve.tensor_reduce(col[:, 0:1], lg[:, :], AX.X, ALU.max)
                dve.drain()
                dve.tensor_scalar(lg[:, :], lg[:, :], col[:, 0:1], None, ALU.subtract).then_inc(done, 1)

            def softmax_norm():
                dve.tensor_reduce(col[:, 1:2], ex[:, :], AX.X, ALU.add)
                dve.drain()
                dve.reciprocal(col[:, 2:3], col[:, 1:2])
                dve.drain()

            dve.wait_ge(S["log"], 1)
            dve.tensor_tensor(lg[:, :], p_log[0:B, 0:NE], b_r[:, :], ALU.add)
            softmax_low(S["low"])
            dve.wait_ge(S["ex1"], 1)
            softmax_norm()
            dve.tensor_scalar(ex[:, :], ex[:, :], col[:, 2:3], None, ALU.mult).then_inc(S["rw"], 1)
            dve.drain()
            dve.wait_ge(S["load"], 1)
            dve.tensor_scalar(lg[:, :], p_load[0:B, 0:NE], float(T), None, ALU.mult)
            dve.drain()
            dve.reciprocal(lg[:, :], lg[:, :])
            dve.drain()
            dve.tensor_scalar(lg[:, :], lg[:, :], CAPACITY, 1.0, ALU.mult, ALU.min)
            dve.drain()
            dve.tensor_tensor(lg[:, :], lg[:, :], ex[:, :], ALU.mult)
            softmax_low(S["s2"])
            dve.wait_ge(S["ex2"], 1)
            softmax_norm()
            dve.tensor_scalar(ex[:, :], ex[:, :], col[:, 2:3], None, ALU.mult)
            dve.drain()
            dve.max(best[:, :], ex[:, :])
            dve.drain()
            dve.max_index(best_i[:, :], best[:, :], ex[:, :])
            dve.drain()
            dve.tensor_copy(best_f[:, :], best_i[:, :])
            dve.tensor_tensor(col[:, 3:4], best[:, 1:2], best[:, 0:1], ALU.subtract).then_inc(S["tops"], 1)
            dve.wait_ge(S["ex3"], 1)
            dve.tensor_scalar(col[:, 5:6], col[:, 4:5], 1.0, None, ALU.add)
            dve.drain()
            dve.reciprocal(col[:, 6:7], col[:, 5:6])
            dve.drain()
            dve.tensor_tensor(col[:, 7:8], col[:, 6:7], col[:, 4:5], ALU.mult)
            dve.drain()
            dve.tensor_scalar(hot[:, 0, :], iota8[:, :], best_f[:, 0:1], col[:, 6:7], ALU.is_equal, ALU.mult)
            dve.tensor_scalar(hot[:, 1, :], iota8[:, :], best_f[:, 1:2], col[:, 7:8], ALU.is_equal, ALU.mult)
            dve.drain()
            dve.tensor_tensor(wd[:, :], hot[:, 0, :], hot[:, 1, :], ALU.add).then_inc(S["wd"], 1)


def experts(nc, d):
    with Phase(nc, "moe") as m:
        ident = m.sb("ident", [128, 128])
        w1 = m.sb("w1", [128, NE, FF])
        b1 = m.sb("b1", [FF, NE])
        w2 = m.sb("w2", [FF, NE, C])
        b2 = m.sb("b2", [NE, C])
        gamma = m.sb("gamma", [H, C])
        beta = m.sb("beta", [H, C])
        ones = m.sb("ones", [NE, H])
        half_neg = m.sb("half_neg", [H, 4])
        u = [m.sb(f"u{p}", [H, 4, C]) for p in range(2)]
        h1 = [m.sb(f"h1{p}", [H, 4, C]) for p in range(2)]
        we = [m.sb(f"we{p}", [128, 2, NE]) for p in range(2)]
        we_t = [m.sb(f"we_t{p}", [NE, 2]) for p in range(2)]
        w_rep = [m.sb(f"w_rep{p}", [NE, 2, H]) for p in range(2)]
        u_z = [m.sb(f"u_z{p}", [128, 2, T]) for p in range(2)]
        hid = [m.sb(f"hid{k}", [FF, 2, T]) for k in range(4)]
        y = m.sb("y", [H, 4, C])
        sq = m.sb("sq", [H, 4, C])
        st = m.sb("st", [H, 4, 4])
        h2 = [m.sb(f"h2{p}", [H, 4, C]) for p in range(2)]
        p_t = m.ps("p_t", [128, 512])
        p_h = [m.ps(f"p_h{k}", [128, 2, 512]) for k in range(2)]
        p_y = [m.ps(f"p_y{p}", [128, 512]) for p in range(2)]
        S = {n: m.sem(n) for n in "consts ones_set ut ut_sb hid_mm gelu hid_w y_mm rep var rstd fin_used h2_done".split()}
        loaded = [m.sem(f"loaded{p}") for p in range(2)]
        stored = [m.sem(f"stored{p}") for p in range(2)]
        N = B // 2
        blk = m.block()

        @blk.sync
        def _(sp):
            for a in range(2):
                sp.dma_start(w1[64 * a:64 * a + 64, :, :], d["L0_ffn_W1"].rearrange("e c f -> c e f")).then_inc(S["consts"], 16)
            sp.dma_start(b1[:, :], d["b1_cols"]).then_inc(S["consts"], 16)
            sp.dma_start(w2[:, :, :], d["L0_ffn_W2"].rearrange("e f c -> f e c")).then_inc(S["consts"], 16)
            sp.dma_start(b2[:, :], d["L0_ffn_b2"]).then_inc(S["consts"], 16)
            sp.dma_start(gamma[:, :], on_partitions(d["L0_ffn_gamma"], H)).then_inc(S["consts"], 16)
            sp.dma_start(beta[:, :], on_partitions(d["L0_ffn_beta"], H)).then_inc(S["consts"], 16)
            sp.dma_start(ident[:, :], d["c_ident"]).then_inc(S["consts"], 16)
            with sp.Fori(0, N // 2) as i:
                for p in range(2):
                    n = i * 2 + p
                    pair = bass.ds(n * 2, 2)
                    sp.wait_ge(S["h2_done"], n + 1)
                    for t in range(2):
                        rows = slice(H * t, H * t + H)
                        sp.dma_start(u[p][:, 2 * t:2 * t + 2, :], d["u"][pair, rows, :].rearrange("a p c -> p a c")).then_inc(loaded[p], 16)
                        sp.dma_start(h1[p][:, 2 * t:2 * t + 2, :], d["h1"][pair, rows, :].rearrange("a p c -> p a c")).then_inc(loaded[p], 16)
                    sp.dma_start(we[p][:, :, :], on_partitions(d["w_route"][pair, :], 128)).then_inc(loaded[p], 16)
                    sp.dma_start(we_t[p][:, :], d["w_route"][pair, :].rearrange("a e -> e a"), allow_slow_non_contiguous=True).then_inc(loaded[p], 16)
            for p in range(2):
                sp.wait_ge(stored[p], 32 * (N // 2))

        @blk.gpsimd
        def _(pool):
            for p in range(2):
                pool.memset(u_z[p][:, :, :], 0.0).then_inc(S["ones_set"], 1)
            pool.memset(half_neg[:, :], -0.5).then_inc(S["ones_set"], 1)
            pool.memset(ones[:, :], 1.0).then_inc(S["ones_set"], 1)
            pool.wait_ge(S["ones_set"], 4)
            with pool.Fori(0, N // 2) as i:
                for p in range(2):
                    n = i * 2 + p
                    pool.wait_ge(S["var"], n + 1)
                    pool.tensor_tensor(st[:, 3, :], st[:, 2, :], half_neg[:, :], ALU.pow).then_inc(S["rstd"], 1)
                    pool.wait_ge(S["h2_done"], n + 3)
                    for t in range(2):
                        pool.dma_start(d["h2"][bass.ds(n * 2, 2), H * t:H * t + H, :].rearrange("a p c -> p a c"),
                                       h2[p][:, 2 * t:2 * t + 2, :]).then_inc(stored[p], 16)
                    pool.wait_ge(stored[p], i * 32 + 32)

        @blk.scalar
        def _(act):
            act.wait_ge(S["consts"], 16 * 8)
            act.wait_ge(S["ones_set"], 4)
            act.sem_inc(S["gelu"], 2)
            with act.Fori(0, N // 2) as i:
                for p in range(2):
                    n = i * 2 + p
                    act.wait_ge(S["ut"], n + 1)
                    for a in range(2):
                        q = slice(64 * a, 64 * a + 64)
                        ins = act.activation(u_z[p][q, a, :], p_t[q, 0:T], ACT.Copy)
                    ins.then_inc(S["ut_sb"], 1)
                    for e in range(NE):
                        act.wait_ge(S["hid_mm"], n * NE + e + 1)
                        act.wait_ge(S["y_mm"], n * NE + e + 1)
                        act.activation(hid[e % 4][:, :, :], p_h[e % 2][:, :, 0:T], ACT.Gelu,
                                       bias=b1[:, e:e + 1]).then_inc(S["gelu"], 1)

        @blk.tensor
        def _(pe):
            pe.wait_ge(S["consts"], 16 * 8)
            pe.sem_inc(S["y_mm"], 4)
            with pe.Fori(0, N // 2) as i:
                for p in range(2):
                    n = i * 2 + p
                    pe.wait_ge(loaded[p], i * 96 + 96)
                    pe.wait_ge(S["ut_sb"], n + 1)
                    for t in range(2):
                        ins = pe.transpose(p_t[:, H * t:H * t + H], u[p][:, 2 * t:2 * t + 2, :].rearrange("p a c -> p (a c)"), ident[0:H, 0:H])
                    ins.then_inc(S["ut"], 1)
                    pe.wait_ge(S["ut_sb"], n + 2)

                    def up(e):
                        pe.wait_ge(S["gelu"], n * NE + e + 1)
                        for a in range(2):
                            ins = pe.matmul(p_h[e % 2][:, a, 0:T], w1[:, e, :], u_z[p][:, a, :], start=True, stop=True)
                        ins.then_inc(S["hid_mm"], 1)

                    def down(e):
                        pe.wait_ge(S["hid_w"], n * NE + e + 1)
                        for t in range(2):
                            for a in range(2):
                                g = 2 * t + a
                                ins = pe.matmul(p_y[p][0:H, C * g:C * g + C], hid[e % 4][:, a, H * t:H * t + H], w2[:, e, :],
                                                start=False, stop=False, skip_group_check=True)
                        ins.then_inc(S["y_mm"], 1)

                    up(0)
                    up(1)
                    pe.wait_ge(S["rep"], n + 1)
                    pe.wait_ge(S["fin_used"], n + 1)
                    for t in range(2):
                        for a in range(2):
                            g = 2 * t + a
                            pe.matmul(p_y[p][0:H, C * g:C * g + C], w_rep[p][:, a, :], b2[:, :], start=(g == 0), stop=False, skip_group_check=True)
                    for e in range(NE):
                        if e + 2 < NE:
                            up(e + 2)
                        down(e)

        @blk.vector
        def _(dve):
            dve.wait_ge(S["consts"], 16 * 8)
            dve.wait_ge(S["ones_set"], 4)
            dve.sem_inc(S["h2_done"], 2)
            dve.sem_inc(S["fin_used"], 2)
            dve.sem_inc(S["ut_sb"], 1)

            def second_biases(n, p):
                dve.wait_ge(loaded[p], (n - p) // 2 * 96 + 96)
                for a in range(2):
                    ins = dve.tensor_scalar(w_rep[p][:, a, :], ones[:, :], we_t[p][:, a:a + 1], None, ALU.mult)
                ins.then_inc(S["rep"], 1)

            def weigh(n, p, e):
                dve.wait_ge(S["gelu"], n * NE + e + 3)
                for a in range(2):
                    ins = dve.tensor_scalar(hid[e % 4][:, a, :], hid[e % 4][:, a, :], we[p][:, a, e:e + 1], None, ALU.mult)
                ins.then_inc(S["hid_w"], 1)

            def residual_norm(n, p):
                dve.wait_ge(S["y_mm"], n * NE + 12)
                dve.tensor_tensor(y[:, :, :], p_y[p][0:H, 0:4 * C].rearrange("p (g c) -> p g c", g=4), u[p][:, :, :], ALU.add).then_inc(S["fin_used"], 1)
                dve.drain()
                dve.tensor_reduce(st[:, 0, :], y[:, :, :], AX.X, ALU.add)
                dve.drain()
                dve.tensor_scalar(st[:, 0, :], st[:, 0, :], 1.0 / C, None, ALU.mult)
                dve.drain()
                dve.tensor_tensor(y[:, :, :], y[:, :, :], bcast(st[:, 0, :], 2, C), ALU.subtract)
                dve.drain()
                dve.tensor_tensor(sq[:, :, :], y[:, :, :], y[:, :, :], ALU.mult)
                dve.drain()
                dve.tensor_reduce(st[:, 1, :], sq[:, :, :], AX.X, ALU.add)
                dve.drain()
                dve.tensor_scalar(st[:, 2, :], st[:, 1, :], 1.0 / C, 1e-5, ALU.mult, ALU.add).then_inc(S["var"], 1)

            def finish(n, p):
                dve.wait_ge(S["rstd"], n + 1)
                dve.tensor_tensor(y[:, :, :], y[:, :, :], bcast(st[:, 3, :], 2, C), ALU.mult)
                dve.drain()
                dve.tensor_tensor(y[:, :, :], y[:, :, :], bcast(gamma[:, :], 1, 4), ALU.mult)
                dve.drain()
                dve.tensor_tensor(y[:, :, :], y[:, :, :], bcast(beta[:, :], 1, 4), ALU.add)
                dve.drain()
                dve.tensor_tensor(h2[p][:, :, :], y[:, :, :], h1[p][:, :, :], ALU.add).then_inc(S["h2_done"], 1)

            def tick(i, p, front, back, tail):
                if front:
                    second_biases(i + 1, 1 - p)
                for e in range(NE):
                    if front:
                        weigh(i + 1, 1 - p, e)
                    if back and e == 1:
                        residual_norm(i, p)
                    if back and e == 3:
                        finish(i, p)

            in_ticks(dve, N, tick)


NR, KM = 4, 15
ROWS = NR * T
QUAD = 32 * KM
Q_LOW = H // 8
Q_HIGH = ROWS // 32 - Q_LOW
T_LOW = 8 * Q_LOW
NONE = 300.0
FILL, GONE = -3.0e38, -3.3e38


def select_constants():
    inv = 1.0 / 10000.0 ** (np.arange(0, C, 2, dtype=np.float32) / C)
    f = np.outer(np.arange(T, dtype=np.float32), inv)
    two = lambda a: np.repeat(a, 2, 1).reshape(2, H, C).transpose(1, 0, 2)
    t = np.arange(T)
    keep = (np.arange(KM)[None, :] <= t[:, None]).astype(np.float32)
    keep = np.repeat(keep[:, None, :], NR, 1).reshape(2, H, NR * KM).transpose(1, 0, 2)
    ahead = np.triu(np.ones((H, H)), 1) * FILL
    return {"c_cos": two(np.cos(f)), "c_sin": two(np.sin(f)), "c_keep": keep, "c_none": (1 - keep) * NONE,
            "c_time": t.reshape(2, H).T, "c_ahead": ahead}


def pipelined(eng, n, front, back, back_first=False):
    order = lambda i, p, more: (
        (back(i, p), more and front(i + 1, 1 - p)) if back_first else (more and front(i + 1, 1 - p), back(i, p)))
    front(0, 0)
    with eng.Fori(0, n // 2 - 1) as k:
        for p in range(2):
            order(k * 2 + p, p, True)
    order(n - 2, 0, True)
    order(n - 1, 1, False)


def select_keys(nc, d):
    with Phase(nc, "sel") as m:
        ident = m.sb("ident", [128, 128])
        ident_b = m.sb("ident_b", [H, H], BF16)
        ahead_b = m.sb("ahead_b", [H, H], BF16)
        ahead = m.sb("ahead", [H, H])
        w = m.sb("w", [C, 6, C])
        w_rot = m.sb("w_rot", [C, 6, C])
        cos = m.sb("cos", [H, 2, C])
        sin = m.sb("sin", [H, 2, C])
        keep = m.sb("keep", [H, 2, NR * KM])
        none = m.sb("none", [H, 2, NR * KM])
        time = m.sb("time", [H, 2])
        rows = [m.sb(f"rows{p}", [H, 2, C]) for p in range(2)]
        sq = m.sb("sq", [H, 2, C])
        st = m.sb("st", [H, 4, 2])
        u = m.sb("u", [H, 2, 2, C])
        pad = m.sb("pad", [H, 1])
        u_t = m.sb("u_t", [C, T])
        by_cos = m.sb("by_cos", [H, 2, 6, C])
        by_sin = m.sb("by_sin", [H, 2, 6, C])
        rope = m.sb("rope", [H, 2, 6, C])
        sq2 = m.sb("sq2", [H, 2, 5, C])
        ss = m.sb("ss", [H, 3, 2, 5])
        nrm = m.sb("nrm", [H, 2, 5, C])
        rope_t = [m.sb(f"rope_t{p}", [128, 3, T]) for p in range(2)]
        q_n = m.sb("q_n", [C, T, NR])
        part = [m.sb(f"part{p}", [H, 2, 3, C], BF16) for p in range(2)]
        rest = m.sb("rest", [H, 2, 2, C])
        vals = m.sb("vals", [H, 2, NR, 16])
        nums = m.sb("nums", [H, 2, NR, 16], U32)
        left = m.sb("left", [H, 2, NR, T])
        num_f = m.sb("num_f", [H, 2, NR, KM])
        num_k = m.sb("num_k", [H, 2, NR * KM])
        dist_f = m.sb("dist_f", [H, 2, NR * KM])
        num_o = [m.sb(f"num_o{p}", [H, 2, NR * KM], BF16) for p in range(2)]
        dist_o = [m.sb(f"dist_o{p}", [H, 2, NR * KM], BF16) for p in range(2)]
        p_t = m.ps("p_t", [128, 512])
        p_q = m.ps("p_q", [128, 512])
        p_a = m.ps("p_a", [128, 512])
        p_b = m.ps("p_b", [128, 512])
        p_low = [m.ps(f"p_low{k}", [128, 512]) for k in range(2)]
        p_high = [m.ps(f"p_high{k}", [128, 512]) for k in range(2)]
        S = {n: m.sem(n) for n in "consts w_set ready var std u_done ut ut_sb proj proj_used rope ss norm nrm rt rt_sb nt q_done q_stored part_done logit picked chosen".split()}
        rows_in = [m.sem(f"rows_in{p}") for p in range(2)]
        stored = [m.sem(f"stored{p}") for p in range(2)]
        blk = m.block()

        @blk.sync
        def _(sp):
            for dst, src in ((ident[:, :], "c_ident"), (ahead[:, :], "c_ahead"), (cos[:, :, :], "c_cos"), (sin[:, :, :], "c_sin"),
                             (keep[:, :, :], "c_keep"), (none[:, :, :], "c_none"), (time[:, :], "c_time")):
                sp.dma_start(dst, d[src]).then_inc(S["consts"], 16)
            sp.dma_start(w[:, 0:4, :], d["L1_attn_Wi"].rearrange("c (r o) -> c r o", r=NR)).then_inc(S["consts"], 16)
            for k in (4, 5):
                sp.dma_start(w[:, k, :], d["L1_attn_Wp"]).then_inc(S["consts"], 16)

            def load(n, p):
                sp.wait_ge(S["nrm"], n + 1)
                sp.dma_start(rows[p][:, :, :], d["h2"][bass.ds(n, 1), :, :].rearrange("a (t p) c -> p (a t) c", t=2)).then_inc(rows_in[p], 16)

            def back(n, p):
                one = bass.ds(n, 1)
                sp.wait_ge(S["part_done"], n + 3)
                sp.dma_start(d["key_parts"][one, :, :].rearrange("a (t p) c -> p (a t) c", t=2), part[p][:, :, :, :].rearrange("p t k c -> p t (k c)")).then_inc(stored[p], 16)
                sp.wait_ge(S["chosen"], n + 3)
                half = bass.ds((n - p) // 2, 1)
                for name, tile in (("num", num_o[p]), ("dist", dist_o[p])):
                    low, high = d[name + "_low"][p][half, :], d[name + "_high"][p][half, :]
                    row = NR * KM
                    sp.dma_start(low.rearrange("a (t k) -> (a t) k", k=row), tile[0:T_LOW, 0, :]).then_inc(stored[p], 16)
                    sp.dma_start(high[:, 0:(H - T_LOW) * row].rearrange("a (t k) -> (a t) k", k=row), tile[T_LOW:H, 0, :]).then_inc(stored[p], 16)
                    sp.dma_start(high[:, (H - T_LOW) * row:].rearrange("a (t k) -> (a t) k", k=row), tile[:, 1, :]).then_inc(stored[p], 16)

            def tick(i, p, front, ready, tail):
                if front and not ready:
                    load(0, 0)
                if not (isinstance(i, int) and i >= B - 2):
                    load(i + 2, p)
                if ready:
                    back(i, p)

            in_ticks(sp, B, tick, peeled=2)
            for p in range(2):
                sp.wait_ge(stored[p], 112 * (B // 2) + 112)
            sp.wait_ge(S["q_stored"], 16 * B + 16)

        @blk.gpsimd
        def _(pool):
            def front(n, p):
                for t in range(2):
                    pool.wait_ge(S["proj_used"], n * 2 + t + 2)
                    if t == 0:
                        pool.wait_ge(S["rt"], n + 1)
                        pool.wait_ge(S["nrm"], n + 2)
                    pool.tensor_tensor(rope[:, t, :, :], by_cos[:, t, :, :], by_sin[:, t, :, :], ALU.add).then_inc(S["rope"], 1)

            pipelined(pool, B, front, lambda n, p: None)

        @blk.scalar
        def _(act):
            act.wait_ge(S["consts"], 160)
            act.activation(ident_b[:, :], ident[0:H, 0:H], ACT.Copy).then_inc(S["w_set"], 1)
            act.activation(ahead_b[:, :], ahead[:, :], ACT.Copy).then_inc(S["w_set"], 1)
            wp = lambda a, k: a[:, :, :].rearrange("c g (o k) -> c (g o) k", k=2)[:, :, k]
            act.activation(wp(w_rot, 0), wp(w, 1), ACT.Copy, scale=-1.0).then_inc(S["w_set"], 1)
            act.activation(wp(w_rot, 1), wp(w, 0), ACT.Copy).then_inc(S["w_set"], 1)
            act.sem_inc(S["q_stored"], 16)
            act.sem_inc(S["rt_sb"], 2)
            act.sem_inc(S["ut_sb"], 1)
            act.sem_inc(S["q_done"], 1)

            def std(n):
                act.wait_ge(S["var"], n + 1)
                act.activation(st[:, 2, :], st[:, 1, :], ACT.Sqrt).then_inc(S["std"], 1)

            std(0)

            def front(n, p):
                act.wait_ge(S["ut"], n + 2)
                act.activation(u_t[:, :], p_t[0:C, 0:T], ACT.Copy).then_inc(S["ut_sb"], 1)
                act.wait_ge(S["ss"], n + 1)
                act.activation(ss[:, 1, :, :], ss[:, 0, :, :], ACT.Sqrt).then_inc(S["norm"], 1)
                if not (isinstance(n, int) and n == B - 1):
                    std(n + 1)
                act.wait_ge(S["rt"], n + 2)
                act.wait_ge(S["logit"], n + 1)
                act.activation(rope_t[p][:, 0:2, :], p_q[:, 0:2 * T].rearrange("p (g t) -> p g t", g=2), ACT.Copy)
                act.activation(rope_t[p][:, 2, :], p_t[:, 0:T], ACT.Copy).then_inc(S["rt_sb"], 1)
                act.wait_ge(S["nt"], n + 2)
                act.wait_ge(S["q_stored"], n * 16 + 16)
                for r in range(NR):
                    half, col = 64 * (r % 2), T * (r // 2)
                    ins = act.activation(q_n[:, :, r], p_a[half:half + 64, col:col + T], ACT.Copy)
                ins.then_inc(S["q_done"], 1)
                act.wait_ge(S["q_done"], n + 2)
                act.dma_start(d["q_n"][bass.ds(n, 1), :, :].rearrange("a c q -> (a c) q"), q_n[:, :, :].rearrange("c t r -> c (t r)")).then_inc(S["q_stored"], 16)

            pipelined(act, B, front, lambda n, p: None)

        @blk.tensor
        def _(pe):
            pe.wait_ge(S["w_set"], 4)
            pe.wait_ge(S["ready"], 1)
            pe.sem_inc(S["rt"], 1)
            pe.sem_inc(S["nt"], 1)
            pe.sem_inc(S["ut"], 1)
            pe.sem_inc(S["logit"], 2)

            def front(n, p):
                pe.wait_ge(S["u_done"], n + 1)
                pe.wait_ge(S["rt_sb"], n + 2)
                for t in range(2):
                    ins = pe.transpose(p_t[:, H * t:H * t + H], u[:, t, :, :].rearrange("p g c -> p (g c)"), ident[0:H, 0:H])
                ins.then_inc(S["ut"], 1)
                pe.wait_ge(S["ut_sb"], n + 2)
                for t in range(2):
                    if t == 0:
                        pe.wait_ge(S["q_done"], n + 1)
                    pe.wait_ge(S["proj_used"], n * 2 + t + 1)
                    lhs = u_t[:, H * t:H * t + H]
                    pe.matmul(p_a[0:H, 0:6 * C], lhs, w[:, :, :], start=True, stop=True)
                    pe.matmul(p_b[0:H, 0:6 * C], lhs, w_rot[:, :, :], start=True, stop=True).then_inc(S["proj"], 1)
                pe.wait_ge(S["rope"], n * 2 + 2)
                pe.wait_ge(S["rt_sb"], n + 2)
                for g in range(3):
                    for t in range(2):
                        dst = p_t[:, H * t:H * t + H] if g == 2 else p_q[:, T * g + H * t:T * g + H * t + H]
                        ins = pe.transpose(dst, rope[:, t, 2 * g:2 * g + 2, :].rearrange("p g c -> p (g c)"), ident[0:H, 0:H])
                ins.then_inc(S["rt"], 1)
                pe.wait_ge(S["rt_sb"], n + 3)
                pe.wait_ge(S["picked"], n + 1)
                for k in range(2):
                    pe.matmul(p_low[k][0:H, 0:2 * H], ident_b[:, :], bcast(ahead_b[:, :], 1, 2), start=True, stop=False, skip_group_check=True)
                    pe.matmul(p_high[k][0:H, 0:2 * T].rearrange("p (g s) -> p g s", g=2)[:, :, H:T], ident_b[:, :], bcast(ahead_b[:, :], 1, 2), start=True, stop=False, skip_group_check=True)
                for g in range(2):
                    for k in range(2):
                        q = slice(64 * k, 64 * k + 64)
                        pe.matmul(p_low[k][0:H, H * g:H * g + H], rope_t[p][q, g, 0:H], rope_t[p][q, 2, 0:H], start=False, stop=False, skip_group_check=True)
                for g in range(2):
                    for k in range(2):
                        q = slice(64 * k, 64 * k + 64)
                        ins = pe.matmul(p_high[k][0:H, T * g:T * g + T], rope_t[p][q, g, H:T], rope_t[p][q, 2, :], start=False, stop=False, skip_group_check=True)
                ins.then_inc(S["logit"], 1)
                pe.wait_ge(S["nrm"], n + 3)
                pe.wait_ge(S["proj_used"], n * 2 + 3)
                for g in range(2):
                    for t in range(2):
                        ins = pe.transpose(p_a[:, T * g + H * t:T * g + H * t + H], nrm[:, t, 2 * g:2 * g + 2, :].rearrange("p g c -> p (g c)"), ident[0:H, 0:H])
                ins.then_inc(S["nt"], 1)

            pipelined(pe, B, front, lambda n, p: None)

        @blk.vector
        def _(dve):
            dve.wait_ge(S["consts"], 160)
            dve.sem_inc(S["ready"], 1)
            dve.sem_inc(S["nrm"], 2)
            dve.sem_inc(S["proj_used"], 1)
            dve.sem_inc(S["picked"], 1)
            dve.sem_inc(S["chosen"], 2)
            dve.sem_inc(S["part_done"], 2)
            for p in range(2):
                dve.sem_inc(stored[p], 112)

            EACH = [(t, r) for t in range(2) for r in range(NR)]

            def front_1(n, p):
                x = rows[p]
                dve.wait_ge(rows_in[p], (n - p) // 2 * 16 + 16)
                dve.tensor_reduce(st[:, 0, :], x[:, :, :], AX.X, ALU.add)
                dve.drain()
                dve.tensor_scalar(st[:, 0, :], st[:, 0, :], 1.0 / C, None, ALU.mult)
                dve.drain()
                dve.tensor_tensor(x[:, :, :], x[:, :, :], bcast(st[:, 0, :], 2, C), ALU.subtract)
                dve.drain()
                dve.tensor_tensor(sq[:, :, :], x[:, :, :], x[:, :, :], ALU.mult)
                dve.drain()
                dve.tensor_reduce(st[:, 3, :], sq[:, :, :], AX.X, ALU.add)
                dve.drain()
                dve.tensor_scalar(st[:, 1, :], st[:, 3, :], 1.0 / C, 1e-5, ALU.mult, ALU.add).then_inc(S["var"], 1)
                dve.wait_ge(S["std"], n + 1)
                dve.reciprocal(st[:, 2, :], st[:, 2, :])
                dve.drain()
                dve.wait_ge(S["ut"], n + 1)
                for k in range(2):
                    ins = dve.tensor_tensor(u[:, :, k, :], x[:, :, :], bcast(st[:, 2, :], 2, C), ALU.mult)
                ins.then_inc(S["u_done"], 1)

            def front_2(n, t):
                dve.wait_ge(S["proj"], n * 2 + t + 1)
                if t == 0 and not (isinstance(n, int) and n == 0):
                    dve.wait_ge(S["rope"], n * 2)
                view = lambda a: a[0:H, 0:6 * C].rearrange("p (g c) -> p g c", c=C)
                dve.tensor_tensor(by_cos[:, t, :, :], view(p_a), bcast(cos[:, t, :], 1, 6), ALU.mult)
                dve.tensor_tensor(by_sin[:, t, :, :], view(p_b), bcast(sin[:, t, :], 1, 6), ALU.mult).then_inc(S["proj_used"], 1)

            def front_3(n):
                dve.wait_ge(S["rope"], n * 2 + 2)
                for t in range(2):
                    dve.tensor_tensor(sq2[:, t, :, :], rope[:, t, 0:5, :], rope[:, t, 0:5, :], ALU.mult)
                dve.drain()
                dve.tensor_reduce(ss[:, 0, :, :], sq2[:, :, :, :], AX.X, ALU.add).then_inc(S["ss"], 1)

            def front_4(n, p):
                dve.wait_ge(S["norm"], n + 1)
                dve.tensor_scalar(ss[:, 2, :, :], ss[:, 1, :, :], 1e-12, None, ALU.max)
                dve.drain()
                dve.reciprocal(ss[:, 2, :, :], ss[:, 2, :, :])
                dve.drain()
                dve.wait_ge(S["nt"], n + 1)
                for t in range(2):
                    ins = dve.tensor_tensor(nrm[:, t, :, :], rope[:, t, 0:5, :], bcast(ss[:, 2, t, :], 2, C), ALU.mult)
                ins.then_inc(S["nrm"], 1)
                dve.drain()
                dve.wait_ge(stored[p], (n - p) // 2 * 112 + 112)
                key = nrm[:, :, 4, :]
                hi, mid, lo = (part[p][:, :, k, :] for k in range(3))
                dve.tensor_copy(hi, key)
                dve.drain()
                dve.tensor_tensor(rest[:, 0, :, :], key, hi, ALU.subtract)
                dve.drain()
                dve.tensor_copy(mid, rest[:, 0, :, :])
                dve.drain()
                dve.tensor_tensor(rest[:, 1, :, :], rest[:, 0, :, :], mid, ALU.subtract)
                dve.drain()
                dve.tensor_copy(lo, rest[:, 1, :, :]).then_inc(S["part_done"], 1)

            def logits_of(t, r):
                k, g, width = r % 2, r // 2, (H, T)[t]
                return (p_low, p_high)[t][k][0:H, width * g:width * g + width]

            def back_1(n):
                dve.wait_ge(S["logit"], n + 3)
                dve.memset(pad[:, :], 0.0)
                for t, r in EACH:
                    dve.max(vals[:, t, r, 0:8], logits_of(t, r))
                dve.drain()

            def back_2():
                for t, r in EACH:
                    dve.max_index(nums[:, t, r, 0:8], vals[:, t, r, 0:8], logits_of(t, r))
                    ins = dve.match_replace(left[:, t, r, 0:(H, T)[t]], vals[:, t, r, 0:8], logits_of(t, r), GONE)
                ins.then_inc(S["picked"], 1)
                dve.drain()

            def back_3():
                for t, r in EACH:
                    dve.max(vals[:, t, r, 8:16], left[:, t, r, 0:(H, T)[t]])
                dve.drain()

            def back_4(n, p):
                for t, r in EACH:
                    dve.max_index(nums[:, t, r, 8:16], vals[:, t, r, 8:16], left[:, t, r, 0:(H, T)[t]])
                dve.drain()
                for t in range(2):
                    dve.tensor_copy(num_f[:, t, :, :], nums[:, t, :, 0:KM])
                dve.drain()
                dve.wait_ge(stored[p], (n - p) // 2 * 112 + 112)
                f = num_f[:, :, :, :].rearrange("p t r k -> p t (r k)")
                dve.tensor_tensor(num_k[:, :, :], f, keep[:, :, :], ALU.mult)
                for t in range(2):
                    dve.tensor_scalar(dist_f[:, t, :], f[:, t, :], time[:, t:t + 1], 0.0, ALU.subtract, ALU.min)
                dve.drain()
                dve.tensor_tensor(num_o[p][:, :, :], num_k[:, :, :], none[:, :, :], ALU.add)
                dve.tensor_tensor(dist_o[p][:, :, :], dist_f[:, :, :], keep[:, :, :], ALU.mult).then_inc(S["chosen"], 1)

            def tick(i, p, front, back, tail):
                if front and not back:
                    front_1(0, 0)
                if back:
                    back_1(i)
                if front:
                    front_2(i + 1, 0)
                if back:
                    back_2()
                if front:
                    front_2(i + 1, 1)
                if front:
                    front_3(i + 1)
                if not (isinstance(i, int) and i >= B - 2):
                    front_1(i + 2, p)
                if back:
                    back_3()
                if front:
                    front_4(i + 1, 1 - p)
                if back:
                    back_4(i, p)

            in_ticks(dve, B, tick, peeled=2)


GRP = 8
TOKG = GRP * KM
DUO = 4
TOKD = DUO * KM
SLOT = KM + 1
STEPS = {"low": (B // 2 * Q_LOW, Q_LOW, 1), "high": (B // 2 * Q_HIGH, Q_HIGH, 2)}
ACT_SCALE = float(np.pi / np.sqrt(3.0))


def relation_constants():
    r = np.arange(128)[:, None] % (DUO * SLOT) // SLOT
    c = np.arange(TOKD)[None, :] // KM
    return {"c_own": (r == c).astype(np.float32), "c_half": (np.arange(128)[:, None] // 64 == np.arange(2)).astype(np.float32), "c_keynum": np.stack([np.arange(H), np.arange(H) + H], 1)}


def skewed(eng, n, stages):
    deep = max(lag for lag, _ in stages)
    start = deep + deep % 2
    stop = start + (n - start) // 2 * 2

    def tick(i, p, whole):
        for lag, run in stages:
            if whole or 0 <= i - lag < n:
                run(i - lag, (p - lag) % 2)

    for i in range(start):
        tick(i, i % 2, False)
    with eng.Fori(0, (stop - start) // 2) as k:
        for p in range(2):
            tick(k * 2 + (start + p), p, True)
    for i in range(stop, n + deep):
        tick(i, i % 2, False)


def relations(nc, d, tag):
    n_steps, per_pair, tiles = STEPS[tag]
    with Phase(nc, "rel_" + tag) as m:
        ident = m.sb("ident", [128, 128])
        own = m.sb("own", [128, TOKD])
        keynum = m.sb("keynum", [H, 2])
        w1 = m.sb("w1", [128, 2, C])
        w1_d = m.sb("w1_d", [1, C])
        w1_x = m.sb("w1_x", [1, C])
        w1_dp = m.sb("w1_dp", [1, 3, C], BF16)
        w1_d6 = m.sb("w1_d6", [6, 2, C], BF16)
        b1 = m.sb("b1", [128, 1])
        b1_s = m.sb("b1_s", [128, 1])
        w2 = m.sb("w2", [C, C])
        w2_t = m.sb("w2_t", [C, C])
        w_cm = m.sb("w_cm", [C, 3])
        w_out = m.sb("w_out", [128, 6])
        half = m.sb("half", [128, 2])
        parts = [m.sb(f"parts{p}", [H, 2, tiles, 3, C], BF16) for p in range(2)]
        num = [m.sb(f"num{p}", [H, 2, QUAD], BF16) for p in range(2)]
        dist = [m.sb(f"dist{p}", [6, QUAD], BF16) for p in range(2)]
        q_n = [m.sb(f"q_n{p}", [128, 32]) for p in range(2)]
        hot = [m.sb(f"hot{p}", [H, tiles, 2, QUAD], BF16) for p in range(2)]
        sel = [m.sb(f"sel{p}", [128, 32, KM]) for p in range(2)]
        two = [m.sb(f"two{p}", [128, 32 // DUO, 2, DUO, SLOT]) for p in range(2)]
        gram = [m.sb(f"gram{p}", [128, QUAD]) for p in range(2)]
        hid = [m.sb(f"hid{p}", [128, QUAD]) for p in range(2)]
        out = [m.sb(f"out{p}", [6, QUAD]) for p in range(2)]
        p_sel = [m.ps(f"p_sel{p}", [128, 512]) for p in range(2)]
        p_gram = [m.ps(f"p_gram{p}", [128, 512]) for p in range(2)]
        p_hid = [m.ps(f"p_hid{p}", [128, 512]) for p in range(2)]
        p_out = [m.ps(f"p_out{p}", [128, 512]) for p in range(2)]
        p_w = p_out[0]
        S = {n: m.sem(n) for n in "consts zero wd wd_in w2t w2t_sb wout wout_sb hot gath sel_sb query gr mask clip hid_mm silu out_mm out_sb".split()}
        loaded = [m.sem(f"loaded{p}") for p in range(2)]
        query_in = [m.sem(f"query_in{p}") for p in range(2)]
        dist_in = [m.sem(f"dist_in{p}") for p in range(2)]
        stored = [m.sem(f"stored{p}") for p in range(2)]
        per_load = 16 * 2
        blk = m.block()

        @blk.sync
        def _(sp):
            sp.dma_start(ident[:, :], d["c_ident"]).then_inc(S["consts"], 16)
            sp.dma_start(own[:, :], d["c_own"]).then_inc(S["consts"], 16)
            sp.dma_start(half[:, :], d["c_half"]).then_inc(S["consts"], 16)
            sp.dma_start(keynum[:, :], d["c_keynum"]).then_inc(S["consts"], 16)
            sp.wait_ge(S["zero"], 5)
            for g in range(2 * DUO):
                sp.dma_start(w1[SLOT * g:SLOT * g + SLOT, g // DUO, :], d["L1_attn_W1"][0:SLOT, :]).then_inc(S["consts"], 16)
            sp.dma_start(w1_x[:, :], d["L1_attn_W1"][SLOT:SLOT + 1, :]).then_inc(S["consts"], 16)
            for a in range(2):
                sp.dma_start(b1[64 * a:64 * a + 64, :], d["L1_attn_b1"].rearrange("(p a) -> p a", a=1)).then_inc(S["consts"], 16)
            sp.dma_start(w2[:, :], d["L1_attn_W2"]).then_inc(S["consts"], 16)
            sp.dma_start(w_cm[:, 0:2], d["L1_attn_Wc"]).then_inc(S["consts"], 16)
            sp.dma_start(w_cm[:, 2:3], d["L1_attn_Wm"], allow_slow_non_contiguous=True).then_inc(S["consts"], 16)
            sp.wait_ge(S["wd"], 1)
            for a in range(2):
                for k in range(3):
                    sp.dma_start(w1_d6[3 * a + k:3 * a + k + 1, a, :], w1_dp[:, k, :]).then_inc(S["wd_in"], 16)

            def of_step(what, s):
                return d[what + tag].rearrange("a b (q c) -> a (b q) c", c=QUAD)[:, bass.ds(s, 1), :].rearrange("a s c -> a (s c)")

            def load(s, p):
                pair = s // per_pair
                sp.wait_ge(S["hot"], s + 1)
                sp.wait_ge(S["gath"], s + 1)
                rows = H * tiles
                sp.dma_start(parts[p][:, :, :, :, :].rearrange("p a t k c -> p a t (k c)"),
                             d["key_parts"][bass.ds(pair * 2, 2), 0:rows, :].rearrange("a (t p) c -> p a t c", t=tiles)).then_inc(loaded[p], 16)
                sp.dma_start(num[p][:, :, :], on_partitions(of_step("num_", s), H)).then_inc(loaded[p], 16)

            def load_queries(s, p):
                pair, quad = s // per_pair, s % per_pair
                sp.wait_ge(S["query"], s + 1)
                first = quad * 32 + (0 if tag == "low" else 32 * Q_LOW)
                sp.dma_start(q_n[p][:, :], d["q_n"][bass.ds(pair * 2, 2), :, bass.ds(first, 32)].rearrange("a c q -> (a c) q")).then_inc(query_in[p], 16)

            def load_dist(s, p):
                sp.wait_ge(S["hid_mm"], s + 1)
                for a in range(2):
                    sp.dma_start(dist[p][3 * a:3 * a + 3, :], on_partitions(of_step("dist_", s)[a], 3)).then_inc(dist_in[p], 16)

            skewed(sp, n_steps, [(0, load), (1, load_queries), (2, load_dist)])
            for p in range(2):
                sp.wait_ge(stored[p], 16 * ((n_steps - p + 1) // 2) + 16)

        @blk.gpsimd
        def _(pool):
            for t in (w_out[:, :], w1[:, :, :], w1_d6[:, :, :], two[0][:, :, :, :, :], two[1][:, :, :, :, :]):
                pool.memset(t, 0.0).then_inc(S["zero"], 1)
            pool.wait_ge(S["zero"], 5)
            pool.wait_ge(S["consts"], 16 * 18)
            pool.sem_inc(S["query"], 2)
            pool.sem_inc(S["clip"], 2)

            def masked(s, p):
                pool.wait_ge(S["mask"], s + 3)

            def query(s, p):
                pool.wait_ge(query_in[p], (s - p) // 2 * 16 + 16)
                pool.wait_ge(S["gr"], s + 1)
                pool.tensor_tensor(two[p][:, :, :, :, KM], bcast(q_n[p][:, :].rearrange("p (g q) -> p g q", q=DUO), 2, 2),
                                   bcast(bcast(half[:, :], 1, 32 // DUO), 3, DUO), ALU.mult).then_inc(S["query"], 1)

            def clip(s, p):
                pool.tensor_scalar(gram[p][:, :], gram[p][:, :], -1.0, None, ALU.max).then_inc(S["clip"], 1)

            skewed(pool, n_steps, [(2, masked), (1, query), (2, clip)])

        @blk.scalar
        def _(act):
            act.wait_ge(S["consts"], 16 * 18)
            act.activation(b1_s[:, :], b1[:, :], ACT.Copy, scale=ACT_SCALE)
            act.wait_ge(S["w2t"], 1)
            act.activation(w2_t[:, :], p_w[0:C, 0:C], ACT.Copy).then_inc(S["w2t_sb"], 1)
            act.wait_ge(S["zero"], 5)
            act.wait_ge(S["wout"], 1)
            for a in range(2):
                q = slice(64 * a, 64 * a + 64)
                act.activation(w_out[q, 3 * a:3 * a + 3], p_w[q, 64:67], ACT.Copy, scale=1.0 / ACT_SCALE).then_inc(S["wout_sb"], 1)
            act.drain()
            act.sem_inc(S["sel_sb"], 2)
            act.sem_inc(S["silu"], 2)

            def copy_sel(s, p):
                act.wait_ge(S["gath"], s + 3)
                act.wait_ge(S["gr"], s + 1)
                for a in range(2):
                    q = slice(64 * a, 64 * a + 64)
                    act.activation(two[p][q, :, a, :, 0:KM], p_sel[p][q, 0:QUAD].rearrange("p (g q k) -> p g q k", q=DUO, k=KM), ACT.Copy)
                act.activation(sel[p][:, :, :], p_sel[p][:, 0:QUAD].rearrange("p (q k) -> p q k", k=KM), ACT.Copy).then_inc(S["sel_sb"], 1)

            def silu(s, p):
                act.wait_ge(S["hid_mm"], s + 3)
                act.wait_ge(S["out_mm"], s + 1)
                act.activation(hid[p][:, :], p_hid[p][:, 0:QUAD], ACT.Silu, scale=ACT_SCALE, bias=b1_s[:, 0:1]).then_inc(S["silu"], 1)

            def store(s, p):
                act.wait_ge(S["out_sb"], s + 2)
                act.dma_start(d["heads_" + tag][bass.ds(s, 1), :, :, :].rearrange("a g c t -> (a c) g t"), out[p][:, :].rearrange("c (g t) -> c g t", t=TOKG)).then_inc(stored[p], 16)

            skewed(act, n_steps, [(1, copy_sel), (3, silu), (5, store)])

        @blk.tensor
        def _(pe):
            pe.wait_ge(S["consts"], 16 * 18)
            pe.transpose(p_w[0:C, 0:C], w2[:, :], ident[0:C, 0:C]).then_inc(S["w2t"], 1)
            pe.wait_ge(S["w2t_sb"], 1)
            for a in range(2):
                ins = pe.matmul(p_w[64 * a:64 * a + 64, 64:67], w2_t[:, :], w_cm[:, :], start=True, stop=True)
            ins.then_inc(S["wout"], 1)
            pe.wait_ge(S["wout_sb"], 2)
            pe.wait_ge(S["wd_in"], 96)
            pe.sem_inc(S["gath"], 2)
            pe.sem_inc(S["gr"], 2)
            pe.sem_inc(S["hid_mm"], 2)
            pe.sem_inc(S["out_mm"], 2)

            def gather(s, p):
                pe.wait_ge(S["hot"], s + 3)
                last = 3 * tiles - 1
                for k in range(3):
                    for t in range(tiles):
                        for a in range(2):
                            ins = pe.matmul(p_sel[p][64 * a:64 * a + 64, 0:QUAD], parts[p][:, a, t, k, :], hot[p][:, t, a, :],
                                            start=(k == 0 and t == 0), stop=(k * tiles + t == last))
                ins.then_inc(S["gath"], 1)

            def grams(s, p):
                pe.wait_ge(S["sel_sb"], s + 3)
                pe.wait_ge(S["query"], s + 3)
                for g in range(32 // DUO):
                    ins = pe.matmul(p_gram[p][:, TOKD * g:TOKD * g + TOKD], two[p][:, g, :, :, :].rearrange("p a q k -> p (a q k)"),
                                    sel[p][:, DUO * g:DUO * g + DUO, :].rearrange("p q k -> p (q k)"), start=True, stop=True)
                ins.then_inc(S["gr"], 1)

            def first_layer(s, p):
                pe.wait_ge(S["clip"], s + 3)
                pe.wait_ge(dist_in[p], (s - p) // 2 * 32 + 32)
                pe.matmul(p_hid[p][:, 0:QUAD], w1_d6[:, :, :].rearrange("p a c -> p (a c)"), dist[p][:, :], start=True, stop=False)
                pe.matmul(p_hid[p][:, 0:QUAD], w1[:, :, :].rearrange("p a c -> p (a c)"), gram[p][:, :], start=False, stop=True).then_inc(S["hid_mm"], 1)

            def heads(s, p):
                pe.wait_ge(S["silu"], s + 3)
                if isinstance(s, int):
                    pe.wait_ge(S["out_sb"], max(s, 1))
                pe.matmul(p_out[p][0:6, 0:QUAD], w_out[:, :], hid[p][:, :], start=True, stop=True).then_inc(S["out_mm"], 1)

            skewed(pe, n_steps, [(1, gather), (2, grams), (3, first_layer), (4, heads)])

        @blk.vector
        def _(dve):
            dve.wait_ge(S["consts"], 16 * 18)
            dve.tensor_scalar(w1_d[:, :], w1_x[:, :], 1.0 / -T, None, ALU.mult)
            dve.drain()
            dve.tensor_copy(w1_dp[:, 0, :], w1_d[:, :])
            for k in (1, 2):
                dve.drain()
                dve.tensor_tensor(w1_d[:, :], w1_d[:, :], w1_dp[:, k - 1, :], ALU.subtract)
                dve.drain()
                ins = dve.tensor_copy(w1_dp[:, k, :], w1_d[:, :])
            ins.then_inc(S["wd"], 1)
            dve.sem_inc(S["hot"], 2)
            dve.sem_inc(S["out_sb"], 1)
            dve.sem_inc(S["mask"], 2)
            for p in range(2):
                dve.sem_inc(stored[p], 16)

            def one_hot(s, p):
                dve.wait_ge(loaded[p], (s - p) // 2 * per_load + per_load)
                dve.wait_ge(S["gath"], s + 1)
                for t in range(tiles):
                    ins = dve.tensor_scalar(hot[p][:, t, :, :], num[p][:, :, :], keynum[:, t:t + 1], None, ALU.is_equal)
                ins.then_inc(S["hot"], 1)

            def mask(s, p):
                dve.wait_ge(S["gr"], s + 3)
                dve.wait_ge(S["hid_mm"], s + 1)
                dve.scalar_tensor_tensor(out=gram[p][:, :].rearrange("p (g c) -> p g c", c=TOKD), in0=p_gram[p][:, 0:QUAD].rearrange("p (g c) -> p g c", c=TOKD),
                                         scalar=1.0, in1=bcast(own[:, :], 1, 32 // DUO), op0=ALU.min, op1=ALU.mult).then_inc(S["mask"], 1)

            def copy_out(s, p):
                dve.wait_ge(S["out_mm"], s + 3)
                dve.wait_ge(stored[p], (s - p) // 2 * 16 + 16)
                dve.tensor_copy(out[p][:, :], p_out[p][0:6, 0:QUAD]).then_inc(S["out_sb"], 1)

            skewed(dve, n_steps, [(0, one_hot), (2, mask), (4, copy_out)])


NG = T // 2
GRID = 16
CK = 31
WIDE = 6
NCK = NG // CK


def sample_constants():
    p = np.arange(TOKG)
    own = (p[:, None] // KM == np.arange(GRP)[None, :]).astype(np.float32)
    g = np.arange(NG)[:, None]
    r = np.arange(TOKG)[None, :]
    shut = np.where(r % KM <= 2 * g + r // KM // NR, 0.0, -1e30)
    return {"c_row": own, "c_shut": shut, "c_cells": np.repeat(-np.arange(GRID)[None, :], TOKG, 0)}


def sample(nc, d):
    with Phase(nc, "smp") as m:
        ident = m.sb("ident", [128, 128])
        row = m.sb("row", [TOKG, GRP])
        shut = m.sb("shut", [NG, TOKG])
        cells = m.sb("cells", [TOKG, GRID])
        ones = m.sb("ones", [C, NG])
        b2 = m.sb("b2", [C, 1])
        b2_rep = m.sb("b2_rep", [C, NG])
        w_cm = m.sb("w_cm", [C, 3])
        b_cm = m.sb("b_cm", [NG, 3])
        b_all = m.sb("b_all", [NG, 3])
        wo = m.sb("wo", [C, NR, C])
        pal = m.sb("pal", [C, NR, NR, GRID, GRID])
        pal_w = m.sb("pal_w", [128, GRID, 128])
        heads = [m.sb(f"heads{p}", [NG, 2, 3, TOKG]) for p in range(2)]
        h2 = [m.sb(f"h2{p}", [NG, 2, 128]) for p in range(2)]
        z = m.sb("z", [NG, 2, 2, TOKG])
        pos = m.sb("pos", [NG, 2, 2, TOKG])
        low = m.sb("low", [NG, 2, GRP, KM])
        red = m.sb("red", [NG, 3, 2, GRP])
        exps = m.sb("exps", [NG, 2, GRP, KM])
        wn = m.sb("wn", [NG, 2, GRP, KM])
        w = m.sb("w", [TOKG, 2, NG])
        far = m.sb("far", [TOKG, 2, NG, GRID])
        hat_y = m.sb("hat_y", [TOKG, 2, NG, GRID])
        hat_x = [m.sb(f"hat_x{p}", [TOKG, 2, NG, GRID]) for p in range(2)]
        wy = [m.sb(f"wy{p}", [TOKG, 2, NG, GRID]) for p in range(2)]
        own = [m.sb(f"own{k}", [TOKG, CK, GRP, GRID]) for k in range(2)]
        cell = m.sb("cell", [128, GRID, 2, NG])
        y_t = m.sb("y_t", [128, 2 * NG])
        p_pos = m.ps("p_pos", [128, 512])
        p_wt = m.ps("p_wt", [128, 512])
        p_cell = [m.ps(f"p_cell{k}", [128, 512]) for k in range(4)]
        p_y = m.ps("p_y", [128, 512])
        p_r = m.ps("p_r", [128, 512])
        S = {n: m.sem(n) for n in "consts zero ones_set rep bias palw palw_sb b_done tanh low exps wn pos pos_t w_t w_sb hats wy own cells_mm cell_sb y_mm y_sb y_r h3".split()}
        heads_in = [m.sem(f"heads_in{p}") for p in range(2)]
        h2_in = [m.sem(f"h2_in{p}") for p in range(2)]
        stored = [m.sem(f"stored{p}") for p in range(2)]
        N, NC = B // 2, 2 * NCK
        blk = m.block()

        @blk.sync
        def _(sp):
            sp.wait_ge(S["zero"], 2)
            for dst, src in ((ident[:, :], d["c_ident"]), (row[:, :], d["c_row"]), (shut[:, :], d["c_shut"]), (cells[:, :], d["c_cells"]),
                             (b2[:, :], d["L1_attn_b2"].rearrange("(p a) -> p a", a=1)), (w_cm[:, 0:2], d["L1_attn_Wc"]),
                             (b_cm[:, 0:2], on_partitions(d["L1_attn_bc"], NG)), (b_cm[:, 2:3], on_partitions(d["L1_attn_bm"], NG)),
                             (wo[:, :, :], d["L1_attn_Wo"].rearrange("r c o -> c r o"))):
                sp.dma_start(dst, src).then_inc(S["consts"], 16)
            sp.dma_start(w_cm[:, 2:3], d["L1_attn_Wm"], allow_slow_non_contiguous=True).then_inc(S["consts"], 16)
            for r in range(NR):
                sp.dma_start(pal[:, r, r, :, :], d["L1_attn_palette"]).then_inc(S["consts"], 16)

            def load_heads(n, p):
                sp.wait_ge(S["tanh"], n + 1)
                sp.wait_ge(S["low"], n + 1)
                for tag, steps, first in (("low", Q_LOW, 0), ("high", Q_HIGH, 4 * Q_LOW)):
                    sp.dma_start(heads[p][first:first + 4 * steps, :, :, :].rearrange("p a c t -> p (a c t)"),
                                 d["heads_" + tag][bass.ds(n * steps, steps), :, :, :].rearrange("s g c t -> (s g) (c t)")).then_inc(heads_in[p], 16)

            def load_h2(n, p):
                sp.dma_start(h2[p][:, :, :], d["h2"][bass.ds(n * 2, 2), :, :].rearrange("a (g t) c -> g a (t c)", t=2)).then_inc(h2_in[p], 16)

            def tick(i, p, front, back, tail):
                q = 1 - p
                if not back and front:
                    load_heads(0, 0)
                    for n in range(2):
                        load_h2(n, n)
                at_end = isinstance(i, int) and i >= N - 2
                if not at_end:
                    load_heads(i + 2, p)
                if tail:
                    sp.wait_ge(S["h3"], i + 1)
                    sp.dma_start(d["h3"][bass.ds(i * 2 - 2, 2), :, :].rearrange("a (g t) c -> g a (t c)", t=2), h2[q][:, :, :]).then_inc(stored[q], 16)
                    sp.wait_ge(stored[q], (i - 1 - q) // 2 * 16 + 16)
                    if front:
                        load_h2(i + 1, q)

            in_ticks(sp, N, tick, peeled=2)

        @blk.gpsimd
        def _(pool):
            pool.memset(pal[:, :, :, :, :], 0.0).then_inc(S["zero"], 1)
            pool.memset(pal_w[:, :, :], 0.0).then_inc(S["zero"], 1)
            pool.memset(ones[:, :], 1.0).then_inc(S["ones_set"], 1)

        @blk.scalar
        def _(act):
            act.wait_ge(S["palw"], 1)
            for a in range(2):
                for k in range(2):
                    q = slice(64 * a, 64 * a + 64)
                    act.activation(pal_w[q, 8 * k:8 * k + 8, 64 * a:64 * a + 64], p_cell[k][q, :].rearrange("p (x c) -> p x c", c=C),
                                   ACT.Copy, scale=1.0 / NR).then_inc(S["palw_sb"], 1)
            act.wait_ge(S["b_done"], 1)
            act.sem_inc(S["tanh"], 2)
            act.sem_inc(S["exps"], 1)
            act.sem_inc(S["hats"], 1)
            act.sem_inc(S["cell_sb"], 4)

            def tanh(n, p):
                act.wait_ge(heads_in[p], (n - p) // 2 * 32 + 32)
                act.wait_ge(S["pos"], n + 1)
                for c in range(2):
                    ins = act.activation(z[:, :, c, :], heads[p][:, :, c, :], ACT.Tanh, bias=b_all[:, c:c + 1])
                ins.then_inc(S["tanh"], 1)

            def exps_of(n):
                act.wait_ge(S["low"], n + 3)
                act.wait_ge(S["wn"], n + 1)
                act.activation(exps[:, :, :, :], low[:, :, :, :], ACT.Exp).then_inc(S["exps"], 1)

            def distances(c, first, last):
                at = p_pos[0:TOKG, 0:4 * NG].rearrange("p (a c g) -> p a c g", a=2, c=2)[:, :, c, :]
                for x in range(first, last):
                    act.activation(far[:, :, :, x], at, ACT.Abs, bias=cells[:, x:x + 1])

            def hat(n, p, c):
                act.drain()
                if c == 1:
                    act.wait_ge(S["wy"], n + 1)
                    act.activation(hat_y[:, :, :, :], far[:, :, :, :], ACT.Relu, scale=-1.0, bias=1.0)
                    act.drain()
                else:
                    act.wait_ge(S["cells_mm"], NC * n + 8)
                    act.activation(hat_x[p][:, :, :, :], far[:, :, :, :], ACT.Relu, scale=-1.0, bias=1.0).then_inc(S["hats"], 1)
                    act.drain()

            def copy_cells(n, k):
                act.wait_ge(S["cells_mm"], NC * n + k + 17)
                if k == 0:
                    act.wait_ge(S["y_mm"], n + 1)
                a, c = k // NCK, k % NCK
                act.activation(cell[:, :, a, CK * c:CK * c + CK], p_cell[k % 4][:, 0:CK * GRID].rearrange("p (g x) -> p x g", x=GRID), ACT.Copy).then_inc(S["cell_sb"], 1)

            def tick(i, p, front, back, tail):
                n, q = i + 1, 1 - p
                for k in range(NC):
                    if front and k == 0:
                        tanh(n, q)
                        exps_of(n)
                    if back:
                        copy_cells(i, k)
                    if front and k == 2:
                        act.wait_ge(S["pos_t"], n + 2)
                        distances(1, 0, GRID)
                    if front and k == 3:
                        hat(n, q, 1)
                    if front and k == 4:
                        distances(0, 0, GRID)
                    if front and k == 5:
                        hat(n, q, 0)

            in_ticks(act, N, tick)

        @blk.tensor
        def _(pe):
            pe.wait_ge(S["consts"], 16 * 14)
            for k in range(2):
                for a in range(2):
                    for x in range(8):
                        for r in range(NR):
                            ins = pe.matmul(p_cell[k][64 * a:64 * a + 64, C * x:C * x + C], pal[:, r, :, :, 8 * k + x].rearrange("p r y -> p (r y)"), wo[:, r, :],
                                            start=(r == 0), stop=(r == NR - 1))
            ins.then_inc(S["palw"], 1)
            pe.wait_ge(S["rep"], 1)
            pe.matmul(p_r[0:NG, 0:3], b2_rep[:, :], w_cm[:, :], start=True, stop=True).then_inc(S["bias"], 1)
            pe.wait_ge(S["palw_sb"], 4)
            pe.sem_inc(S["pos_t"], 1)
            pe.sem_inc(S["w_t"], 1)
            pe.sem_inc(S["cells_mm"], 16)
            pe.sem_inc(S["y_mm"], 1)
            pe.sem_inc(S["y_r"], 1)

            def cell_sums(n, p, k):
                a, c = k // NCK, k % NCK
                pe.wait_ge(S["own"], NC * n + k + 1)
                pe.wait_ge(S["cell_sb"], NC * n + k + 1)
                for g in reversed(range(CK)):
                    f = max(0, g + 1 - WIDE)
                    ins = pe.matmul(p_cell[k % 4][:, GRID * f:GRID * g + GRID], own[k % 2][:, g, :, :].rearrange("p r y -> p (r y)"),
                                    hat_x[p][:, a, CK * c + f:CK * c + g + 1, :].rearrange("p g x -> p (g x)"), start=True, stop=True)
                ins.then_inc(S["cells_mm"], 1)

            def products(n):
                pe.wait_ge(S["cell_sb"], NC * n + NC + 4)
                pe.wait_ge(S["y_sb"], n + 1)
                for x in range(GRID):
                    ins = pe.matmul(p_y[:, 0:2 * NG], pal_w[:, x, :], cell[:, x, :, :].rearrange("p a g -> p (a g)"), start=(x == 0), stop=(x == GRID - 1))
                ins.then_inc(S["y_mm"], 1)

            def turned(n):
                pe.wait_ge(S["pos"], n + 2)
                pe.wait_ge(S["hats"], n + 1)
                for a in range(2):
                    for c in range(2):
                        ins = pe.transpose(p_pos[0:TOKG, NG * (2 * a + c):NG * (2 * a + c) + NG], pos[:, a, c, :], ident[0:NG, 0:NG])
                ins.then_inc(S["pos_t"], 1)
                pe.wait_ge(S["wn"], n + 2)
                pe.wait_ge(S["w_sb"], n + 1)
                for a in range(2):
                    ins = pe.transpose(p_wt[0:TOKG, NG * a:NG * a + NG], wn[:, a, :, :].rearrange("p r k -> p (r k)"), ident[0:NG, 0:NG])
                ins.then_inc(S["w_t"], 1)

            def rows_of(n):
                pe.wait_ge(S["y_sb"], n + 2)
                pe.wait_ge(S["h3"], n + 1)
                for a in range(2):
                    ins = pe.transpose(p_r[0:NG, 128 * a:128 * a + 128], y_t[:, NG * a:NG * a + NG], ident[:, :])
                ins.then_inc(S["y_r"], 1)

            def tick(i, p, front, back, tail):
                for k in range(NC):
                    if back:
                        cell_sums(i, p, k)
                    if tail and k == 0:
                        products(i - 1)
                    if front and k == 1:
                        turned(i + 1)
                    if tail and k == 3:
                        rows_of(i - 1)

            in_ticks(pe, N, tick)

        @blk.vector
        def _(dve):
            dve.wait_ge(S["consts"], 16 * 14)
            dve.wait_ge(S["ones_set"], 1)
            dve.tensor_scalar(b2_rep[:, :], ones[:, :], b2[:, 0:1], None, ALU.mult).then_inc(S["rep"], 1)
            dve.wait_ge(S["bias"], 1)
            dve.tensor_tensor(b_all[:, :], p_r[0:NG, 0:3], b_cm[:, :], ALU.add).then_inc(S["b_done"], 1)
            dve.drain()
            dve.sem_inc(S["low"], 2)
            for name in ("pos", "wn", "w_sb", "wy", "y_sb", "h3"):
                dve.sem_inc(S[name], 1)

            flat = lambda t: t[:, :, :, :].rearrange("p a r k -> p (a r) k")
            g16 = lambda t: t[:, :, :, :].rearrange("p a g y -> p (a g) y")
            reds = lambda k: red[:, k, :, :].rearrange("p a r -> p (a r)")

            def logits(n, p):
                dve.wait_ge(heads_in[p], (n - p) // 2 * 32 + 32)
                dve.wait_ge(S["exps"], n + 1)
                dve.scalar_tensor_tensor(out=low[:, :, :, :].rearrange("p a r k -> p a (r k)"), in0=heads[p][:, :, 2, :], scalar=b_all[:, 2:3],
                                         in1=bcast(shut[:, :], 1, 2), op0=ALU.add, op1=ALU.add)
                dve.drain()
                dve.tensor_reduce(reds(0), flat(low), AX.X, ALU.max)
                dve.drain()
                dve.tensor_tensor(flat(low), flat(low), bcast(reds(0), 2, KM), ALU.subtract).then_inc(S["low"], 1)

            def positions(n):
                dve.wait_ge(S["tanh"], n + 3)
                dve.wait_ge(S["pos_t"], n + 1)
                dve.tensor_scalar(pos[:, :, :, :], z[:, :, :, :], 1.0, 0.5 * (GRID - 1), ALU.add, ALU.mult)
                dve.drain()
                dve.tensor_scalar(pos[:, :, :, :], pos[:, :, :, :], 0.0, float(GRID - 1), ALU.max, ALU.min).then_inc(S["pos"], 1)

            def weights(n):
                dve.wait_ge(S["exps"], n + 2)
                dve.tensor_reduce(reds(1), flat(exps), AX.X, ALU.add)
                dve.drain()
                dve.reciprocal(red[:, 2, :, :], red[:, 1, :, :])
                dve.drain()
                dve.wait_ge(S["w_t"], n + 1)
                dve.tensor_tensor(flat(wn), flat(exps), bcast(reds(2), 2, KM), ALU.mult).then_inc(S["wn"], 1)

            def weighted(n, p):
                dve.wait_ge(S["w_t"], n + 2)
                dve.tensor_copy(w[:, :, :], p_wt[0:TOKG, 0:2 * NG].rearrange("p (a g) -> p a g", a=2)).then_inc(S["w_sb"], 1)
                dve.drain()
                dve.wait_ge(S["hats"], n + 2)
                dve.tensor_tensor(g16(wy[p]), g16(hat_y), bcast(w[:, :, :].rearrange("p a g -> p (a g)"), 2, GRID), ALU.mult).then_inc(S["wy"], 1)
                dve.drain()

            def own_rows(n, p, k):
                a, c = k // NCK, k % NCK
                dve.wait_ge(S["cells_mm"], NC * n + k + 15)
                for r in range(GRP):
                    ins = dve.tensor_scalar(own[k % 2][:, :, r, :], wy[p][:, a, CK * c:CK * c + CK, :], row[:, r:r + 1], None, ALU.mult)
                ins.then_inc(S["own"], 1)

            def copy_y(n):
                dve.wait_ge(S["y_mm"], n + 2)
                dve.wait_ge(S["y_r"], n + 1)
                dve.tensor_copy(y_t[:, :], p_y[:, 0:2 * NG]).then_inc(S["y_sb"], 1)

            def add_h2(n, p):
                dve.wait_ge(S["y_r"], n + 2)
                dve.wait_ge(h2_in[p], (n - p) // 2 * 16 + 16)
                dve.tensor_tensor(h2[p][:, :, :], p_r[0:NG, 0:256].rearrange("p (a c) -> p a c", a=2), h2[p][:, :, :], ALU.add).then_inc(S["h3"], 1)

            def tick(i, p, front, back, tail):
                n, q = i + 1, 1 - p
                for k in range(NC):
                    if back:
                        own_rows(i, p, k)
                    if front and k == 0:
                        logits(n, q)
                        positions(n)
                    if front and k == 1:
                        weights(n)
                    if tail and k == 2:
                        copy_y(i - 1)
                    if tail and k == 4:
                        add_h2(i - 1, q)
                    if front and k == 7:
                        weighted(n, q)

            in_ticks(dve, N, tick)


NH, NX, DH = 4, 4, 16
FAR = -1.0e30


def ffn_constants():
    minus = np.zeros((128, 1))
    minus[::32] = -1.0
    return {"c_ahead30": np.triu(np.ones((H, H)), 1) * FAR, "c_behind30": np.tril(np.ones((H, H)), -1) * FAR, "c_minus": minus}


def normed(dve, x, sq, mean, ssum, var, width, eps, then):
    dve.tensor_reduce(mean, x, AX.X, ALU.add)
    dve.drain()
    dve.tensor_scalar(mean, mean, 1.0 / width, None, ALU.mult)
    dve.drain()
    dve.tensor_tensor(x, x, bcast(mean, 2, width), ALU.subtract)
    dve.drain()
    dve.tensor_tensor(sq, x, x, ALU.mult)
    dve.drain()
    dve.tensor_reduce(ssum, sq, AX.X, ALU.add)
    dve.drain()
    dve.tensor_scalar(var, ssum, 1.0 / width, eps, ALU.mult, ALU.add).then_inc(then, 1)


def head_residual(nc, d):
    with Phase(nc, "hres") as m:
        ident = m.sb("ident", [128, 128])
        b_h = m.sb("b_h", [H, C])
        rows = m.sb("rows", [H, 2, NH, C])
        sq = m.sb("sq", [H, 2, NH, C])
        st = m.sb("st", [H, 5, 2 * NH])
        u_t = m.sb("u_t", [128, 2, T])
        res = m.sb("res", [H, 2, C])
        p_t = m.ps("p_t", [128, 512])
        p_s = [m.ps(f"p_s{a}", [128, 512]) for a in range(2)]
        S = {n: m.sem(n) for n in "rows_in consts var std u_done ut ut_sb s_mm done out".split()}
        w2 = m.sb("w2", [128, C])
        blk = m.block()

        @blk.sync
        def _(sp):
            for b in range(NH):
                sp.dma_start(rows[:, :, b, :], d["h3"][b, :, :].rearrange("(t p) c -> p t c", t=2)).then_inc(S["rows_in"], 16)
            for a in range(2):
                sp.dma_start(w2[64 * a:64 * a + 64, :], d["hl_w_t"]).then_inc(S["consts"], 16)
            sp.dma_start(b_h[:, :], on_partitions(d["L1_ffn_hl_b"].rearrange("n d -> (n d)"), H)).then_inc(S["consts"], 16)
            sp.dma_start(ident[:, :], d["c_ident"]).then_inc(S["consts"], 16)
            sp.wait_ge(S["done"], 4)
            sp.dma_start(d["resid"].rearrange("(t p) c -> p t c", t=2), res[:, :, :]).then_inc(S["out"], 16)
            sp.wait_ge(S["out"], 16)

        @blk.scalar
        def _(act):
            act.wait_ge(S["var"], 1)
            act.activation(st[:, 3, :], st[:, 2, :], ACT.Sqrt).then_inc(S["std"], 1)
            for b in range(0, NH, 2):
                act.wait_ge(S["ut"], 2)
                act.activation(u_t[:, b // 2, :], p_t[:, 248 * (b // 2):248 * (b // 2) + T], ACT.Copy).then_inc(S["ut_sb"], 1)

        @blk.tensor
        def _(pe):
            pe.wait_ge(S["consts"], 64)
            pe.wait_ge(S["u_done"], 1)
            for k in range(2):
                for t in range(2):
                    ins = pe.transpose(p_t[:, T * k + H * t:T * k + H * t + H], rows[:, t, 2 * k:2 * k + 2, :].rearrange("p b c -> p (b c)"), ident[0:H, 0:H])
                ins.then_inc(S["ut"], 1)
            pe.wait_ge(S["ut_sb"], 2)
            for b in range(NH):
                q = slice(64 * (b % 2), 64 * (b % 2) + 64)
                for t in range(2):
                    ins = pe.matmul(p_s[b % 2][0:H, 128 * (b // 2) + 64 * t:128 * (b // 2) + 64 * t + 64], u_t[q, b // 2, H * t:H * t + H], w2[q, :], start=True, stop=True)
            ins.then_inc(S["s_mm"], 1)

        @blk.vector
        def _(dve):
            dve.wait_ge(S["rows_in"], 64)
            x = rows[:, :, :, :].rearrange("p t b c -> p (t b) c")
            normed(dve, x, sq[:, :, :, :].rearrange("p t b c -> p (t b) c"), st[:, 0, :], st[:, 1, :], st[:, 2, :], C, 1e-5, S["var"])
            dve.wait_ge(S["std"], 1)
            dve.reciprocal(st[:, 4, :], st[:, 3, :])
            dve.drain()
            dve.tensor_tensor(x, x, bcast(st[:, 4, :], 2, C), ALU.mult).then_inc(S["u_done"], 1)
            dve.wait_ge(S["s_mm"], 1)
            for b in range(NH):
                at = 128 * (b // 2)
                dve.tensor_tensor(res[:, :, DH * b:DH * b + DH], p_s[b % 2][0:H, at:at + 128].rearrange("p (t c) -> p t c", t=2)[:, :, DH * b:DH * b + DH],
                                  bcast(b_h[:, DH * b:DH * b + DH], 1, 2), ALU.add).then_inc(S["done"], 1)


def head_mixture(nc, d):
    with Phase(nc, "mix") as m:
        ident = m.sb("ident", [128, 128])
        ident_b = m.sb("ident_b", [H, H], BF16)
        tri = m.sb("tri", [H, 2, H])
        ahead_b = m.sb("ahead_b", [H, H], BF16)
        behind_b = m.sb("behind_b", [H, H], BF16)
        w_h = m.sb("w_h", [C, 128])
        b_h = m.sb("b_h", [H, C])
        b_hc = m.sb("b_hc", [C, 1])
        w_q = m.sb("w_q", [C, NX, 128])
        w_k = m.sb("w_k", [C, 128])
        w_v = m.sb("w_v", [C, C])
        minus = m.sb("minus", [128, 1])
        w_g = m.sb("w_g", [128, 2, 2, NX])
        b_g = m.sb("b_g", [H, NH * NX])
        w_1 = m.sb("w_1", [128, 128])
        w_2 = m.sb("w_2", [128, 128])
        b_1 = m.sb("b_1", [128, 1])
        b_2 = m.sb("b_2", [H, DH])
        ln_g, ln_b, fn_g, fn_b = (m.sb(n, [H, DH]) for n in ("ln_g", "ln_b", "fn_g", "fn_b"))
        w_f = m.sb("w_f", [128, 2, NH])
        resid = m.sb("resid", [H, 2, C])
        half_neg = m.sb("half_neg", [H, 8])
        rows = [m.sb(f"rows{p}", [H, 2, C]) for p in range(2)]
        kept = [m.sb(f"kept{p}", [H, 2, C]) for p in range(2)]
        sq = m.sb("sq", [H, 2, C])
        st = m.sb("st", [H, 4, 2])
        u = m.sb("u", [H, 2, 2, C])
        u_t = m.sb("u_t", [C, T])
        sx_t = m.sb("sx_t", [C, T])
        sx = m.sb("sx", [H, 2, C])
        full = [m.sb(f"full{p}", [H, 2, C]) for p in range(2)]
        q_t = m.sb("q_t", [128, NX, T])
        q_m = [m.sb(f"q_m{p}", [128, NX, T]) for p in range(2)]
        k_z = [m.sb(f"k_z{p}", [128, NH, T]) for p in range(2)]
        v_1 = [m.sb(f"v_1{p}", [H, 2, NH, 32]) for p in range(2)]
        tops = m.sb("tops", [H, 2, NX, 128])
        e_0 = [m.sb(f"e_0{k}", [H, NX, T]) for k in range(2)]
        e_1 = [m.sb(f"e_1{k}", [H, NX, H]) for k in range(2)]
        o_t = m.sb("o_t", [128, NX, T])
        den = m.sb("den", [H, 2, NH, NX])
        qkv = m.sb("qkv", [H, 2, 16, DH])
        qkv_p = m.sb("qkv_p", [H, 2, 16, DH])
        qkv_t = m.sb("qkv_t", [128, 4, H])
        gate = m.sb("gate", [H, 2 * NH, NX])
        gate_e = m.sb("gate_e", [H, 2 * NH, NX])
        red = m.sb("red", [H, 4, 2 * NH])
        prod = m.sb("prod", [H, 2, NH, NX, DH])
        fx = m.sb("fx", [H, 2 * NH, DH])
        sq16 = m.sb("sq16", [H, 2 * NH, DH])
        vs = m.sb("vs", [H, 6, 2 * NH])
        fx_t = m.sb("fx_t", [128, H])
        hx_t = m.sb("hx_t", [128, H])
        hm_t = m.sb("hm_t", [128, H])
        hx = m.sb("hx", [H, 2 * NH, DH])
        fo = m.sb("fo", [H, 2 * NH, DH])
        fo_t = m.sb("fo_t", [128, H])
        fg = m.sb("fg", [H, 2, NH])
        fg_e = m.sb("fg_e", [H, 2, NH])
        fr = m.sb("fr", [H, 3, 2])
        res = [m.sb(f"res{p}", [H, 2, C]) for p in range(2)]
        p_f = m.ps("p_f", [128, 512])
        p_b = m.ps("p_b", [128, 512])
        ring = [m.ps(f"ring{k}", [128, 512]) for k in range(4)]
        p_av = [m.ps(f"p_av{t}", [128, 512]) for t in range(2)]
        S = {n: m.sem(n) for n in ("zero consts cast ready var rstd u_done fmm fev sx_read max_mm q_used s_used key_mm st_used "
                                   "av ot av_t av_used masked bmm bact bdve var1 rstd1 fo_done done").split()}
        loaded = [m.sem(f"loaded{p}") for p in range(2)]
        kept_in = [m.sem(f"kept_in{p}") for p in range(2)]
        stored = [m.sem(f"stored{p}") for p in range(2)]
        NCONST = 32
        bank = lambda k, n: ring[k % 4][0:n, 0:496]
        e2 = lambda ap: ap.rearrange("p (e s) -> p e s", e=2)
        blk = m.block()

        @blk.sync
        def _(sp):
            sp.wait_ge(S["zero"], 11)
            col = lambda v: v.rearrange("(p a) -> p a", a=1)
            loads = [(ident[:, :], d["c_ident"]), (tri[:, 0, :], d["c_ahead30"]), (tri[:, 1, :], d["c_behind30"]), (minus[:, :], d["c_minus"]),
                     (w_h[:, 0:C], d["hl_w_t"]), (b_h[:, :], on_partitions(d["L1_ffn_hl_b"].rearrange("n d -> (n d)"), H)),
                     (b_hc[:, :], col(d["L1_ffn_hl_b"].rearrange("n d -> (n d)"))),
                     (b_g[:, :], on_partitions(d["L1_ffn_gate_b"].rearrange("n e -> (n e)"), H)), (b_2[:, :], on_partitions(d["L1_ffn_fc2_b"], H)),
                     (w_f[0:C, 0, :], d["fgate_t"]), (w_f[C:128, 1, :], d["fgate_t"]), (resid[:, :, :], d["resid"].rearrange("(t p) c -> p t c", t=2))]
            loads += [(t[:, :], on_partitions(d["L1_ffn_" + n], H)) for t, n in ((ln_g, "ln_g"), (ln_b, "ln_b"), (fn_g, "fnorm_g"), (fn_b, "fnorm_b"))]
            for n in range(NH):
                q = slice(DH * n, DH * n + DH)
                loads += [(w_q[q, :, 32 * n + 1:32 * n + 1 + DH], d["wq_t"][n]), (w_k[q, 32 * n + 1:32 * n + 1 + DH], d["wk_t"][n]),
                          (w_v[q, q], d["wv_t"][n]), (w_g[64 * (n % 2):64 * (n % 2) + 64, n // 2, n % 2, :], d["gate_t"][n])]
            assert len(loads) == NCONST
            for dst, src in loads:
                sp.dma_start(dst, src).then_inc(S["consts"], 16)
            for n in range(2 * NH):
                q = slice(DH * n, DH * n + DH)
                for dst, src in ((w_1[q, q], d["fc1_t"]), (w_2[q, q], d["fc2_t"]), (b_1[q, :], col(d["L1_ffn_fc1_b"]))):
                    sp.dma_start(dst, src).then_inc(S["consts"], 16)

            def load(tile, n, done):
                sp.dma_start(tile[:, :, :], d["h3"][bass.ds(n, 1), :, :].rearrange("a (t p) c -> p (a t) c", t=2)).then_inc(done, 16)

            def tick(i, p, front, back, tail):
                q = 1 - p
                if not back and front:
                    load(rows[0], 0, loaded[0])
                    for n in range(2):
                        load(kept[n], n, kept_in[n])
                if not (isinstance(i, int) and i >= B - 2):
                    if back:
                        sp.wait_ge(S["u_done"], i + 1)
                    load(rows[p], i + 2, loaded[p])
                if tail:
                    sp.wait_ge(S["done"], i + 2)
                    sp.dma_start(d["out"][bass.ds(i - 1, 1), :, :].rearrange("a (t p) c -> p (a t) c", t=2), res[q][:, :, :]).then_inc(stored[q], 16)
                    if front:
                        load(kept[q], i + 1, kept_in[q])

            in_ticks(sp, B, tick, peeled=2)
            for p in range(2):
                sp.wait_ge(stored[p], 16 * (B // 2) + 16)

        ALL = 16 * (NCONST + 3 * 2 * NH)

        @blk.gpsimd
        def _(pool):
            for t in (w_h[:, :], w_f[:, :, :], w_q[:, :, :], w_k[:, :], w_v[:, :], w_g[:, :, :, :], w_1[:, :], w_2[:, :], tops[:, :, :, :], k_z[0][:, :, :], k_z[1][:, :, :]):
                pool.memset(t, 0.0).then_inc(S["zero"], 1)
            pool.memset(half_neg[:, :], -0.5).then_inc(S["ready"], 1)
            for p in range(2):
                pool.memset(v_1[p][:, :, :, DH:DH + 1], 1.0).then_inc(S["ready"], 1)
                pool.memset(v_1[p][:, :, :, DH + 1:32], 0.0).then_inc(S["ready"], 1)
            pool.wait_ge(S["ready"], 5)
            pool.sem_inc(S["masked"], 1)

            def rstd(n):
                pool.wait_ge(S["var"], n + 1)
                pool.tensor_tensor(st[:, 3, :], st[:, 2, :], half_neg[:, 0:2], ALU.pow).then_inc(S["rstd"], 1)

            def masked(n, p):
                pool.wait_ge(S["av_used"], 2 * n + 4)
                pool.wait_ge(S["bmm"], 7 * n + 3)
                for t in range(2):
                    ins = pool.tensor_tensor(qkv_p[:, t, :, :].rearrange("p (n e) d -> p n e d", n=NH), qkv[:, t, :, :].rearrange("p (n e) d -> p n e d", n=NH),
                                             bcast(full[p][:, t, :].rearrange("p (n d) -> p n d", n=NH), 2, NX), ALU.mult)
                ins.then_inc(S["masked"], 1)

            def rstd1(n, k):
                pool.wait_ge(S["var1"], 2 * n + k + 1)
                pool.tensor_tensor(vs[:, 3, :], vs[:, 2, :], half_neg[:, :], ALU.pow).then_inc(S["rstd1"], 1)

            def tick(i, p, front, back, tail):
                if front and not back:
                    rstd(0)
                if not (isinstance(i, int) and i >= B - 2):
                    rstd(i + 2)
                if tail:
                    for k in range(2):
                        rstd1(i - 1, k)
                if back:
                    masked(i, p)

            in_ticks(pool, B, tick, peeled=2)

        @blk.scalar
        def _(act):
            act.wait_ge(S["consts"], ALL)
            act.activation(ident_b[:, :], ident[0:H, 0:H], ACT.Copy).then_inc(S["cast"], 1)
            act.activation(ahead_b[:, :], tri[:, 0, :], ACT.Copy).then_inc(S["cast"], 1)
            act.activation(behind_b[:, :], tri[:, 1, :], ACT.Copy).then_inc(S["cast"], 1)
            act.wait_ge(S["ready"], 5)
            act.sem_inc(S["st_used"], 24)
            act.sem_inc(S["fev"], 1)

            def front_of(n, p):
                def copy(k, dst, src, **kw):
                    act.wait_ge(S["fmm"], 4 * n + k + 1)
                    return act.activation(dst, src, ACT.Identity if "bias" in kw else ACT.Copy, **kw)
                copy(0, u_t[:, :], p_f[0:C, 0:T]).then_inc(S["fev"], 1)
                copy(1, sx_t[:, :], p_f[0:C, 256:256 + T], bias=b_hc[:, 0:1]).then_inc(S["fev"], 1)
                act.wait_ge(S["key_mm"], 12 * n + 12)
                act.wait_ge(S["av"], 4 * n + 4)
                for h in range(NH):
                    q = slice(32 * h, 32 * h + 32)
                    copy(3, k_z[p][q, h, :], p_f[q, 0:T], bias=minus[q, 0:1])
                copy(3, v_1[p][:, :, :, 0:DH], p_f[0:H, 256:384].rearrange("p (t n o) -> p t n o", t=2, n=NH)).then_inc(S["fev"], 1)
                for k in range(2):
                    act.wait_ge(S["max_mm"], 16 * n + k + 1)
                    act.activation(q_t[:, 2 * k:2 * k + 2, :], e2(bank(k, 128)), ACT.Copy).then_inc(S["q_used"], 1)

            def exps(n, h):
                act.wait_ge(S["av"], 4 * n + h + 7)
                for k in range(3):
                    v = 3 * h + k
                    act.wait_ge(S["key_mm"], 12 * n + v + 25)
                    if k < 2:
                        dst, src = e_0[h % 2][:, 2 * k:2 * k + 2, :], e2(bank(v, H))
                    else:
                        dst, src = e_1[h % 2][:, :, :], bank(v, H).rearrange("p (e s) -> p e s", e=4)
                    act.activation(dst, src, ACT.Exp, scale=float(DH) ** 0.5).then_inc(S["st_used"], 1)

            def tail_of(n, k):
                if k == 0:
                    act.wait_ge(S["bmm"], 7 * n + 8)
                    act.activation(qkv_t[:, :, :], p_b[:, 0:4 * H].rearrange("p (g s) -> p g s", g=4), ACT.Copy).then_inc(S["bact"], 1)
                elif k == 1:
                    act.wait_ge(S["bdve"], 4 * n + 1)
                    act.activation(gate_e[:, :, :], gate[:, :, :], ACT.Exp).then_inc(S["bact"], 1)
                elif k == 2:
                    act.wait_ge(S["bmm"], 7 * n + 10)
                    act.activation(fx_t[:, :], p_b[:, 0:H], ACT.Copy).then_inc(S["bact"], 1)
                elif k == 3:
                    act.wait_ge(S["bmm"], 7 * n + 13)
                    act.activation(fo_t[:, :], p_b[:, 0:H], ACT.Copy).then_inc(S["bact"], 1)
                else:
                    act.wait_ge(S["bdve"], 4 * n + 4)
                    act.activation(fg_e[:, :, :], fg[:, :, :], ACT.Exp).then_inc(S["bact"], 1)

            def tick(i, p, front, back, tail):
                if front:
                    front_of(i + 1, 1 - p)
                for k in range(2):
                    if tail:
                        tail_of(i - 1, k)
                for h in range(NH):
                    if back:
                        exps(i, h)
                    if tail and h % 2:
                        tail_of(i - 1, 2 + h // 2)
                if back:
                    act.wait_ge(S["av"], 4 * i + 12)
                    for k in range(2):
                        ins = act.activation(o_t[:, 2 * k:2 * k + 2, :], e2(p_av[k][:, 0:2 * T]), ACT.Copy)
                    ins.then_inc(S["ot"], 1)
                if tail:
                    tail_of(i - 1, 4)

            in_ticks(act, B, tick)

        @blk.tensor
        def _(pe):
            pe.wait_ge(S["cast"], 3)
            pe.wait_ge(S["ready"], 5)
            pe.sem_inc(S["key_mm"], 24)
            pe.sem_inc(S["av"], 8)
            pe.sem_inc(S["bmm"], 7)

            def turn(n, v):
                if v < 4:
                    pe.wait_ge(S["st_used"], 12 * n + 9 + v)
                    pe.wait_ge(S["s_used"], 14 * n + 14)
                elif v < 6:
                    pe.wait_ge(S["q_used"], 2 * n + v - 3)
                else:
                    pe.wait_ge(S["s_used"], 14 * n + 14 + v - 5)

            def head_of(n, p):
                pe.wait_ge(S["u_done"], n + 1)
                pe.wait_ge(S["fev"], 3 * n + 1)
                pe.wait_ge(S["sx_read"], n + 1)
                for t in range(2):
                    ins = pe.transpose(p_f[:, H * t:H * t + H], u[:, t, :, :].rearrange("p g c -> p (g c)"), ident[0:H, 0:H])
                ins.then_inc(S["fmm"], 1)
                pe.wait_ge(S["fev"], 3 * n + 2)
                pe.matmul(p_f[:, 256:256 + T], w_h[:, :], u_t[:, :], start=True, stop=True).then_inc(S["fmm"], 1)
                pe.wait_ge(S["fev"], 3 * n + 3)
                pe.matmul(p_f[:, 0:T], w_k[:, :], sx_t[:, :], start=True, stop=True).then_inc(S["fmm"], 1)
                for t in range(2):
                    pe.matmul(p_f[0:H, 256 + 64 * t:320 + 64 * t], sx_t[:, H * t:H * t + H], w_v[:, :], start=True, stop=True)
                for t in range(2):
                    ins = pe.matmul(p_f[0:H, 384 + 64 * t:448 + 64 * t], u_t[:, H * t:H * t + H], w_h[:, 0:C], start=True, stop=True)
                ins.then_inc(S["fmm"], 1)

                for k in range(2):
                    turn(n, k)
                    for e in range(2):
                        ins = pe.matmul(bank(k, 128)[:, T * e:T * e + T], w_q[:, 2 * k + e, :], sx_t[:, :], start=True, stop=True)
                    ins.then_inc(S["max_mm"], 1)
                pe.wait_ge(S["q_used"], 2 * n + 2)
                pe.wait_ge(S["fev"], 3 * n + 4)

            def scores_by_query(n, p, h):
                for k in range(3):
                    v = 2 + 3 * h + k
                    turn(n, v)
                    dst = bank(v, H)
                    if k == 0:
                        dst = dst.rearrange("p (e s) -> p e s", e=4)
                        pe.matmul(dst, ident_b[:, :], bcast(ahead_b[:, :], 1, 4), start=True, stop=False, skip_group_check=True)
                        for e in range(4):
                            ins = pe.matmul(dst[:, e, :], q_t[:, e, 0:H], k_z[p][:, h, 0:H], start=False, stop=False, skip_group_check=True)
                    else:
                        dst = e2(dst)
                        pe.matmul(dst[:, :, H:T], ident_b[:, :], bcast(ahead_b[:, :], 1, 2), start=True, stop=False, skip_group_check=True)
                        for e in range(2):
                            ins = pe.matmul(dst[:, e, :], q_t[:, 2 * (k - 1) + e, H:T], k_z[p][:, h, :], start=False, stop=False, skip_group_check=True)
                    ins.then_inc(S["max_mm"], 1)

            def tops_turned(n):
                for k in range(2):
                    turn(n, 14 + k)
                    pe.wait_ge(S["s_used"], 14 * n + 26)
                    for e in range(2):
                        for t in range(2):
                            ins = pe.matmul(bank(14 + k, 128)[:, T * e + H * t:T * e + H * t + H], tops[:, t, 2 * k + e, :], ident[0:H, 0:H], start=True, stop=True)
                    ins.then_inc(S["max_mm"], 1)

            def scores(n, p, h, front):
                for k in range(3):
                    v = 3 * h + k
                    if v < 4:
                        pe.wait_ge(S["st_used"], 12 * n + 21 + v)
                        if front:
                            pe.wait_ge(S["s_used"], 14 * n + 14 + 14 + 11 + v)
                    else:
                        pe.wait_ge(S["st_used"], 12 * n + 21 + v)
                    dst = bank(v, H)
                    if k < 2:
                        dst = e2(dst)
                        pe.matmul(dst[:, :, 0:H], ident_b[:, :], bcast(behind_b[:, :], 1, 2), start=True, stop=False, skip_group_check=True)
                        ins = pe.matmul(dst, k_z[p][:, h, 0:H], q_m[p][:, 2 * k:2 * k + 2, :], start=False, stop=False, skip_group_check=True)
                    else:
                        dst = dst.rearrange("p (e s) -> p e s", e=4)
                        pe.matmul(dst, ident_b[:, :], bcast(behind_b[:, :], 1, 4), start=True, stop=False, skip_group_check=True)
                        ins = pe.matmul(dst, k_z[p][:, h, H:T], q_m[p][:, :, H:T], start=False, stop=False, skip_group_check=True)
                    ins.then_inc(S["key_mm"], 1)

            def values(n, p, h):
                pe.wait_ge(S["st_used"], 12 * n + 24 + 3 * h + 3)
                if h == 0:
                    pe.wait_ge(S["av_used"], 2 * n + 2)
                for k in range(2):
                    dst = p_av[k][32 * h:32 * h + 32, 0:2 * T]
                    pe.matmul(dst, v_1[p][:, 0, h, :], e_0[h % 2][:, 2 * k:2 * k + 2, :].rearrange("p e s -> p (e s)"), start=True, stop=False)
                    ins = pe.matmul(e2(dst)[:, :, H:T], v_1[p][:, 1, h, :], e_1[h % 2][:, 2 * k:2 * k + 2, :], start=False, stop=True)
                ins.then_inc(S["av"], 1)

            def values_turned(n):
                pe.wait_ge(S["ot"], n + 1)
                for t in range(2):
                    for e in range(NX):
                        ins = pe.transpose(p_av[t][0:H, 128 * e:128 * e + 128], o_t[:, e, H * t:H * t + H], ident[:, :])
                ins.then_inc(S["av_t"], 1)

            def tail_of(n, k):
                if k == 0:
                    pe.wait_ge(S["masked"], n + 2)
                    pe.wait_ge(S["done"], n + 2)
                    for g in range(4):
                        ins = pe.transpose(p_b[:, H * g:H * g + H], qkv_p[:, g // 2, 8 * (g % 2):8 * (g % 2) + 8, :].rearrange("p e d -> p (e d)"), ident[0:H, 0:H])
                    ins.then_inc(S["bmm"], 1)
                elif k == 1:
                    pe.wait_ge(S["bact"], 5 * n + 1)
                    for g in range(4):
                        ins = pe.matmul(p_b[0:H, 8 * g:8 * g + 8], qkv_t[:, g, :], w_g[:, g % 2, :, :].rearrange("p a e -> p (a e)"), start=True, stop=True)
                    ins.then_inc(S["bmm"], 1)
                elif k == 2:
                    pe.wait_ge(S["bdve"], 4 * n + 2)
                    pe.transpose(p_b[:, 0:H], fx[:, :, :].rearrange("p n d -> p (n d)"), ident[0:H, 0:H]).then_inc(S["bmm"], 1)
                elif k == 3:
                    pe.wait_ge(S["bact"], 5 * n + 3)
                    pe.matmul(p_b[:, 256:256 + H], w_1[:, :], fx_t[:, :], start=True, stop=True).then_inc(S["bmm"], 1)
                elif k == 4:
                    pe.wait_ge(S["bdve"], 4 * n + 3)
                    pe.matmul(p_b[0:H, 0:128], hm_t[:, :], w_2[:, :], start=True, stop=True).then_inc(S["bmm"], 1)
                elif k == 5:
                    pe.wait_ge(S["rstd1"], 2 * n + 2)
                    pe.wait_ge(S["fo_done"], n + 1)
                    pe.transpose(p_b[:, 0:H], fo[:, :, :].rearrange("p n d -> p (n d)"), ident[0:H, 0:H]).then_inc(S["bmm"], 1)
                elif k == 6:
                    pe.wait_ge(S["bact"], 5 * n + 4)
                    pe.matmul(p_b[0:H, 256:264], fo_t[:, :], w_f[:, :, :].rearrange("p t h -> p (t h)"), start=True, stop=True).then_inc(S["bmm"], 1)

            def tick(i, p, front, back, tail):
                def step(k):
                    if tail:
                        tail_of(i - 1, k)

                if front:
                    head_of(i + 1, 1 - p)
                step(0)
                for h in range(NH):
                    if front:
                        scores_by_query(i + 1, 1 - p, h)
                    if h == 1:
                        step(1)
                if front:
                    tops_turned(i + 1)
                if back:
                    pe.wait_ge(S["s_used"], 14 * i + 28)
                    scores(i, p, 0, front)
                for h in range(NH):
                    if back and h + 1 < NH:
                        scores(i, p, h + 1, front)
                    if h == 1:
                        step(3)
                    if back:
                        values(i, p, h)
                    if h < 2:
                        step(2 + 2 * h)
                    if h == NH - 2:
                        step(5)
                step(6)
                if back:
                    values_turned(i)

            in_ticks(pe, B, tick)

        @blk.vector
        def _(dve):
            dve.wait_ge(S["consts"], ALL)
            dve.wait_ge(S["ready"], 5)
            dve.sem_inc(S["s_used"], 14)
            dve.sem_inc(S["sx_read"], 1)
            dve.sem_inc(S["av_used"], 2)
            dve.sem_inc(S["done"], 2)
            for p in range(2):
                dve.sem_inc(stored[p], 16)

            def layer_norm(n, p):
                x = rows[p]
                dve.wait_ge(loaded[p], (n - p) // 2 * 16 + 16)
                normed(dve, x[:, :, :], sq[:, :, :], st[:, 0, :], st[:, 1, :], st[:, 2, :], C, 1e-5, S["var"])
                dve.wait_ge(S["rstd"], n + 1)
                for k in range(2):
                    ins = dve.tensor_tensor(u[:, :, k, :], x[:, :, :], bcast(st[:, 3, :], 2, C), ALU.mult)
                ins.then_inc(S["u_done"], 1)

            def head_of(n, p):
                dve.wait_ge(S["fev"], 3 * n + 4)
                dve.wait_ge(S["masked"], n)
                dve.tensor_tensor(sx[:, :, :], p_f[0:H, 384:512].rearrange("p (t c) -> p t c", t=2), bcast(b_h[:, :], 1, 2), ALU.add).then_inc(S["sx_read"], 1)
                dve.drain()
                dve.tensor_scalar(full[p][:, :, :], sx[:, :, :], 0.0, None, ALU.not_equal)

            def maxima(n, h):
                for k in range(3):
                    v = 2 + 3 * h + k
                    dve.wait_ge(S["max_mm"], 16 * n + v + 1)
                    if k == 0:
                        ins = dve.tensor_reduce(tops[:, 0, :, 32 * h], bank(v, H).rearrange("p (e s) -> p e s", e=4), AX.X, ALU.max)
                    else:
                        ins = dve.tensor_reduce(tops[:, 1, 2 * (k - 1):2 * k, 32 * h], e2(bank(v, H)), AX.X, ALU.max)
                    ins.then_inc(S["s_used"], 1)

            def with_tops(n, p):
                for k in range(2):
                    dve.wait_ge(S["max_mm"], 16 * n + 15 + k)
                    dve.wait_ge(S["key_mm"], 12 * n + 12)
                    dve.tensor_tensor(q_m[p][:, 2 * k:2 * k + 2, :], e2(bank(14 + k, 128)), q_t[:, 2 * k:2 * k + 2, :], ALU.add).then_inc(S["s_used"], 1)

            def normed_values(n):
                dve.wait_ge(S["av_t"], n + 1)
                for t in range(2):
                    o = p_av[t][0:H, :].rearrange("p (e n d) -> p n e d", e=NX, n=NH)
                    dve.reciprocal(den[:, t, :, :], o[:, :, :, DH])
                    dve.drain()
                    if t == 0:
                        dve.wait_ge(S["masked"], n + 1)
                    dve.tensor_tensor(qkv[:, t, :, :].rearrange("p (n e) d -> p n e d", n=NH), o[:, :, :, 0:DH], bcast(den[:, t, :, :], 3, DH), ALU.mult).then_inc(S["av_used"], 1)

            def norm16(n, y, k, gain, shift, out, done):
                normed(dve, y, sq16[:, :, :], vs[:, 0, :], vs[:, 1, :], vs[:, 2, :], DH, 1e-8, S["var1"])
                dve.wait_ge(S["rstd1"], 2 * n + k + 1)
                dve.tensor_tensor(y, y, bcast(vs[:, 3, :], 2, DH), ALU.mult)
                dve.drain()
                dve.tensor_tensor(y, y, bcast(gain[:, :], 1, 2 * NH), ALU.mult)
                dve.drain()
                dve.tensor_tensor(out, y, bcast(shift[:, :], 1, 2 * NH), ALU.add).then_inc(done, 1)

            def tail_of(n, p, k):
                x = fx[:, :, :]
                if k == 0:
                    dve.wait_ge(S["bmm"], 7 * n + 9)
                    dve.tensor_tensor(gate[:, :, :].rearrange("p (t n) e -> p t (n e)", t=2), p_b[0:H, 0:32].rearrange("p (t g) -> p t g", t=2), bcast(b_g[:, :], 1, 2), ALU.add)
                    dve.drain()
                    dve.tensor_reduce(red[:, 0, :], gate[:, :, :], AX.X, ALU.max)
                    dve.drain()
                    dve.tensor_tensor(gate[:, :, :], gate[:, :, :], bcast(red[:, 0, :], 2, NX), ALU.subtract).then_inc(S["bdve"], 1)
                elif k == 1:
                    dve.wait_ge(S["bact"], 5 * n + 2)
                    dve.tensor_reduce(red[:, 1, :], gate_e[:, :, :], AX.X, ALU.add)
                    dve.drain()
                    dve.reciprocal(red[:, 2, :], red[:, 1, :])
                    dve.drain()
                    dve.tensor_tensor(gate[:, :, :], gate_e[:, :, :], bcast(red[:, 2, :], 2, NX), ALU.mult)
                    dve.drain()
                    g32 = prod[:, :, :, :, :].rearrange("p t n e d -> p (t n e) d")
                    dve.tensor_tensor(g32, qkv_p[:, :, :, :].rearrange("p t g d -> p (t g) d"), bcast(gate[:, :, :].rearrange("p g e -> p (g e)"), 2, DH), ALU.mult)
                    dve.drain()
                    dve.tensor_reduce(fx[:, :, :], prod[:, :, :, :, :].rearrange("p t n e d -> p (t n) d e"), AX.X, ALU.add)
                    dve.drain()
                    dve.tensor_tensor(x, x, resid[:, :, :].rearrange("p t (n d) -> p (t n) d", n=NH), ALU.add)
                    dve.drain()
                elif k == 2:
                    norm16(n, x, 0, ln_g, ln_b, x, S["bdve"])
                elif k == 3:
                    dve.wait_ge(S["bmm"], 7 * n + 11)
                    dve.tensor_scalar(hx_t[:, :], p_b[:, 256:256 + H], b_1[:, 0:1], 0.0, ALU.add, ALU.max)
                    dve.drain()
                    dve.scalar_tensor_tensor(out=hm_t[:, :], in0=fx_t[:, :], scalar=0.0, in1=hx_t[:, :], op0=ALU.not_equal, op1=ALU.mult).then_inc(S["bdve"], 1)
                elif k == 4:
                    dve.wait_ge(S["bmm"], 7 * n + 12)
                    dve.tensor_tensor(hx[:, :, :], p_b[0:H, 0:128].rearrange("p (g d) -> p g d", d=DH), bcast(b_2[:, :], 1, 2 * NH), ALU.add)
                    dve.drain()
                    dve.scalar_tensor_tensor(out=hx[:, :, :], in0=x, scalar=0.0, in1=hx[:, :, :], op0=ALU.not_equal, op1=ALU.mult)
                    dve.drain()
                    dve.tensor_tensor(hx[:, :, :], hx[:, :, :], x, ALU.add)
                    dve.drain()
                    norm16(n, hx[:, :, :], 1, fn_g, fn_b, fo[:, :, :], S["fo_done"])
                elif k == 5:
                    dve.wait_ge(S["bmm"], 7 * n + 14)
                    logits = p_b[0:H, 256:264].rearrange("p (t h) -> p t h", t=2)
                    dve.tensor_reduce(fr[:, 0, :], logits, AX.X, ALU.max)
                    dve.drain()
                    dve.tensor_tensor(fg[:, :, :], logits, bcast(fr[:, 0, :], 2, NH), ALU.subtract).then_inc(S["bdve"], 1)
                elif k == 6:
                    dve.wait_ge(S["bact"], 5 * n + 5)
                    dve.tensor_reduce(fr[:, 1, :], fg_e[:, :, :], AX.X, ALU.add)
                    dve.drain()
                    dve.reciprocal(fr[:, 2, :], fr[:, 1, :])
                    dve.drain()
                    dve.tensor_tensor(fg[:, :, :], fg_e[:, :, :], bcast(fr[:, 2, :], 2, NH), ALU.mult)
                    dve.drain()
                    dve.tensor_tensor(fo[:, :, :], fo[:, :, :], bcast(fg[:, :, :].rearrange("p t h -> p (t h)"), 2, DH), ALU.mult)
                    dve.drain()
                    dve.wait_ge(kept_in[p], (n - p) // 2 * 16 + 16)
                    dve.wait_ge(stored[p], (n - p) // 2 * 16 + 16)
                    dve.tensor_tensor(res[p][:, :, :], fo[:, :, :].rearrange("p (t n) d -> p t (n d)", t=2), kept[p][:, :, :], ALU.add).then_inc(S["done"], 1)

            def tick(i, p, front, back, tail):
                def step(k):
                    if tail:
                        tail_of(i - 1, 1 - p, k)

                if front and not back:
                    layer_norm(0, 0)
                if front:
                    head_of(i + 1, 1 - p)
                for h in range(NH):
                    if front:
                        maxima(i + 1, h)
                    if h == 1:
                        step(0)
                    if h == 3:
                        step(1)
                if front:
                    with_tops(i + 1, 1 - p)
                if not (isinstance(i, int) and i >= B - 2):
                    layer_norm(i + 2, p)
                for k in range(2, 6):
                    step(k)
                if back:
                    normed_values(i)
                step(6)

            in_ticks(dve, B, tick, peeled=2)


def constants():
    tables = {"c_ident": np.eye(128), "c_iota": np.arange(256.0)}
    for made in (stu_constants(), select_constants(), relation_constants(), sample_constants(), ffn_constants()):
        tables.update(made)
    return {k: np.ascontiguousarray(v, np.float32) for k, v in tables.items()}


LAYOUTS = {
    "m_u_taps": ("L0_attn_m_u", (2, 1, 0)),
    "b1_cols": ("L0_ffn_b1", (1, 0)),
    "wq_t": ("L1_ffn_wq", (0, 3, 1, 2)),
    "wk_t": ("L1_ffn_wk", (0, 2, 1)),
    "wv_t": ("L1_ffn_wv", (0, 2, 1)),
    "gate_t": ("L1_ffn_gate_w", (0, 2, 1)),
    "fc1_t": ("L1_ffn_fc1_w", (1, 0)),
    "fc2_t": ("L1_ffn_fc2_w", (1, 0)),
    "fgate_t": ("L1_ffn_fgate_w", (1, 0)),
}

SCRATCH = {
    "h0": ([B, T, C], F32), "h1": ([B, T, C], F32), "u": ([B, T, C], F32), "w_route": ([B, NE], F32), "h2": ([B, T, C], F32),
    "num_low": ([2, B // 2, T_LOW * NR * KM], BF16), "dist_low": ([2, B // 2, T_LOW * NR * KM], BF16),
    "num_high": ([2, B // 2, (T - T_LOW) * NR * KM], BF16), "dist_high": ([2, B // 2, (T - T_LOW) * NR * KM], BF16),
    "q_n": ([B, C, ROWS], F32), "key_parts": ([B, T, 3 * C], BF16),
    "heads_low": ([STEPS["low"][0], 4, 6, TOKG], F32), "heads_high": ([STEPS["high"][0], 4, 6, TOKG], F32),
    "h3": ([B, T, C], F32), "resid": ([T, C], F32),
}


def tower(nc, d):
    for name, (shape, dt) in SCRATCH.items():
        d[name] = nc.dram_tensor("scratch_" + name, shape, dt, kind="Internal").ap()
    token_attention(nc, d)
    spectral_unit(nc, d)
    routing(nc, d)
    experts(nc, d)
    select_keys(nc, d)
    relations(nc, d, "low")
    relations(nc, d, "high")
    sample(nc, d)
    head_residual(nc, d)
    head_mixture(nc, d)


def kernel(**inputs):
    import concourse.bacc as bacc
    from concourse.bass_utils import run_bass_kernel_spmd

    arrays = {k: np.ascontiguousarray(v) for k, v in inputs.items()}
    for name, (source, axes) in LAYOUTS.items():
        arrays[name] = np.ascontiguousarray(np.transpose(arrays[source], axes))
    arrays["hl_w_t"] = np.ascontiguousarray(arrays["L1_ffn_hl_w"].reshape(C, C).T)
    arrays.update(constants())
    nc = bacc.Bacc("TRN2", target_bir_lowering=False, num_devices=1)
    d = {k: nc.dram_tensor(f"in_{k}_dram", a.shape, mybir.dt.from_np(a.dtype), kind="ExternalInput").ap() for k, a in arrays.items()}
    d["out"] = nc.dram_tensor("out_0_dram", (B, T, C), F32, kind="ExternalOutput").ap()
    tower(nc, d)
    r = run_bass_kernel_spmd(nc, [{f"in_{k}_dram": a for k, a in arrays.items()}], core_ids=[0])
    return r.results[0]["out_0_dram"]
```
